# Optimizing a Trainium2 kernel written in Bass

```python
import numpy as np
import jax
import jax.numpy as jnp

def _softmax(x, axis=-1):
    return jax.nn.softmax(x, axis=axis)

def _gelu(x):
    return jax.nn.gelu(x, approximate=True)

def _silu(x):
    return jax.nn.silu(x)

def _sigmoid(x):
    return jax.nn.sigmoid(x)

def _layernorm(x, axis=-1, eps=1e-05):
    m = jnp.mean(x, axis=axis, keepdims=True)
    v = jnp.var(x, axis=axis, keepdims=True)
    return (x - m) / jnp.sqrt(v + eps)

def _scatter_add(tgt, idx, src, axis=0):
    return tgt.at[idx].add(src)

def _segment_sum(src, seg, n):
    return jax.ops.segment_sum(src, seg, n)
kernel_name = 'mk_flamingo_gated_d2_seqx_r8_377252'

def setup_inputs(seed: int=0):
    np.random.seed(seed)
    _w = jnp.asarray

    def _rec_inputs():
        import jax
        import jax.numpy as jnp
        _rk = jax.random.key(seed)
        x = 7.22e-05 + 1 * jax.random.normal(jax.random.fold_in(_rk, 1), (8, 100, 128), jnp.float32)
        _lenS = 100 - jax.random.randint(jax.random.fold_in(_rk, 7), (8,), 0, max(1, 100 // 4) + 1, jnp.int32)
        _lenS2 = 1444 - jax.random.randint(jax.random.fold_in(_rk, 8), (8,), 0, max(1, 1444 // 4) + 1, jnp.int32)
        _ctx_1024P = jax.random.normal(jax.random.fold_in(_rk, 11), (8, 16, 128), jnp.float32)
        _ctx_1024c = jax.random.dirichlet(jax.random.fold_in(_rk, 511), 0.3 * jnp.ones((16,), jnp.float32), (8, 1444))
        _ctx_1024t = jnp.einsum('bsk,bkd->bsd', _ctx_1024c, _ctx_1024P)
        _ctx_1024t = _ctx_1024t * jax.lax.rsqrt(jnp.mean(jnp.square(_ctx_1024t)) + 1e-12) * 0.953939
        ctx_1024 = 4.13588e-05 + 0.999923 * (_ctx_1024t + 0.3 * jax.random.normal(jax.random.fold_in(_rk, 611), (8, 1444, 128), jnp.float32))
        _ctxb_2048x8P = jax.random.normal(jax.random.fold_in(_rk, 13), (8, 16, 8), jnp.float32)
        _ctxb_2048x8c = jax.random.dirichlet(jax.random.fold_in(_rk, 513), 0.3 * jnp.ones((16,), jnp.float32), (8, 1444))
        _ctxb_2048x8t = jnp.einsum('bsk,bkd->bsd', _ctxb_2048x8c, _ctxb_2048x8P)
        _ctxb_2048x8t = _ctxb_2048x8t * jax.lax.rsqrt(jnp.mean(jnp.square(_ctxb_2048x8t)) + 1e-12) * 0.953939
        ctxb_2048x8 = -0.00745576 + 0.997402 * (_ctxb_2048x8t + 0.3 * jax.random.normal(jax.random.fold_in(_rk, 613), (8, 1444, 8), jnp.float32))
        _validS = jnp.arange(100)[None, :] < _lenS[:, None]
        _validS2 = jnp.arange(1444)[None, :] < _lenS2[:, None]
        _causal = jnp.tril(jnp.ones((100, 100), dtype=bool))
        mask_1x1xSxS2_bk0 = jnp.logical_not(jnp.broadcast_to(_validS2[0:1, None, None, :], (1, 1, 100, 1444)))
        _g = jax.random.normal(jax.random.fold_in(_rk, 9001), (2, 2), jnp.float32)
        _g = jnp.sign(_g) * jnp.maximum(jnp.abs(_g), 1.0) + (_g == 0) * 1.0
        g_xattn = _g[0]
        g_ffn = _g[1]
        return (x, ctx_1024, ctxb_2048x8, mask_1x1xSxS2_bk0, g_xattn, g_ffn)
    x, ctx_1024, ctxb_2048x8, mask_1x1xSxS2_bk0, g_xattn, g_ffn = _rec_inputs()

    def _L0_xattn_setup():
        import jax, jax.numpy as jnp
        import numpy as np
        import math
        EMBED_DIM = 128
        NUM_HEADS = 16
        HEAD_DIM = EMBED_DIM // NUM_HEADS
        B, S = (4, 256)
        key = jax.random.key(seed)
        ks = jax.random.split(key, 7)
        std = math.sqrt(2.0 / EMBED_DIM)
        inp = {'query': jax.random.normal(ks[0], (B, S, EMBED_DIM), dtype=jnp.float32), 'key': jax.random.normal(ks[1], (B, S, EMBED_DIM), dtype=jnp.float32), 'value': jax.random.normal(ks[2], (B, S, EMBED_DIM), dtype=jnp.float32), 'Wq': jax.random.normal(ks[3], (EMBED_DIM, EMBED_DIM), dtype=jnp.float32) * std, 'bq': jnp.zeros((EMBED_DIM,), dtype=jnp.float32), 'Wk': jax.random.normal(ks[4], (EMBED_DIM, EMBED_DIM), dtype=jnp.float32) * std, 'bk': jnp.zeros((EMBED_DIM,), dtype=jnp.float32), 'Wv': jax.random.normal(ks[5], (EMBED_DIM, EMBED_DIM), dtype=jnp.float32) * std, 'bv': jnp.zeros((EMBED_DIM,), dtype=jnp.float32), 'Wo': jax.random.normal(ks[6], (EMBED_DIM, EMBED_DIM), dtype=jnp.float32) * std, 'bo': jnp.zeros((EMBED_DIM,), dtype=jnp.float32), 'mask': jnp.tril(jnp.ones((S, S), dtype=bool))[None, None, :, :]}
        return inp
    _L0_xattn_all = _L0_xattn_setup()
    _L0_xattn_in = {k: v for k, v in _L0_xattn_all.items() if k in ('Wq', 'bq', 'Wk', 'bk', 'Wv', 'bv', 'Wo', 'bo')}
    del _L0_xattn_all

    def _L0_ffn_setup():
        import jax, jax.numpy as jnp
        import numpy as np
        E, K, NG, TG = (64, 8, 8, 4)
        CAP = 128
        SCALE = 2.5

        def _route(x_flat, gate_weight, e_bias):
            T = x_flat.shape[0]
            logits = x_flat.astype(jnp.float32) @ gate_weight.astype(jnp.float32).T
            scores = jax.nn.sigmoid(logits)
            sfc = scores + e_bias[None, :]
            group_scores = jax.lax.top_k(sfc.reshape(T, NG, E // NG), 2)[0].sum(-1)
            _, gidx = jax.lax.top_k(group_scores, TG)
            gmask = jnp.zeros((T, NG), jnp.float32).at[jnp.arange(T)[:, None], gidx].set(1.0)
            smask = jnp.repeat(gmask, E // NG, axis=1)
            tmp = jnp.where(smask > 0, sfc, 0.0)
            _, topk_idx = jax.lax.top_k(tmp, K)
            topk_w = jnp.take_along_axis(scores, topk_idx, axis=1)
            topk_w = topk_w / (topk_w.sum(-1, keepdims=True) + 1e-20)
            return (topk_idx, topk_w * SCALE)

        def _moe_forward(hidden_states, gate_weight, e_bias, w1, w2, w3, shared_gate, shared_up, shared_down):
            B, S, H = hidden_states.shape
            T = B * S
            x = hidden_states.reshape(T, H)
            topk_idx, topk_w = _route(x, gate_weight, e_bias)
            Sk = T * K
            flat_e = topk_idx.reshape(-1)
            order = jnp.argsort(flat_e)
            sorted_e = flat_e[order]
            counts = jax.ops.segment_sum(jnp.ones((Sk,), jnp.int32), flat_e, num_segments=E)
            offsets = jnp.cumsum(counts) - counts
            pos = jnp.arange(Sk) - offsets[sorted_e]
            tok_sorted = x[order // K]
            xe = jnp.zeros((E, CAP, H), x.dtype).at[sorted_e, pos].set(tok_sorted, mode='drop')
            h = jax.nn.silu(jnp.einsum('ech,efh->ecf', xe, w1)) * jnp.einsum('ech,efh->ecf', xe, w3)
            ye = jnp.einsum('ecf,ehf->ech', h, w2)
            pos_c = jnp.minimum(pos, CAP - 1)
            vals = ye[sorted_e, pos_c]
            vals = jnp.where((pos < CAP)[:, None], vals, 0.0)
            flat_w = topk_w.reshape(-1)[order].astype(vals.dtype)
            flat_t = (jnp.arange(Sk) // K)[order]
            out = jax.ops.segment_sum(vals * flat_w[:, None], flat_t, num_segments=T)
            shared = jax.nn.silu(x @ shared_gate.T) * (x @ shared_up.T) @ shared_down.T
            return (out + shared).reshape(B, S, H)
        key = jax.random.key(seed)
        ks = jax.random.split(key, 9)
        B, S, H, F = (1, 256, 128, 64)
        bound = 1.0 / 32.0
        return {'hidden_states': jax.random.normal(ks[0], (B, S, H), jnp.float32), 'gate_weight': jax.random.uniform(ks[1], (E, H), jnp.float32, -bound, bound), 'e_bias': jnp.zeros((E,), jnp.float32), 'w1': jax.random.normal(ks[2], (E, F, H), jnp.float32) * 0.02, 'w2': jax.random.normal(ks[3], (E, H, F), jnp.float32) * 0.02, 'w3': jax.random.normal(ks[4], (E, F, H), jnp.float32) * 0.02, 'shared_gate': jax.random.normal(ks[5], (2 * F, H), jnp.float32) * 0.02, 'shared_up': jax.random.normal(ks[6], (2 * F, H), jnp.float32) * 0.02, 'shared_down': jax.random.normal(ks[7], (H, 2 * F), jnp.float32) * 0.02}
    _L0_ffn_all = _L0_ffn_setup()
    _L0_ffn_in = {k: v for k, v in _L0_ffn_all.items() if k in ('gate_weight', 'e_bias', 'w1', 'w2', 'w3', 'shared_gate', 'shared_up', 'shared_down')}
    del _L0_ffn_all

    def _L1_xattn_setup():
        import jax, jax.numpy as jnp
        import numpy as np
        D_MODEL = 128
        NUM_HEADS = 16
        THRESHOLD = 0.1
        key = jax.random.key(seed)
        ks = jax.random.split(key, 12)
        B, L, D, C = (2, 256, D_MODEL, 8)
        s = 1.0 / np.sqrt(D)
        inp = {'q_x': jax.random.normal(ks[0], (B, L, D), jnp.float32), 'k_x': jax.random.normal(ks[1], (B, L, D), jnp.float32), 'v_x': jax.random.normal(ks[2], (B, L, D), jnp.float32), 'energy_coeffs': jax.random.normal(ks[3], (B, L, C), jnp.float32), 'Wq': jax.random.normal(ks[4], (D, D), jnp.float32) * s, 'bq': jnp.zeros((D,), jnp.float32), 'Wk': jax.random.normal(ks[5], (D, D), jnp.float32) * s, 'bk': jnp.zeros((D,), jnp.float32), 'Wv': jax.random.normal(ks[6], (D, D), jnp.float32) * s, 'bv': jnp.zeros((D,), jnp.float32), 'Wo': jax.random.normal(ks[7], (D, D), jnp.float32) * s, 'bo': jnp.zeros((D,), jnp.float32)}
        return inp
    _L1_xattn_all = _L1_xattn_setup()
    _L1_xattn_in = {k: v for k, v in _L1_xattn_all.items() if k in ('Wq', 'bq', 'Wk', 'bk', 'Wv', 'bv', 'Wo', 'bo')}
    del _L1_xattn_all

    def _L1_ffn_setup():
        import jax, jax.numpy as jnp
        import numpy as np
        H = 128
        I = 352
        E = 8
        TOP_K = 2

        def _moe(hidden_states, router_w, gate_w, up_w, down_w):
            B, S, Hd = hidden_states.shape
            x = hidden_states.reshape(-1, Hd)
            logits = x @ router_w.T
            probs = jax.nn.softmax(logits.astype(jnp.float32), axis=-1)
            top_w, top_idx = jax.lax.top_k(probs, TOP_K)
            top_w = top_w.astype(x.dtype)
            onehot = jax.nn.one_hot(top_idx, E, dtype=x.dtype)
            w_te = jnp.einsum('tk,tke->te', top_w, onehot)
            g = jnp.einsum('th,eih->tei', x, gate_w)
            u = jnp.einsum('th,eih->tei', x, up_w)
            h = jax.nn.silu(g) * u
            y = jnp.einsum('tei,ehi,te->th', h, down_w, w_te)
            return y.reshape(B, S, Hd)
        key = jax.random.key(seed)
        ks = jax.random.split(key, 5)
        s = 0.02
        return {'hidden_states': jax.random.normal(ks[0], (2, 128, H), dtype=jnp.float32), 'router_w': jax.random.normal(ks[1], (E, H), dtype=jnp.float32) * s, 'gate_w': jax.random.normal(ks[2], (E, I, H), dtype=jnp.float32) * s, 'up_w': jax.random.normal(ks[3], (E, I, H), dtype=jnp.float32) * s, 'down_w': jax.random.normal(ks[4], (E, H, I), dtype=jnp.float32) * s}
    _L1_ffn_all = _L1_ffn_setup()
    _L1_ffn_in = {k: v for k, v in _L1_ffn_all.items() if k in ('router_w', 'gate_w', 'up_w', 'down_w')}
    del _L1_ffn_all
    return {'x': x, 'ctx_1024': ctx_1024, 'ctxb_2048x8': ctxb_2048x8, 'mask_1x1xSxS2_bk0': mask_1x1xSxS2_bk0, 'g_xattn': g_xattn, 'g_ffn': g_ffn, 'L0_xattn_Wq': _L0_xattn_in['Wq'], 'L0_xattn_bq': _L0_xattn_in['bq'], 'L0_xattn_Wk': _L0_xattn_in['Wk'], 'L0_xattn_bk': _L0_xattn_in['bk'], 'L0_xattn_Wv': _L0_xattn_in['Wv'], 'L0_xattn_bv': _L0_xattn_in['bv'], 'L0_xattn_Wo': _L0_xattn_in['Wo'], 'L0_xattn_bo': _L0_xattn_in['bo'], 'L0_ffn_gate_weight': _L0_ffn_in['gate_weight'], 'L0_ffn_e_bias': _L0_ffn_in['e_bias'], 'L0_ffn_w1': _L0_ffn_in['w1'], 'L0_ffn_w2': _L0_ffn_in['w2'], 'L0_ffn_w3': _L0_ffn_in['w3'], 'L0_ffn_shared_gate': _L0_ffn_in['shared_gate'], 'L0_ffn_shared_up': _L0_ffn_in['shared_up'], 'L0_ffn_shared_down': _L0_ffn_in['shared_down'], 'L1_xattn_Wq': _L1_xattn_in['Wq'], 'L1_xattn_bq': _L1_xattn_in['bq'], 'L1_xattn_Wk': _L1_xattn_in['Wk'], 'L1_xattn_bk': _L1_xattn_in['bk'], 'L1_xattn_Wv': _L1_xattn_in['Wv'], 'L1_xattn_bv': _L1_xattn_in['bv'], 'L1_xattn_Wo': _L1_xattn_in['Wo'], 'L1_xattn_bo': _L1_xattn_in['bo'], 'L1_ffn_router_w': _L1_ffn_in['router_w'], 'L1_ffn_gate_w': _L1_ffn_in['gate_w'], 'L1_ffn_up_w': _L1_ffn_in['up_w'], 'L1_ffn_down_w': _L1_ffn_in['down_w']}

def reference(x, ctx_1024, ctxb_2048x8, mask_1x1xSxS2_bk0, g_xattn, g_ffn, L0_xattn_Wq, L0_xattn_bq, L0_xattn_Wk, L0_xattn_bk, L0_xattn_Wv, L0_xattn_bv, L0_xattn_Wo, L0_xattn_bo, L0_ffn_gate_weight, L0_ffn_e_bias, L0_ffn_w1, L0_ffn_w2, L0_ffn_w3, L0_ffn_shared_gate, L0_ffn_shared_up, L0_ffn_shared_down, L1_xattn_Wq, L1_xattn_bq, L1_xattn_Wk, L1_xattn_bk, L1_xattn_Wv, L1_xattn_bv, L1_xattn_Wo, L1_xattn_bo, L1_ffn_router_w, L1_ffn_gate_w, L1_ffn_up_w, L1_ffn_down_w):
    import jax
    import jax.numpy as jnp

    def _L0_xattn_ref(query, key, value, Wq, bq, Wk, bk, Wv, bv, Wo, bo, mask):
        import jax, jax.numpy as jnp
        import numpy as np
        import math
        EMBED_DIM = 128
        NUM_HEADS = 16
        HEAD_DIM = EMBED_DIM // NUM_HEADS
        B, S = (4, 256)
        Bt, St, E = query.shape
        H, D = (NUM_HEADS, HEAD_DIM)
        q = (query @ Wq.T + bq).reshape(Bt, St, H, D).transpose(0, 2, 1, 3)
        k = (key @ Wk.T + bk).reshape(Bt, -1, H, D).transpose(0, 2, 1, 3)
        v = (value @ Wv.T + bv).reshape(Bt, -1, H, D).transpose(0, 2, 1, 3)
        scores = jnp.einsum('bhqd,bhkd->bhqk', q, k) / math.sqrt(D)
        neg_inf = jnp.asarray(jnp.finfo(scores.dtype).min, scores.dtype)
        scores = jnp.where(mask, scores, neg_inf)
        attention = jax.nn.softmax(scores, axis=-1)
        out = jnp.einsum('bhqk,bhkd->bhqd', attention, v)
        out = out.transpose(0, 2, 1, 3).reshape(Bt, St, E)
        return out @ Wo.T + bo

    def _L0_ffn_ref(hidden_states, gate_weight, e_bias, w1, w2, w3, shared_gate, shared_up, shared_down):
        import jax, jax.numpy as jnp
        import numpy as np
        E, K, NG, TG = (64, 8, 8, 4)
        CAP = 128
        SCALE = 2.5

        def _route(x_flat, gate_weight, e_bias):
            T = x_flat.shape[0]
            logits = x_flat.astype(jnp.float32) @ gate_weight.astype(jnp.float32).T
            scores = jax.nn.sigmoid(logits)
            sfc = scores + e_bias[None, :]
            group_scores = jax.lax.top_k(sfc.reshape(T, NG, E // NG), 2)[0].sum(-1)
            _, gidx = jax.lax.top_k(group_scores, TG)
            gmask = jnp.zeros((T, NG), jnp.float32).at[jnp.arange(T)[:, None], gidx].set(1.0)
            smask = jnp.repeat(gmask, E // NG, axis=1)
            tmp = jnp.where(smask > 0, sfc, 0.0)
            _, topk_idx = jax.lax.top_k(tmp, K)
            topk_w = jnp.take_along_axis(scores, topk_idx, axis=1)
            topk_w = topk_w / (topk_w.sum(-1, keepdims=True) + 1e-20)
            return (topk_idx, topk_w * SCALE)

        def _moe_forward(hidden_states, gate_weight, e_bias, w1, w2, w3, shared_gate, shared_up, shared_down):
            B, S, H = hidden_states.shape
            T = B * S
            x = hidden_states.reshape(T, H)
            topk_idx, topk_w = _route(x, gate_weight, e_bias)
            Sk = T * K
            flat_e = topk_idx.reshape(-1)
            order = jnp.argsort(flat_e)
            sorted_e = flat_e[order]
            counts = jax.ops.segment_sum(jnp.ones((Sk,), jnp.int32), flat_e, num_segments=E)
            offsets = jnp.cumsum(counts) - counts
            pos = jnp.arange(Sk) - offsets[sorted_e]
            tok_sorted = x[order // K]
            xe = jnp.zeros((E, CAP, H), x.dtype).at[sorted_e, pos].set(tok_sorted, mode='drop')
            h = jax.nn.silu(jnp.einsum('ech,efh->ecf', xe, w1)) * jnp.einsum('ech,efh->ecf', xe, w3)
            ye = jnp.einsum('ecf,ehf->ech', h, w2)
            pos_c = jnp.minimum(pos, CAP - 1)
            vals = ye[sorted_e, pos_c]
            vals = jnp.where((pos < CAP)[:, None], vals, 0.0)
            flat_w = topk_w.reshape(-1)[order].astype(vals.dtype)
            flat_t = (jnp.arange(Sk) // K)[order]
            out = jax.ops.segment_sum(vals * flat_w[:, None], flat_t, num_segments=T)
            shared = jax.nn.silu(x @ shared_gate.T) * (x @ shared_up.T) @ shared_down.T
            return (out + shared).reshape(B, S, H)
        return _moe_forward(hidden_states, gate_weight, e_bias, w1, w2, w3, shared_gate, shared_up, shared_down)

    def _L1_xattn_ref(q_x, k_x, v_x, energy_coeffs, Wq, bq, Wk, bk, Wv, bv, Wo, bo):
        import jax, jax.numpy as jnp
        import numpy as np
        D_MODEL = 128
        NUM_HEADS = 16
        THRESHOLD = 0.1
        B, L, D = q_x.shape
        H = NUM_HEADS
        Dh = D // H

        def proj(x, W, b):
            y = x @ W + b
            return y.reshape(B, -1, H, Dh).transpose(0, 2, 1, 3)
        Q = proj(q_x, Wq, bq)
        K = proj(k_x, Wk, bk)
        V = proj(v_x, Wv, bv)
        scores = jnp.einsum('bhqd,bhkd->bhqk', Q, K) / np.sqrt(Dh).astype(np.float32)
        attn = jax.nn.softmax(scores, axis=-1)
        attn = jnp.nan_to_num(attn, nan=0.0)
        energy = jnp.abs(energy_coeffs).mean(axis=-1)
        gate = jax.nn.sigmoid((energy - THRESHOLD) * 10.0)[:, None, None, :]
        attn = attn * gate
        out = jnp.einsum('bhqk,bhkd->bhqd', attn, V)
        out = out.transpose(0, 2, 1, 3).reshape(B, L, D)
        return out @ Wo + bo

    def _L1_ffn_ref(hidden_states, router_w, gate_w, up_w, down_w):
        import jax, jax.numpy as jnp
        import numpy as np
        H = 128
        I = 352
        E = 8
        TOP_K = 2

        def _moe(hidden_states, router_w, gate_w, up_w, down_w):
            B, S, Hd = hidden_states.shape
            x = hidden_states.reshape(-1, Hd)
            logits = x @ router_w.T
            probs = jax.nn.softmax(logits.astype(jnp.float32), axis=-1)
            top_w, top_idx = jax.lax.top_k(probs, TOP_K)
            top_w = top_w.astype(x.dtype)
            onehot = jax.nn.one_hot(top_idx, E, dtype=x.dtype)
            w_te = jnp.einsum('tk,tke->te', top_w, onehot)
            g = jnp.einsum('th,eih->tei', x, gate_w)
            u = jnp.einsum('th,eih->tei', x, up_w)
            h = jax.nn.silu(g) * u
            y = jnp.einsum('tei,ehi,te->th', h, down_w, w_te)
            return y.reshape(B, S, Hd)
        return _moe(hidden_states, router_w, gate_w, up_w, down_w)
    x = x + jnp.tanh(g_xattn[0]) * _L0_xattn_ref(_layernorm(x, axis=-1), ctx_1024, ctx_1024, L0_xattn_Wq, L0_xattn_bq, L0_xattn_Wk, L0_xattn_bk, L0_xattn_Wv, L0_xattn_bv, L0_xattn_Wo, L0_xattn_bo, mask_1x1xSxS2_bk0)
    x = x + jnp.tanh(g_ffn[0]) * _L0_ffn_ref(_layernorm(x, axis=-1), L0_ffn_gate_weight, L0_ffn_e_bias, L0_ffn_w1, L0_ffn_w2, L0_ffn_w3, L0_ffn_shared_gate, L0_ffn_shared_up, L0_ffn_shared_down)
    x = x + jnp.tanh(g_xattn[1]) * _L1_xattn_ref(_layernorm(x, axis=-1), ctx_1024, ctx_1024, ctxb_2048x8, L1_xattn_Wq, L1_xattn_bq, L1_xattn_Wk, L1_xattn_bk, L1_xattn_Wv, L1_xattn_bv, L1_xattn_Wo, L1_xattn_bo)
    x = x + jnp.tanh(g_ffn[1]) * _L1_ffn_ref(_layernorm(x, axis=-1), L1_ffn_router_w, L1_ffn_gate_w, L1_ffn_up_w, L1_ffn_down_w)
    return x

_drawn_inputs = setup_inputs


def setup_inputs(seed=0):
    import zlib

    import numpy as np

    out = dict(_drawn_inputs(seed))
    spreads = {'g_ffn': (-1.0, 0.6),
     'L0_xattn_bq': (0.0, 0.1),
     'L0_xattn_bk': (0.0, 2.0),
     'L0_xattn_bv': (0.0, 0.1),
     'L0_xattn_bo': (0.0, 0.1),
     'L0_ffn_e_bias': (0.0, 0.8),
     'L1_xattn_bq': (0.0, 0.551),
     'L1_xattn_bk': (0.0, 2.0),
     'L1_xattn_bv': (0.0, 0.1),
     'L1_xattn_bo': (0.0, 0.1)}
    factors = {'ctxb_2048x8': 64.0,
     'L0_ffn_gate_weight': 8.0,
     'L0_ffn_w1': 8.0,
     'L0_ffn_w2': 8.0,
     'L0_ffn_w3': 8.0,
     'L0_ffn_shared_gate': 8.0,
     'L0_ffn_shared_up': 8.0,
     'L0_ffn_shared_down': 8.0,
     'L1_ffn_router_w': 8.0,
     'L1_ffn_gate_w': 8.0,
     'L1_ffn_up_w': 8.0,
     'L1_ffn_down_w': 8.0}
    for name, (base, spread) in spreads.items():
        noise = np.random.default_rng([zlib.crc32(name.encode()), seed]).standard_normal(out[name].shape)
        drawn = base * np.exp(spread * noise) if base else spread * noise
        out[name] = jnp.asarray(drawn.astype(out[name].dtype))
    for name, factor in factors.items():
        out[name] = (out[name] * factor).astype(out[name].dtype)
    return out
```

```python
from contextlib import ExitStack

import concourse.bass as bass
from concourse import mybir

F32 = mybir.dt.float32
F32R = mybir.dt.float32r
BF16 = mybir.dt.bfloat16
U8 = mybir.dt.uint8
ALU = mybir.AluOpType
ACT = mybir.ActivationFunctionType
AX = mybir.AxisListType.X

B, S, D = 8, 100, 128
NK = 1444
KEY_TILE = 121
KEY_TILES = -(-NK // KEY_TILE)
LAST_ROWS = NK - (KEY_TILES - 1) * KEY_TILE
NKP = KEY_TILES * KEY_TILE
H, DH, G, J = 16, 8, 4, 4
HQ = H * S
GQ = J * S
CHUNKS = [(0, 482), (482, 482), (964, 480)]
V_CHUNKS = 3
V_PER = KEY_TILES // V_CHUNKS
SCALE = float(DH) ** -0.5
BIG = 1e30
EPS = 1e-5
TOK = B * S
HALF = TOK // 2
HB = B // 2

E0, F0 = 64, 64
NG, PER_G, TOP_G, TOP_E = 8, 8, 4, 8
CAP = 128.0
ROUTE_SCALE = 2.5
UNITS0 = E0 // 2 + 1
E1, I1, SPLIT1 = 8, 352, 3
UNITS1 = E1 * SPLIT1
RING = 4

MAX_SLOTS = {3: [0, 1], 4: [2, 3], 5: [4, 5], 6: [6, 7], 7: [8, 9], 8: [10, 11], 9: [12, 13], 10: [14], 11: [15]}
DEN_SLOT, OUT_SLOT = 3, 5
USES_FIRST, USES = 7, 9


def rows_of(t):
    return KEY_TILE if t < KEY_TILES - 1 else LAST_ROWS


def landed(n, slot, ring, each):
    return n * (each // ring) + (each - slot * (each // ring))


CONSTS = 31
PE_STEPS = ["xnT0_0", "xnT0_1", "any_b"] + [f"q0_{u}" for u in range(2 * G + 2)] \
    + ["xnT1_0", "xnT1_1", "logits0", "ranks", "wT0", "moe_sum0", "y0_0", "y0_1", "xnT2_0", "xnT2_1"] \
    + [f"q1_{u}" for u in range(2 * G + 2)] \
    + ["xnT3_0", "xnT3_1", "logits1", "wT1", "moe_sum1", "y1_0", "y1_1"]
ACT_STEPS = ["tanh", "root0", "xnT0_0", "xnT0_1", "energy_exp", "root1", "xnT1_0", "xnT1_1", "router0", "wT0", "yT0",
             "root2", "xnT2_0", "xnT2_1", "root3", "xnT3_0", "xnT3_1", "router1", "wT1", "yT1"]
PE_MARK = {name: i + 1 for i, name in enumerate(PE_STEPS)}
ACT_MARK = {name: i + 1 for i, name in enumerate(ACT_STEPS)}


def flamingo(nc, a, out, scratch):
    with ExitStack() as ctx:
        def sb(name, shape, dt=F32):
            return ctx.enter_context(nc.sbuf_tensor(name, shape, dt))

        def sem(name):
            return ctx.enter_context(nc.semaphore(name))

        ident = sb("ident", [128, 128])
        ident_b = sb("ident_b", [128, 128], BF16)
        head_mask = sb("head_mask", [128, J])
        head16_mask = sb("head16_mask", [128, H])
        max_mask = sb("max_mask", [128, H])
        den_sel = sb("den_sel", [128, 128])
        before = sb("before", [100, S])
        before_b = sb("before_b", [100, S], BF16)
        ones_b = sb("ones_b", [128, 128], BF16)
        ones_f = sb("ones_f", [128, 128])
        zero_b = sb("zero_b", [128, 512], BF16)
        tie_mask = sb("tie_mask", [100, 8, 8])
        gates = sb("gates", [128, 4])
        tgates = sb("tgates", [128, 4])
        wqr = [sb(f"wqr{l}", [128, G, 128]) for l in range(2)]
        wq = [sb(f"wq{l}", [128, 128]) for l in range(2)]
        wk = [sb(f"wk{l}", [128, 128]) for l in range(2)]
        wv = [sb(f"wv{l}", [128, 128]) for l in range(2)]
        wo = [sb(f"wo{l}", [128, G, 128]) for l in range(2)]
        bqr = [sb(f"bqr{l}", [128, G]) for l in range(2)]
        bq = [sb(f"bq{l}", [128, 1]) for l in range(2)]
        bk = [sb(f"bk{l}", [128, 1]) for l in range(2)]
        bv = [sb(f"bv{l}", [128, 128]) for l in range(2)]
        bo = [sb(f"bo{l}", [128, 128]) for l in range(2)]
        wr0 = sb("wr0", [128, E0])
        wr1 = sb("wr1", [128, E1])
        ebias = sb("ebias", [100, E0])

        xres = sb("xres", [100, B, D])
        xn = sb("xn", [100, B, D])
        xnT = sb("xnT", [128, TOK])
        stats = sb("stats", [100, B, 6])
        mv = sb("mv", [100, B, 2])
        rstd = sb("rstd", [100, B])
        var = sb("var", [100, B])
        fix = sb("fix", [100, B])

        mask_u = sb("mask_u", [100, NK], U8)
        maskT_u = sb("maskT_u", [KEY_TILE, KEY_TILES, S], U8)
        negq = sb("negq", [100, NK], BF16)
        any_q = sb("any_q", [100, 1])
        any_big = sb("any_big", [100, 1])
        any_diag = sb("any_diag", [100, S])
        any_b = sb("any_b", [128, S])
        negT = sb("negT", [KEY_TILE, KEY_TILES, S], BF16)
        egate = sb("egate", [KEY_TILE, B * KEY_TILES])

        ctxT = [sb(f"ctxT{i}", [128, NKP]) for i in range(2)]
        khi = sb("khi", [128, NK], F32R)
        klo = sb("klo", [128, NK], F32R)
        kst = [sb(f"kst{i}", [128, G, NK], F32R) for i in range(2)]
        vraw = [sb(f"vraw{i}", [KEY_TILE, V_PER, 128]) for i in range(2)]
        vaug = [sb(f"vaug{i}", [KEY_TILE, KEY_TILES, H * 9 + 24]) for i in range(2)]
        qsel = sb("qsel", [128, G, TOK], F32R)
        qhi = sb("qhi", [128, TOK], F32R)
        qst = [sb(f"qst{i}", [128, HQ], F32R) for i in range(2)]
        qbd = sb("qbd", [128, HQ], F32R)
        mx_part = sb("mx_part", [100, H, len(CHUNKS)])
        negm = sb("negm", [100, 128])
        junk = sb("junk", [100, 2, 512], BF16)
        probs = [sb(f"probs{i}", [KEY_TILE, HQ]) for i in range(2)]
        oraw = sb("oraw", [128, GQ])
        rden = sb("rden", [128, GQ])
        onorm = sb("onorm", [128, GQ])

        tmpf = sb("tmpf", [128, NKP])
        t2 = sb("t2", [128, 512])

        def over(host, off, shape, dt=F32):
            n = 1
            for s in shape[1:]:
                n *= s
            flat = host[:].bitcast(dt) if host.dtype != dt else host[:]
            if len(host.shape) == 3:
                flat = flat.rearrange("p a b -> p (a b)")
            v = flat[0:shape[0], off:off + n]
            if len(shape) == 3:
                v = v.rearrange("p (a b) -> p a b", b=shape[2])
            if len(shape) == 4:
                v = v.rearrange("p (a b c) -> p a b c", b=shape[2], c=shape[3])
            return v

        wts = [sb(f"wts{i}", [128, 3, 128]) for i in range(RING)]
        wb = [sb(f"wb{i}", [128, TOK]) for i in range(RING)]
        sg = [over(tmpf, v * HALF, [128, HALF]) for v in range(2)]
        tu = [over(ctxT[v], (TOK, 1024)[v], [128, HALF]) for v in range(2)]
        hh = [over(tmpf, 2 * HALF, [128, HALF]), over(t2, 0, [128, HALF])]
        yT = over(ctxT[0], 0, [128, TOK])
        rt = [over(ctxT[1], 0, [100, B * E0]), over(ctxT[1], B * E0, [100, B * E0])]
        rsc = over(probs[0], B * E0, [100, B * E0])
        rsel = over(probs[1], 0, [100, B * E0])
        rw = over(probs[1], B * E0, [100, B * E0])
        rsel_b = over(onorm, 0, [100, B, E0], BF16)
        top8 = over(tmpf, 0, [100, B * NG, 8])
        gsc = sb("gsc", [100, B * NG])
        gsel = sb("gsel", [100, B * NG])
        rsum = sb("rsum", [100, B])
        wT = over(tmpf, 512, [64, TOK])

        ps = ctx.enter_context(nc.psum_tensor("ps", [128, 4, 512], F32))
        po = ctx.enter_context(nc.psum_tensor("po", [128, 512], F32))
        pm = ctx.enter_context(nc.psum_tensor("pm", [128, 2, 512], F32))
        pc = ctx.enter_context(nc.psum_tensor("pc", [128, 512], F32))

        consts_in = sem("consts_in")
        x_in = sem("x_in")
        mask_in = sem("mask_in")
        energy_in = sem("energy_in")
        dve_done = sem("dve_done")
        act_done = sem("act_done")
        pe_done = sem("pe_done")
        pool_init = sem("pool_init")
        A = [dict((n, sem(f"{n}{l}")) for n in (
            "scores_ready", "probs_ready", "pv_done", "oraw_ready", "chunk_ready", "max_taken", "tail_ready",
            "khi_ready", "klo_ready", "vraw_ready", "v_written", "qstack_ready", "qbd_ready", "negm_ready",
            "maxrow_ready", "kproj_done", "vproj_done", "onorm_ready", "tail_step", "rowmax_step", "chunk_seen")) for l in range(2)]
        for l in range(2):
            for n in ("ctx_in", "kstack_in"):
                A[l][n] = [sem(f"{n}{l}_{i}") for i in range(2)]
        M = [dict((n, sem(f"m{n}{l}")) for n in (
            "gate_ready", "up_ready", "silu_done", "prod_done", "h_done", "down_done", "w_out")) for l in range(2)]
        for l in range(2):
            M[l]["w_in"] = [sem(f"w_in{l}_{i}") for i in range(RING)]
        out_done = sem("out_done")

        block = ctx.enter_context(nc.Block())

        marks = {}

        @block.vector
        def _(dve):
            n = [0]

            def step(ins, name=None):
                n[0] += 1
                ins.then_inc(dve_done, 1)
                dve.wait_ge(dve_done, n[0])
                if name:
                    marks[name] = n[0]

            def layer_norm(p):
                for b in range(B):
                    step(nc.vector.bn_stats(stats[:, b, :], xres[:, b, :]))
                for b in range(B):
                    step(nc.vector.bn_aggr(mv[:, b, :], stats[:, b, :]))
                step(nc.vector.tensor_scalar(var[:], mv[:, :, 1], EPS, None, ALU.add), f"var{p}")
                dve.wait_ge(act_done, ACT_MARK[f"root{p}"])
                step(nc.vector.reciprocal(rstd[:], rstd[:]))
                step(nc.vector.tensor_tensor(fix[:], rstd[:], rstd[:], ALU.mult))
                step(nc.vector.tensor_tensor(fix[:], fix[:], var[:], ALU.mult))
                step(nc.vector.tensor_scalar(fix[:], fix[:], -0.5, 1.5, ALU.mult, ALU.add))
                step(nc.vector.tensor_tensor(rstd[:], rstd[:], fix[:], ALU.mult))
                for b in range(B):
                    step(nc.vector.tensor_scalar(xn[:, b, :], xres[:, b, :], mv[:, b, 0:1], rstd[:, b:b + 1],
                                                 ALU.subtract, ALU.mult), f"xn{p}" if b == B - 1 else None)

            step(nc.vector.memset(ones_b[:], 1.0))
            step(nc.vector.memset(ones_f[:], 1.0))
            step(nc.vector.memset(zero_b[:], 0.0))
            step(nc.vector.memset(negm[:], 0.0))
            dve.wait_ge(x_in, 16)
            layer_norm(0)

            dve.wait_ge(mask_in, 48)
            dve.wait_ge(consts_in, CONSTS * 16)
            step(nc.vector.tensor_copy(ident_b[:], ident[:]))
            step(nc.vector.tensor_copy(before_b[:], before[:]))
            step(nc.vector.tensor_reduce(any_q[:], mask_u[:], AX, ALU.max))
            step(nc.vector.tensor_scalar(any_big[:], any_q[:], BIG, None, ALU.mult))
            step(nc.vector.tensor_scalar(negq[:], mask_u[:], 1.0, any_big[:, 0:1], ALU.subtract, ALU.mult))
            step(nc.vector.tensor_scalar(any_diag[:], ident[0:S, 0:S], any_q[:, 0:1], None, ALU.mult), "any_diag")
            dve.wait_ge(pe_done, PE_MARK["any_b"])
            step(nc.vector.tensor_copy(any_b[:], pc[:, 0:S]), "any_b")
            step(nc.vector.tensor_scalar(negT[:], maskT_u[:], 1.0, BIG, ALU.subtract, ALU.mult))
            step(nc.vector.tensor_tensor(negT[:], negT[:],
                                         any_b[0:KEY_TILE, :].unsqueeze(1).broadcast_to([KEY_TILE, KEY_TILES, S]),
                                         ALU.mult), "mask_ready")

            dve.wait_ge(energy_in, 32 * B)
            en = tmpf[0:KEY_TILE, 0:B * KEY_TILES * 8].rearrange("p (t e) -> p t e", e=8)
            step(nc.vector.scalar_tensor_tensor(en, en, -1.0, en, ALU.mult, ALU.max))
            step(nc.vector.tensor_reduce(egate[:], en, AX, ALU.add))
            step(nc.vector.tensor_scalar(egate[:], egate[:], 10.0 / 8.0, -1.0, ALU.mult, ALU.add), "energy")
            dve.wait_ge(act_done, ACT_MARK["energy_exp"])
            step(nc.vector.tensor_scalar(egate[:], egate[:], 1.0, None, ALU.add))
            step(nc.vector.reciprocal(egate[:], egate[:]), "gate_ready")

            def queries(l):
                for u in range(2 * G + 2):
                    g, v = u % 5, u // 5
                    dve.wait_ge(pe_done, PE_MARK[f"q{l}_{u}"])
                    cols = slice(v * HALF, (v + 1) * HALF)
                    bias = bqr[l][:, g:g + 1] if g < G else bq[l][:, 0:1]
                    src = ps[:, u % 4, 0:HALF].rearrange("p (b q) -> p b q", q=S)
                    keep = (any_b if l == 0 else ones_f)[:, 0:S].unsqueeze(1).broadcast_to([128, HB, S])
                    dst = t2[:, 0:HALF] if g < G else qhi[:, cols]
                    step(nc.vector.scalar_tensor_tensor(dst.rearrange("p (b q) -> p b q", q=S), src, bias, keep,
                                                        ALU.add, ALU.mult), f"qread{l}_{u}")
                    if g < G:
                        step(nc.vector.tensor_copy(qsel[:, g, cols], t2[:, 0:HALF]))
                        step(nc.vector.tensor_tensor(qsel[64:96, g, cols], t2[64:96, 0:HALF], qsel[64:96, g, cols],
                                                     ALU.subtract))
                marks[f"q_ready{l}"] = n[0]

            def attention(l):
                s = A[l]

                def k_low(b, c):
                    lo, w = CHUNKS[c]
                    dve.wait_ge(s["khi_ready"], b * 3 + (c + 1))
                    nc.vector.scalar_tensor_tensor(klo[:, lo:lo + w], pc[:, 0:w], bk[l][:, 0:1], khi[:, lo:lo + w],
                                                   ALU.add, ALU.subtract).then_inc(s["klo_ready"], 1)

                def head_max(b, h):
                    for c, (lo, w) in enumerate(CHUNKS):
                        dve.wait_ge(s["chunk_ready"], b * (3 * H) + (3 * h + c + 1))
                        if l == 0:
                            k = 3 * h + c
                            if not (isinstance(b, int) and b == 0 and k < 2):
                                dve.wait_ge(s["max_taken"], b * (3 * H) + (k - 1))
                            dve.sem_inc(s["chunk_seen"], 1)
                        i = (3 * h + c) % 2
                        if l == 0:
                            ins = nc.vector.tensor_tensor_reduce(junk[:, i, 0:w], pm[0:S, i, 0:w], negq[:, lo:lo + w], 1.0,
                                                                 -3e38, ALU.add, ALU.max, mx_part[:, h, c:c + 1])
                        else:
                            ins = nc.vector.tensor_reduce(mx_part[:, h, c:c + 1], pm[0:S, i, 0:w], AX, ALU.max)
                        ins.then_inc(s["max_taken"], 1)

                def row_max(b, par):
                    dve.wait_ge(s["max_taken"], b * (3 * H) + 3 * H)
                    nc.vector.tensor_reduce(negm[:, 96:96 + H], mx_part[:], AX, ALU.max).then_inc(s["rowmax_step"], 1)
                    dve.wait_ge(s["rowmax_step"], b * 2 + 1)
                    nc.vector.tensor_scalar(negm[:, 96:96 + H], negm[:, 96:96 + H], -1.0, None,
                                            ALU.mult).then_inc(s["rowmax_step"], 1)
                    dve.wait_ge(s["maxrow_ready"], b + 1)
                    if not (isinstance(b, int) and b < 2):
                        dve.wait_ge(s["pv_done"], b * KEY_TILES - KEY_TILES)
                    nc.vector.tensor_tensor(qst[par][96:128, :].rearrange("p (h q) -> p h q", q=S),
                                            pc[96:128, 0:S].unsqueeze(1).broadcast_to([32, H, S]),
                                            max_mask[96:128, :].unsqueeze(2).broadcast_to([32, H, S]),
                                            ALU.mult).then_inc(s["negm_ready"], 1)

                def normalise(b):
                    dve.wait_ge(s["tail_ready"], 2 * b + 1)
                    nc.vector.reciprocal(rden[:], pc[:, 0:GQ]).then_inc(s["tail_step"], 1)
                    dve.wait_ge(s["tail_step"], b * 4 + 1)
                    dve.wait_ge(s["oraw_ready"], b + 1)
                    nc.vector.tensor_tensor(onorm[:], oraw[:], rden[:], ALU.mult).then_inc(s["onorm_ready"], 1)

                def add_out(b):
                    dve.wait_ge(s["tail_ready"], 2 * b + 2)
                    nc.vector.tensor_tensor(t2[0:S, 0:D], pc[0:S, 0:D], bo[l][0:S, :], ALU.add)\
                        .then_inc(s["tail_step"], 1)
                    dve.wait_ge(s["tail_step"], b * 4 + 2)
                    nc.vector.tensor_scalar(t2[0:S, D:2 * D], t2[0:S, 0:D], tgates[0:S, l:l + 1], None, ALU.mult)\
                        .then_inc(s["tail_step"], 1)
                    dve.wait_ge(s["tail_step"], b * 4 + 3)
                    xb = xres[:, bass.ds(b, 1), :]
                    nc.vector.tensor_tensor(xb, t2[0:S, D:2 * D].unsqueeze(1), xb, ALU.add)\
                        .then_inc(s["tail_step"], 1)

                def slots(b, tail, prep, par):
                    for t in range(KEY_TILES):
                        if prep and t < 3:
                            k_low(b + 1, t)
                        if tail and t == DEN_SLOT:
                            normalise(b - 1)
                        if tail and t == OUT_SLOT:
                            add_out(b - 1)
                        if prep:
                            for h in MAX_SLOTS.get(t, []):
                                head_max(b + 1, h)
                    if prep:
                        row_max(b + 1, 1 - par)

                slots(-1, False, True, 1)
                slots(0, False, True, 0)
                with dve.Fori(0, (B - 2) // 2) as i:
                    for k in range(2):
                        slots(i * 2 + (1 + k), True, True, 1 - k)
                slots(B - 1, True, False, 1)
                normalise(B - 1)
                add_out(B - 1)
                dve.wait_ge(s["tail_step"], 4 * B)

            def experts(l):
                m = M[l]

                def prod(u):
                    for v in range(2):
                        dve.wait_ge(m["silu_done"], u * 2 + (v + 1))
                        dve.wait_ge(m["up_ready"], u * 2 + (v + 1))
                        if not (isinstance(u, int) and u == 0):
                            dve.wait_ge(m["h_done"], u * 2 + (v - 1))
                        nc.vector.tensor_tensor(tu[v], ps[:, 2 + v, 0:HALF], sg[v], ALU.mult)\
                            .then_inc(m["prod_done"], 1)

                units = (UNITS0, UNITS1)[l]
                prod(0)
                with dve.Fori(0, (units - 1) // RING) as i:
                    for k in range(RING):
                        prod(i * RING + (k + 1))
                for u in range((units - 1) // RING * RING + 1, units):
                    prod(u)
                for v in range(2):
                    dve.wait_ge(pe_done, PE_MARK[f"y{l}_{v}"])
                    xh = xres[:, v * HB:(v + 1) * HB, :]
                    step(nc.vector.scalar_tensor_tensor(
                        xh, ps[0:S, v, :].rearrange("p (b d) -> p b d", d=D), tgates[0:S, 2 + l:3 + l], xh,
                        ALU.mult, ALU.add), f"moe_out{l}_{v}")

            def route0():
                t0, t1 = rt
                r3 = lambda ap: ap.rearrange("p (b e) -> p b e", e=E0)
                r4 = lambda ap: ap.rearrange("p (g e) -> p g e", e=PER_G)
                dve.wait_ge(act_done, ACT_MARK["router0"])
                step(nc.vector.tensor_scalar(t0, rsc, 1.0, None, ALU.add))
                step(nc.vector.reciprocal(rsc, t0))
                step(nc.vector.tensor_tensor(r3(t0), r3(rsc), ebias[:].unsqueeze(1).broadcast_to([100, B, E0]), ALU.add))
                for j in range(B * NG):
                    ins = nc.vector.max(top8[:, j, :], t0[:, j * PER_G:(j + 1) * PER_G])
                    n[0] += 1
                    ins.then_inc(dve_done, 1)
                dve.wait_ge(dve_done, n[0])
                step(nc.vector.tensor_tensor(gsc[:], top8[:, :, 0], top8[:, :, 1], ALU.add))
                best_of(gsc[:].rearrange("p (b g) -> p b g", g=NG), gsel[:].rearrange("p (b g) -> p b g", g=NG), TOP_G)
                step(nc.vector.tensor_tensor(r4(t1), r4(t0), gsel[:].unsqueeze(2).broadcast_to([100, B * NG, PER_G]),
                                             ALU.mult))
                for b in range(B):
                    ins = nc.vector.max(top8[:, b, :], r3(t1)[:, b, :])
                    n[0] += 1
                    ins.then_inc(dve_done, 1)
                dve.wait_ge(dve_done, n[0])
                for b in range(B):
                    ins = nc.vector.match_replace(r3(t0)[:, b, :], top8[:, b, :], r3(t1)[:, b, :], -BIG)
                    n[0] += 1
                    ins.then_inc(dve_done, 1)
                dve.wait_ge(dve_done, n[0])
                step(nc.vector.tensor_scalar(rsel, t0, -BIG, None, ALU.is_equal))
                step(nc.vector.tensor_copy(rsel_b, r3(rsel)), "chosen")
                step(nc.vector.tensor_tensor(rw, rsel, rsc, ALU.mult))
                step(nc.vector.tensor_reduce(rsum[:], r3(rw), AX, ALU.add))
                step(nc.vector.tensor_scalar(rsum[:], rsum[:], 1e-20, None, ALU.add))
                step(nc.vector.reciprocal(rsum[:], rsum[:]))
                step(nc.vector.tensor_scalar(rsum[:], rsum[:], ROUTE_SCALE, None, ALU.mult))
                step(nc.vector.tensor_tensor(r3(rw), r3(rw), rsum[:].unsqueeze(2).broadcast_to([100, B, E0]), ALU.mult))
                dve.wait_ge(pe_done, PE_MARK["ranks"])
                step(nc.vector.tensor_scalar(t1, pc[0:S, :], CAP, None, ALU.is_lt))
                step(nc.vector.tensor_tensor(rw, rw, t1, ALU.mult), "weights0")

            def best_of(vals, sel, top):
                t0, t1 = over(xn, 0, [100, B, 8, 8]), over(xn, B * 64, [100, B, 8, 8])
                for b in range(B):
                    mine = vals[:, b, :].unsqueeze(2).broadcast_to([100, 8, 8])
                    other = vals[:, b, :].unsqueeze(1).broadcast_to([100, 8, 8])
                    step(nc.vector.tensor_tensor(t0[:, b], other, mine, ALU.is_gt))
                    step(nc.vector.tensor_tensor(t1[:, b], other, mine, ALU.is_equal))
                    step(nc.vector.tensor_tensor(t1[:, b], t1[:, b], tie_mask[:], ALU.mult))
                step(nc.vector.tensor_tensor(t0, t0, t1, ALU.add))
                step(nc.vector.tensor_reduce(sel, t0, AX, ALU.add))
                step(nc.vector.tensor_scalar(sel, sel, float(top), None, ALU.is_lt))

            def route1():
                r3 = lambda ap: ap.rearrange("p (b e) -> p b e", e=E1)
                lg, ex, sl = rt[0][:, 0:B * E1], rt[0][:, 64:128], rt[0][:, 128:192]
                dve.wait_ge(pe_done, PE_MARK["logits1"])
                step(nc.vector.tensor_reduce(rsum[:], pc[0:S, 0:B * E1].rearrange("p (b e) -> p b e", e=E1), AX, ALU.max))
                step(nc.vector.tensor_tensor(r3(lg), pc[0:S, 0:B * E1].rearrange("p (b e) -> p b e", e=E1),
                                             rsum[:].unsqueeze(2).broadcast_to([100, B, E1]), ALU.subtract), "logits_sub")
                dve.wait_ge(act_done, ACT_MARK["router1"])
                step(nc.vector.tensor_reduce(rsum[:], r3(ex), AX, ALU.add))
                step(nc.vector.reciprocal(rsum[:], rsum[:]))
                step(nc.vector.tensor_tensor(r3(ex), r3(ex), rsum[:].unsqueeze(2).broadcast_to([100, B, E1]), ALU.mult))
                best_of(r3(ex), r3(sl), 2)
                step(nc.vector.tensor_tensor(rw[:, 0:B * E1], ex, sl, ALU.mult), "weights1")

            queries(0)
            attention(0)
            layer_norm(1)
            route0()
            experts(0)
            layer_norm(2)
            queries(1)
            attention(1)
            layer_norm(3)
            route1()
            experts(1)

        @block.gpsimd
        def _(pool):
            nc.gpsimd.memset(maskT_u[:, KEY_TILES - 1, :], 0).then_inc(pool_init, 1)
            nc.gpsimd.memset(tmpf[:], 1.0).then_inc(pool_init, 1)
            for i in range(2):
                nc.gpsimd.memset(ctxT[i][:, NK:NKP], 0.0).then_inc(pool_init, 1)
                nc.gpsimd.memset(vaug[i][:], 1.0).then_inc(pool_init, 1)
                pool.wait_ge(pool_init, 3 * i + 4)
                nc.gpsimd.memset(kst[i][96:128, :, :].bitcast(F32), 1.0).then_inc(pool_init, 1)
                pool.wait_ge(pool_init, 3 * i + 5)

            def attention(l):
                s = A[l]
                ops = (1, 2)[l]

                def queries(b, par):
                    if not (isinstance(b, int) and b == 0):
                        pool.wait_ge(s["chunk_ready"], b * (3 * H))
                    cols = bass.ds(b * S, S)
                    nc.gpsimd.tensor_tensor(qbd[:].rearrange("p (h q) -> p h q", q=S),
                                            qhi[:, cols].unsqueeze(1).broadcast_to([128, H, S]),
                                            head16_mask[:].unsqueeze(2).broadcast_to([128, H, S]),
                                            ALU.mult).then_inc(s["qbd_ready"], 1)
                    if not (isinstance(b, int) and b < 2):
                        pool.wait_ge(s["pv_done"], b * KEY_TILES - KEY_TILES)
                    for g in range(G):
                        nc.gpsimd.tensor_tensor(
                            qst[par][0:96, g * GQ:(g + 1) * GQ].rearrange("p (j q) -> p j q", q=S),
                            qsel[0:96, g, cols].unsqueeze(1).broadcast_to([96, J, S]),
                            head_mask[0:96, :].unsqueeze(2).broadcast_to([96, J, S]),
                            ALU.mult).then_inc(s["qstack_ready"], 1)

                def values(b, c, par):
                    pool.wait_ge(s["vraw_ready"], b * 3 + (c + 1))
                    if c == 0 and not (isinstance(b, int) and b < 2):
                        pool.wait_ge(s["pv_done"], b * KEY_TILES - KEY_TILES)
                    raw = vraw[(c + par) % 2]
                    raw4 = raw[:].rearrange("p t (h e) -> p t h e", e=DH)
                    dst = vaug[par][:, c * V_PER:(c + 1) * V_PER, 0:H * 9].rearrange("p t (h e) -> p t h e", e=9)[:, :, :, 0:DH]
                    bias = bv[l][0:KEY_TILE, :].rearrange("p (h e) -> p h e", e=DH).unsqueeze(1)\
                        .broadcast_to([KEY_TILE, V_PER, H, DH])
                    nc.gpsimd.tensor_tensor(raw4 if l else dst, raw4, bias, ALU.add).then_inc(s["v_written"], 1)
                    if l == 1:
                        pool.wait_ge(s["v_written"], b * (3 * ops) + (c * ops + 1))
                        gate = egate[:, bass.ds(b * KEY_TILES + c * V_PER, V_PER)]
                        nc.gpsimd.tensor_tensor(dst, raw4, gate.unsqueeze(2).unsqueeze(3)
                                                .broadcast_to([KEY_TILE, V_PER, H, DH]), ALU.mult)\
                            .then_inc(s["v_written"], 1)

                def prep(b, par):
                    queries(b, par)
                    for c in range(V_CHUNKS):
                        values(b, c, par)

                pool.wait_ge(dve_done, marks[f"q_ready{l}"])
                if l == 1:
                    pool.wait_ge(dve_done, marks["gate_ready"])
                prep(0, 0)
                prep(1, 1)
                with pool.Fori(0, (B - 2) // 2) as i:
                    for k in range(2):
                        prep(i * 2 + (2 + k), k)

            def experts(l):
                m = M[l]

                def weigh(u, slot):
                    pool.wait_ge(m["w_in"][slot], landed(u, slot, RING, 48))
                    for v in range(2):
                        pool.wait_ge(m["prod_done"], u * 2 + (v + 1))
                        if not (isinstance(u, int) and u == 0):
                            pool.wait_ge(m["down_done"], u * 2 + (v - 1))
                        nc.gpsimd.tensor_tensor(hh[v], tu[v], wb[slot][:, v * HALF:(v + 1) * HALF],
                                                ALU.mult).then_inc(m["h_done"], 1)

                units = (UNITS0, UNITS1)[l]
                weigh(0, 0)
                with pool.Fori(0, (units - 1) // RING) as i:
                    for k in range(RING):
                        weigh(i * RING + (k + 1), (k + 1) % RING)
                for u in range((units - 1) // RING * RING + 1, units):
                    weigh(u, u % RING)

            attention(0)
            experts(0)
            attention(1)
            experts(1)

        @block.scalar
        def _(act):
            n = [0]

            def step(ins, name):
                n[0] += 1
                ins.then_inc(act_done, 1)
                assert ACT_MARK[name] == n[0], (name, n[0])

            def transposed(p):
                act.wait_ge(dve_done, marks[f"var{p}"])
                step(nc.scalar.activation(rstd[:], var[:], ACT.Sqrt), f"root{p}")
                for v in range(2):
                    act.wait_ge(pe_done, PE_MARK[f"xnT{p}_{v}"])
                    step(nc.scalar.copy(xnT[:, v * HALF:(v + 1) * HALF].rearrange("p (b q) -> p b q", q=S),
                                        ps[:, v, :].rearrange("p (b q) -> p b q", q=128)[:, :, 0:S]), f"xnT{p}_{v}")

            def attention(l):
                s = A[l]

                def exp_half(b, t, u):
                    r = rows_of(t)
                    act.wait_ge(s["scores_ready"], b * (2 * KEY_TILES) + (2 * t + u + 1))
                    if not (isinstance(b, int) and b == 0 and t < 2):
                        act.wait_ge(s["pv_done"], b * KEY_TILES + (t - 1))
                    nc.scalar.activation(probs[t % 2][0:r, 2 * u * GQ:2 * (u + 1) * GQ].rearrange("p (g q) -> p g q", q=GQ),
                                         ps[0:r, 2 * u:2 * u + 2, 0:GQ], ACT.Exp,
                                         scale=SCALE).then_inc(s["probs_ready"], 1)

                def k_high(b, c, par):
                    lo, w = CHUNKS[c]
                    act.wait_ge(s["kproj_done"], b * 3 + (c + 1))
                    if not (isinstance(b, int) and b == 0):
                        if c == 0:
                            act.wait_ge(s["chunk_ready"], b * (3 * H))
                            act.wait_ge(s["kstack_in"][1 - par], landed(b - 1, 1 - par, 2, 192))
                    nc.scalar.activation(khi[:, lo:lo + w], pc[:, 0:w], ACT.Identity, bias=bk[l][:, 0:1])\
                        .then_inc(s["khi_ready"], 1)

                def v_raw(b, c, par):
                    act.wait_ge(s["vproj_done"], b * 3 + (c + 1))
                    if not (isinstance(b, int) and b * 3 + c < 2):
                        act.wait_ge(s["v_written"], b * (3 * (1, 2)[l]) + (c - 1) * (1, 2)[l])
                    raw = vraw[(c + par) % 2]
                    nc.scalar.copy(raw[:].rearrange("p t n -> p (t n)"), pc[0:KEY_TILE, :]).then_inc(s["vraw_ready"], 1)

                def outputs(b):
                    act.wait_ge(s["pv_done"], b * KEY_TILES + KEY_TILES)
                    if not (isinstance(b, int) and b == 0):
                        act.wait_ge(s["onorm_ready"], b)
                    nc.scalar.copy(oraw[:], po[:, 0:GQ]).then_inc(s["oraw_ready"], 1)

                def slots(b, main, prep, par):
                    for t in range(KEY_TILES):
                        if main:
                            exp_half(b, t, 0)
                            exp_half(b, t, 1)
                        if prep and t < 3:
                            k_high(b + 1, t, 1 - par)
                    if prep:
                        for c in range(V_CHUNKS):
                            v_raw(b + 1, c, 1 - par)
                    if main:
                        outputs(b)

                slots(-1, False, True, 1)
                slots(0, True, True, 0)
                with act.Fori(0, (B - 2) // 2) as i:
                    for k in range(2):
                        slots(i * 2 + (1 + k), True, True, 1 - k)
                slots(B - 1, True, False, 1)

            def experts(l):
                m = M[l]

                def silu(u):
                    for v in range(2):
                        act.wait_ge(m["gate_ready"], u * 2 + (v + 1))
                        if not (isinstance(u, int) and u == 0):
                            act.wait_ge(m["prod_done"], u * 2 + (v - 1))
                        nc.scalar.activation(sg[v], ps[:, v, 0:HALF], ACT.Silu).then_inc(m["silu_done"], 1)

                units = (UNITS0, UNITS1)[l]
                silu(0)
                with act.Fori(0, (units - 1) // RING) as i:
                    for k in range(RING):
                        silu(i * RING + (k + 1))
                for u in range((units - 1) // RING * RING + 1, units):
                    silu(u)
                act.wait_ge(pe_done, PE_MARK[f"moe_sum{l}"])
                step(nc.scalar.copy(yT.rearrange("p (v n) -> p v n", v=2), pm[:, :, 0:HALF]), f"yT{l}")

            act.wait_ge(consts_in, CONSTS * 16)
            step(nc.scalar.activation(tgates[:], gates[:], ACT.Tanh), "tanh")
            transposed(0)
            act.wait_ge(dve_done, marks["energy"])
            step(nc.scalar.activation(egate[:], egate[:], ACT.Exp, scale=-1.0), "energy_exp")
            attention(0)
            transposed(1)
            act.wait_ge(pe_done, PE_MARK["logits0"])
            step(nc.scalar.activation(rsc, pc[0:S, :], ACT.Exp, scale=-1.0), "router0")
            act.wait_ge(pe_done, PE_MARK["wT0"])
            step(nc.scalar.copy(wT.rearrange("p (v b q) -> p v b q", v=2, q=S),
                                ps[0:E0, 0:2, :].rearrange("p v (b q) -> p v b q", q=128)[:, :, :, 0:S]), "wT0")
            experts(0)
            transposed(2)
            attention(1)
            transposed(3)
            act.wait_ge(dve_done, marks["logits_sub"])
            step(nc.scalar.activation(rt[0][:, 64:128], rt[0][:, 0:64], ACT.Exp), "router1")
            act.wait_ge(pe_done, PE_MARK["wT1"])
            step(nc.scalar.copy(wT[0:E1, :].rearrange("p (v b q) -> p v b q", v=2, q=S),
                                ps[0:E1, 0:2, :].rearrange("p v (b q) -> p v b q", q=128)[:, :, :, 0:S]), "wT1")
            experts(1)

        @block.tensor
        def _(pe):
            n = [0]

            def step(ins, name):
                n[0] += 1
                ins.then_inc(pe_done, 1)
                assert PE_MARK[name] == n[0], (name, n[0])

            def transpose_tokens(p):
                pe.wait_ge(dve_done, marks[f"xn{p}"])
                for v in range(2):
                    for b in range(HB):
                        mm = nc.tensor.transpose(ps[:, v, b * 128:b * 128 + S], xn[:, v * HB + b, :], ident[0:S, 0:S])
                    step(mm, f"xnT{p}_{v}")

            def queries(l):
                for u in range(2 * G + 2):
                    g, v = u % 5, u // 5
                    if g == 0:
                        pe.wait_ge(act_done, ACT_MARK[f"xnT{2 * l}_{v}"])
                    if u == 0 or u == 1:
                        pe.wait_ge(act_done, ACT_MARK[f"xnT{2 * l}_1"])
                    if u >= 4:
                        pe.wait_ge(dve_done, marks[f"qread{l}_{u - 4}"])
                    w = wqr[l][:, g, :] if g < G else wq[l][:]
                    step(nc.tensor.matmul(ps[:, u % 4, 0:HALF], w, xnT[:, v * HALF:(v + 1) * HALF],
                                          start=True, stop=True), f"q{l}_{u}")

            def attention(l):
                s = A[l]

                def k_chunk(b, c, par):
                    lo, w = CHUNKS[c]
                    if c == 0:
                        pe.wait_ge(s["ctx_in"][par], landed(b, par, 2, 16))
                        if not (isinstance(b, int) and b == 0):
                            pe.wait_ge(s["vraw_ready"], b * 3)
                    else:
                        pe.wait_ge(s["klo_ready"], b * 3 + c)
                    nc.tensor.matmul(pc[:, 0:w], wk[l][:], ctxT[par][:, lo:lo + w], start=True,
                                     stop=True).then_inc(s["kproj_done"], 1)

                def v_chunk(b, c, par):
                    if c == 0:
                        pe.wait_ge(s["negm_ready"], b + 1)
                    else:
                        pe.wait_ge(s["vraw_ready"], b * 3 + c)
                    for i in range(V_PER):
                        t = c * V_PER + i
                        mm = nc.tensor.matmul(pc[0:KEY_TILE, i * 128:(i + 1) * 128],
                                              ctxT[par][:, t * KEY_TILE:(t + 1) * KEY_TILE], wv[l][:],
                                              start=True, stop=True)
                    mm.then_inc(s["vproj_done"], 1)

                def max_head(b, h):
                    if h == 0:
                        pe.wait_ge(s["qbd_ready"], b + 1)
                        pe.wait_ge(s["khi_ready"], b * 3 + 3)
                    for c, (lo, w) in enumerate(CHUNKS):
                        k = 3 * h + c
                        if not (isinstance(b, int) and b == 0 and k < 2):
                            pe.wait_ge(s["max_taken"], b * (3 * H) + (k - 1))
                        mm = nc.tensor.matmul(pm[0:S, k % 2, 0:w], qbd[:, h * S:(h + 1) * S], khi[:, lo:lo + w],
                                              start=True, stop=True)
                        mm.then_inc(s["chunk_ready"], 1)

                def max_rows(b):
                    pe.wait_ge(s["rowmax_step"], b * 2 + 2)
                    nc.tensor.transpose(pc[:, 0:S], negm[:], ident[0:S, 0:S]).then_inc(s["maxrow_ready"], 1)

                def scores(b, t, par):
                    r = rows_of(t)
                    if t == 0:
                        pe.wait_ge(s["kstack_in"][par], landed(b, par, 2, 192))
                        pe.wait_ge(s["qstack_ready"], b * 4 + 4)
                        pe.wait_ge(s["negm_ready"], b + 1)
                    for u in range(2):
                        if not (isinstance(b, int) and b == 0 and t == 0):
                            pe.wait_ge(s["probs_ready"], b * (2 * KEY_TILES) + (2 * t + u - 1))
                        for g in range(2 * u, 2 * u + 2):
                            mm = nc.tensor.matmul(ps[0:r, g, 0:GQ], kst[par][:, g, t * KEY_TILE:t * KEY_TILE + r],
                                                  qst[par][:, g * GQ:(g + 1) * GQ], start=True, stop=(l == 1))
                            if l == 0:
                                mm = nc.tensor.matmul(ps[0:r, g, 0:GQ].rearrange("p (j q) -> p j q", q=S),
                                                      ident_b[0:r, 0:r],
                                                      negT[0:r, t, :].unsqueeze(1).broadcast_to([r, J, S]),
                                                      start=False, stop=True)
                        mm.then_inc(s["scores_ready"], 1)

                def weigh(b, t, par):
                    r = rows_of(t)
                    pe.wait_ge(s["probs_ready"], b * (2 * KEY_TILES) + (2 * t + 2))
                    if t == 0:
                        pe.wait_ge(s["v_written"], (b * 3 + 3) * (1, 2)[l])
                        if not (isinstance(b, int) and b == 0):
                            pe.wait_ge(s["oraw_ready"], b)
                    for g in range(G):
                        for j in range(J):
                            h = J * g + j
                            mm = nc.tensor.matmul(po[32 * j:32 * j + 32, g * S:(g + 1) * S],
                                                  vaug[par][0:r, t, 9 * h:9 * h + 32],
                                                  probs[t % 2][0:r, h * S:(h + 1) * S],
                                                  start=(t == 0 and g == 0), stop=(t == KEY_TILES - 1),
                                                  tile_position=(0, 32 * j), skip_group_check=True)
                    mm.then_inc(s["pv_done"], 1)

                def den(b):
                    pe.wait_ge(s["oraw_ready"], b + 1)
                    nc.tensor.matmul(pc[:, 0:GQ], den_sel[:], oraw[:], start=True, stop=True)\
                        .then_inc(s["tail_ready"], 1)

                def project(b):
                    pe.wait_ge(s["onorm_ready"], b + 1)
                    for g in range(G):
                        mm = nc.tensor.matmul(pc[0:S, 0:D], onorm[:, g * S:(g + 1) * S], wo[l][:, g, :],
                                              start=(g == 0), stop=(g == G - 1))
                    mm.then_inc(s["tail_ready"], 1)

                def slots(b, main, tail, prep, par):
                    for t in range(KEY_TILES):
                        if main:
                            scores(b, t, par)
                        if prep and t < 3:
                            k_chunk(b + 1, t, 1 - par)
                        if tail and t == DEN_SLOT:
                            if prep:
                                pe.wait_ge(s["klo_ready"], b * 3 + 6)
                            else:
                                pe.wait_ge(s["vraw_ready"], b * 3 + 3)
                            den(b - 1)
                        if tail and t == OUT_SLOT:
                            project(b - 1)
                        if prep:
                            for h in MAX_SLOTS.get(t, []):
                                max_head(b + 1, h)
                        if main and t >= 1:
                            weigh(b, t - 1, par)
                    if main:
                        weigh(b, KEY_TILES - 1, par)
                    if prep:
                        if tail:
                            pe.wait_ge(s["tail_step"], b * 4 - 2)
                        max_rows(b + 1)
                        for c in range(V_CHUNKS):
                            v_chunk(b + 1, c, 1 - par)

                slots(-1, False, False, True, 1)
                slots(0, True, False, True, 0)
                with pe.Fori(0, (B - 2) // 2) as i:
                    for k in range(2):
                        slots(i * 2 + (1 + k), True, True, True, 1 - k)
                slots(B - 1, True, True, False, 1)
                pe.wait_ge(s["tail_step"], 4 * (B - 1))
                den(B - 1)
                project(B - 1)

            def experts(l):
                m = M[l]
                units = (UNITS0, UNITS1)[l]

                def gate_up(u, slot):
                    pe.wait_ge(m["w_in"][slot], landed(u, slot, RING, 48))
                    for v in range(2):
                        cols = slice(v * HALF, (v + 1) * HALF)
                        if not (isinstance(u, int) and u == 0):
                            pe.wait_ge(m["prod_done"], u * 2 + (v - 1))
                        nc.tensor.matmul(ps[:, v, 0:HALF], wts[slot][:, 0, :], xnT[:, cols], start=True,
                                         stop=True).then_inc(m["gate_ready"], 1)
                        nc.tensor.matmul(ps[:, 2 + v, 0:HALF], wts[slot][:, 1, :], xnT[:, cols], start=True,
                                         stop=True).then_inc(m["up_ready"], 1)

                def down(u, slot):
                    for v in range(2):
                        pe.wait_ge(m["h_done"], u * 2 + (v + 1))
                        nc.tensor.matmul(pm[:, v, 0:HALF], wts[slot][:, 2, :], hh[v], start=False, stop=False,
                                         skip_group_check=True).then_inc(m["down_done"], 1)

                for v in range(2):
                    nc.tensor.matmul(pm[:, v, 0:HALF], zero_b[:, 0:128], zero_b[:, 0:HALF], start=True, stop=False,
                                     skip_group_check=True)
                gate_up(0, 0)
                with pe.Fori(0, (units - 1) // RING) as i:
                    for k in range(RING):
                        gate_up(i * RING + (k + 1), (k + 1) % RING)
                        down(i * RING + k, k)
                for u in range((units - 1) // RING * RING, units):
                    if u + 1 < units:
                        gate_up(u + 1, (u + 1) % RING)
                    down(u, u % RING)
                for v in range(2):
                    mm = nc.tensor.matmul(pm[:, v, 0:HALF], zero_b[:, 0:128], zero_b[:, 0:HALF], start=False, stop=True,
                                          skip_group_check=True)
                step(mm, f"moe_sum{l}")
                pe.wait_ge(act_done, ACT_MARK[f"yT{l}"])
                for v in range(2):
                    for b in range(HB):
                        mm = nc.tensor.transpose(ps[0:S, v, b * D:(b + 1) * D], yT[:, (v * HB + b) * S:(v * HB + b + 1) * S],
                                                 ident[:])
                    step(mm, f"y{l}_{v}")

            def logits(l, w, e):
                pe.wait_ge(act_done, ACT_MARK[f"xnT{2 * l + 1}_1"])
                for b in range(B):
                    mm = nc.tensor.matmul(pc[0:S, b * e:(b + 1) * e], xnT[:, b * S:(b + 1) * S], w[:],
                                          start=True, stop=True)
                step(mm, f"logits{l}")

            def weights_across(l, e):
                pe.wait_ge(dve_done, marks[f"weights{l}"])
                w3 = rw[:, 0:B * e].rearrange("p (b e) -> p b e", e=e)
                for b in range(B):
                    mm = nc.tensor.transpose(ps[0:e, b // HB, (b % HB) * 128:(b % HB) * 128 + S], w3[:, b, :],
                                             ident[0:S, 0:S])
                step(mm, f"wT{l}")

            pe.wait_ge(consts_in, CONSTS * 16)
            pe.wait_ge(pool_init, 8)
            transpose_tokens(0)
            pe.wait_ge(dve_done, marks["any_diag"])
            step(nc.tensor.matmul(pc[:, 0:S], ones_f[0:S, :], any_diag[:], start=True, stop=True), "any_b")
            queries(0)
            pe.wait_ge(dve_done, marks["q_ready0"])
            attention(0)
            transpose_tokens(1)
            logits(0, wr0, E0)
            pe.wait_ge(dve_done, marks["chosen"])
            for b in range(B):
                for c in range(b + 1):
                    mm = nc.tensor.matmul(pc[0:S, b * E0:(b + 1) * E0], (before_b[:] if c == b else ones_b[0:S, 0:S]),
                                          rsel_b[:, c, :], start=(c == 0), stop=(c == b))
            step(mm, "ranks")
            weights_across(0, E0)
            experts(0)
            transpose_tokens(2)
            queries(1)
            pe.wait_ge(dve_done, marks["q_ready1"])
            attention(1)
            transpose_tokens(3)
            logits(1, wr1, E1)
            weights_across(1, E1)
            experts(1)

        @block.sync
        def _(sp):
            sp.dma_start(xres[:], a["x"].rearrange("b q d -> q b d")).then_inc(x_in, 16)

            def context(l, b, par):
                s = A[l]
                if not (isinstance(b, int) and b < 2):
                    sp.wait_ge(s["vproj_done"], b * 3 - 3)
                sp.dma_start(ctxT[par][:, 0:NK], a["ctxT"][bass.ds(b, 1)].rearrange("a p n -> p (a n)"))\
                    .then_inc(s["ctx_in"][par], 16)

            def stack(l, b, par):
                s = A[l]
                sp.wait_ge(s["klo_ready"], b * 3 + 3)
                if not (isinstance(b, int) and b < 2):
                    sp.wait_ge(s["pv_done"], b * KEY_TILES - KEY_TILES)
                for g in range(G):
                    for i, part in enumerate((khi, klo, khi)):
                        sp.dma_start(kst[par][32 * i:32 * i + 32, g, :].bitcast(F32),
                                     part[32 * g:32 * g + 32, :].bitcast(F32)).then_inc(s["kstack_in"][par], 16)

            context(0, 0, 0)
            for name, tile in (("ident", ident), ("head_mask", head_mask), ("head16_mask", head16_mask),
                               ("max_mask", max_mask), ("den_sel", den_sel), ("before", before),
                               ("tie_mask", tie_mask), ("gates", gates), ("wr0", wr0), ("wr1", wr1), ("ebias", ebias)):
                sp.dma_start(tile[:], a[name]).then_inc(consts_in, 16)
            for l in range(2):
                for name, tiles in (("wqr", wqr), ("wq", wq), ("wk", wk), ("wv", wv), ("wo", wo), ("bqr", bqr),
                                    ("bq", bq), ("bk", bk), ("bv", bv), ("bo", bo)):
                    sp.dma_start(tiles[l][:], a[f"{name}{l}"]).then_inc(consts_in, 16)
            sp.dma_start(mask_u[:], a["mask"]).then_inc(mask_in, 16)
            sp.wait_ge(pool_init, 1)
            full = (KEY_TILES - 1) * KEY_TILE
            sp.dma_start(maskT_u[:, 0:KEY_TILES - 1, :], a["maskT"][0:full].rearrange("(t p) q -> p t q", p=KEY_TILE))\
                .then_inc(mask_in, 16)
            sp.dma_start(maskT_u[0:LAST_ROWS, KEY_TILES - 1, :], a["maskT"][full:NK]).then_inc(mask_in, 16)
            sp.wait_ge(pool_init, 2)
            en = tmpf[0:KEY_TILE, 0:B * KEY_TILES * 8].rearrange("p (b t e) -> p b t e", b=B, e=8)
            for b in range(B):
                sp.dma_start(en[:, b, 0:KEY_TILES - 1, :],
                             a["ctxb"][b, 0:full].rearrange("(t p) e -> p t e", p=KEY_TILE)).then_inc(energy_in, 16)
                sp.dma_start(en[0:LAST_ROWS, b, KEY_TILES - 1, :], a["ctxb"][b, full:NK]).then_inc(energy_in, 16)

            def attention(l, first):
                if not first:
                    context(l, 0, 0)
                context(l, 1, 1)
                stack(l, 0, 0)
                context(l, 2, 0)
                stack(l, 1, 1)
                context(l, 3, 1)
                with sp.Fori(0, (B - 4) // 2) as i:
                    for k in range(2):
                        stack(l, i * 2 + (2 + k), k)
                        context(l, i * 2 + (4 + k), k)
                stack(l, B - 2, 0)
                stack(l, B - 1, 1)

            def experts(l):
                m = M[l]
                units = (UNITS0, UNITS1)[l]

                def load(u, slot):
                    if not (isinstance(u, int) and u < RING):
                        sp.wait_ge(m["down_done"], u * 2 - (2 * RING - 2))
                    sp.dma_start(wts[slot][:], a[f"experts{l}"][bass.ds(u, 1)].rearrange("a p c n -> p (a c) n"))\
                        .then_inc(m["w_in"][slot], 16)
                    for i in range(2):
                        row = scratch[l][bass.ds(u * 2 + i, 1), :]
                        sp.dma_start(wb[slot][64 * i:64 * i + 64, :], row.broadcast_to([64, TOK]))\
                            .then_inc(m["w_in"][slot], 16)

                sp.wait_ge(act_done, ACT_MARK[f"wT{l}"])
                if l == 0:
                    sp.dma_start(scratch[0][0:E0, :], wT).then_inc(m["w_out"], 16)
                    sp.dma_start(scratch[0][E0:E0 + 2, :].rearrange("a (b n) -> a b n", n=100),
                                 ones_f[0:2, 0:100].unsqueeze(1).broadcast_to([2, 8, 100])).then_inc(m["w_out"], 16)
                    sp.wait_ge(m["w_out"], 32)
                else:
                    rows = scratch[1].rearrange("(e s) t -> s e t", s=2 * SPLIT1)
                    for i in range(2 * SPLIT1):
                        sp.dma_start(rows[i], wT[0:E1, :]).then_inc(m["w_out"], 16)
                    sp.wait_ge(m["w_out"], 16 * 2 * SPLIT1)
                for u in range(RING):
                    load(u, u)
                with sp.Fori(0, (units - RING) // RING) as i:
                    for k in range(RING):
                        load(i * RING + (RING + k), k)
                for u in range(units // RING * RING, units):
                    load(u, u % RING)

            attention(0, True)
            experts(0)
            sp.wait_ge(dve_done, marks["moe_out0_1"])
            attention(1, False)
            experts(1)
            sp.wait_ge(dve_done, marks["moe_out1_1"])
            sp.dma_start(out.rearrange("b q d -> q b d"), xres[:]).then_inc(out_done, 16)
            sp.wait_ge(out_done, 16)


_IN = ["x", "ctxT", "ctxb", "mask", "maskT", "ident", "head_mask", "head16_mask", "max_mask", "den_sel", "before",
       "tie_mask", "gates", "wr0", "wr1", "ebias", "experts0", "experts1"] + [
    f"{n}{l}" for l in range(2) for n in ("wqr", "wq", "wk", "wv", "wo", "bqr", "bq", "bk", "bv", "bo")]


def kernel(**inputs):
    import numpy as np
    import concourse.bacc as bacc
    from concourse.bass_utils import run_bass_kernel_spmd

    i = {k: np.asarray(v) for k, v in inputs.items()}
    a = {"x": i["x"], "ctxT": i["ctx_1024"].transpose(0, 2, 1), "ctxb": i["ctxb_2048x8"]}
    mask = i["mask_1x1xSxS2_bk0"][0, 0]
    a["mask"], a["maskT"] = mask, mask.T

    f = np.float32
    row = np.arange(128)
    a["ident"] = np.eye(128, dtype=f)
    a["head_mask"] = ((row[:, None] % 32 // DH == np.arange(J)) & (row[:, None] < 96)).astype(f)
    a["head16_mask"] = (row[:, None] // DH == np.arange(H)).astype(f)
    a["max_mask"] = (row[:, None] - 96 == np.arange(H)).astype(f)
    a["den_sel"] = (row[:, None] == row // 32 * 32 + DH).astype(f)
    a["before"] = (row[:S, None] < row[:S]).astype(f)
    a["tie_mask"] = np.ascontiguousarray(np.broadcast_to((np.arange(8) < np.arange(8)[:, None]).astype(f), (S, 8, 8)))

    a["gates"] = np.broadcast_to(np.concatenate([i["g_xattn"], i["g_ffn"]]), (128, 4))
    for l in range(2):
        w = {n: i[f"L{l}_xattn_W{n}"] for n in "qkvo"}
        if l == 0:
            w = {n: m.T for n, m in w.items()}
        b = {n: i[f"L{l}_xattn_b{n}"] for n in "qkvo"}
        a[f"wqr{l}"] = np.tile(w["q"].reshape(128, G, 1, 32), (1, 1, 4, 1)).reshape(128, G, 128)
        a[f"wq{l}"], a[f"wk{l}"], a[f"wv{l}"] = w["q"], w["k"], w["v"]
        wo = np.zeros((J, 32, G, D), f)
        wo[:, 0:DH] = w["o"].reshape(G, J, DH, D).transpose(1, 2, 0, 3)
        a[f"wo{l}"] = wo.reshape(128, G, D)
        a[f"bqr{l}"] = np.tile(b["q"].reshape(G, 32), (1, 4)).T
        a[f"bq{l}"], a[f"bk{l}"] = b["q"][:, None], b["k"][:, None]
        a[f"bv{l}"], a[f"bo{l}"] = np.broadcast_to(b["v"], (128, 128)), np.broadcast_to(b["o"], (128, 128))
    a["wr0"], a["wr1"] = i["L0_ffn_gate_weight"].T, i["L1_ffn_router_w"].T
    a["ebias"] = np.broadcast_to(i["L0_ffn_e_bias"], (S, E0))

    ex = np.zeros((UNITS0, 128, 3, 128), f)
    ex[:-1, :, 0] = i["L0_ffn_w1"].reshape(-1, 128, D).transpose(0, 2, 1)
    ex[:-1, :, 1] = i["L0_ffn_w3"].reshape(-1, 128, D).transpose(0, 2, 1)
    ex[:-1, :, 2] = i["L0_ffn_w2"].transpose(0, 2, 1).reshape(-1, 128, D)
    ex[-1, :, 0], ex[-1, :, 1], ex[-1, :, 2] = (i["L0_ffn_shared_gate"].T, i["L0_ffn_shared_up"].T,
                                                i["L0_ffn_shared_down"].T)
    a["experts0"] = ex
    part = I1 // SPLIT1 + 1
    ex = np.zeros((E1, SPLIT1, 128, 3, 128), f)
    for k in range(SPLIT1):
        lo, hi = k * part, min((k + 1) * part, I1)
        ex[:, k, :, 0, :hi - lo] = i["L1_ffn_gate_w"][:, lo:hi].transpose(0, 2, 1)
        ex[:, k, :, 1, :hi - lo] = i["L1_ffn_up_w"][:, lo:hi].transpose(0, 2, 1)
        ex[:, k, :hi - lo, 2] = i["L1_ffn_down_w"][:, :, lo:hi].transpose(0, 2, 1)
    a["experts1"] = ex.reshape(UNITS1, 128, 3, 128)

    nc = bacc.Bacc("TRN2", target_bir_lowering=False, num_devices=1)
    arrays, aps = {}, {}
    for name in _IN:
        arr = np.ascontiguousarray(a[name])
        arrays[f"in_{name}"] = arr
        aps[name] = nc.dram_tensor(f"in_{name}", arr.shape, mybir.dt.from_np(arr.dtype), kind="ExternalInput").ap()
    out = nc.dram_tensor("out_dram", (B, S, D), F32, kind="ExternalOutput").ap()
    scratch = [nc.dram_tensor(f"routing{l}", (2 * (UNITS0, UNITS1)[l], TOK), F32, kind="Internal").ap() for l in range(2)]
    flamingo(nc, aps, out, scratch)
    r = run_bass_kernel_spmd(nc, [arrays], core_ids=[0])
    return r.results[0]["out_dram"]
```

```python
from contextlib import ExitStack

import concourse.bass as bass
from concourse import mybir

F32 = mybir.dt.float32
F32R = mybir.dt.float32r
BF16 = mybir.dt.bfloat16
U8 = mybir.dt.uint8
ALU = mybir.AluOpType
ACT = mybir.ActivationFunctionType
AX = mybir.AxisListType.X

B, S, D = 8, 100, 128
NK = 1444
KEY_TILE = 121
KEY_TILES = -(-NK // KEY_TILE)
LAST_ROWS = NK - (KEY_TILES - 1) * KEY_TILE
NKP = KEY_TILES * KEY_TILE
H, DH, G, J = 16, 8, 4, 4
HQ = H * S
GQ = J * S
CHUNKS = [(0, 482), (482, 482), (964, 480)]
V_CHUNKS = 3
V_PER = KEY_TILES // V_CHUNKS
SCALE = float(DH) ** -0.5
BIG = 1e30
EPS = 1e-5
TOK = B * S
HALF = TOK // 2
HB = B // 2

E0, F0 = 64, 64
NG, PER_G, TOP_G, TOP_E = 8, 8, 4, 8
CAP = 128.0
ROUTE_SCALE = 2.5
UNITS0 = E0 // 2 + 1
E1, I1, SPLIT1 = 8, 352, 3
UNITS1 = E1 * SPLIT1
RING = 4

MAX_ROWS = [S, 128]
MAX_BLOCKS = [H, -(-HQ // 128)]
MAX_PER_SLOT = [[1, 4, 4, 4, 5, 5, 5, 5, 5, 5, 5, 0], [1, 3, 3, 4, 4, 4, 4, 4, 4, 4, 4, 0]]
MAX_SLOTS = [[range(sum(m[:t]), sum(m[:t + 1])) for t in range(KEY_TILES)] for m in MAX_PER_SLOT]
V_SLOTS = [7, 8, 9]
DEN_SLOT, OUT_SLOT = 3, 6
RECIPROCAL_SLOTS = {3: [0, 1], 4: [2, 3]}
NEGM_WRITES = [2, 3]
TAIL = G + 3
OUT_TAKEN = G + 1


def rows_of(t):
    return KEY_TILE if t < KEY_TILES - 1 else LAST_ROWS


def landed(n, slot, ring, each):
    return n * (each // ring) + (each - slot * (each // ring))


CONSTS = 31
PE_STEPS = ["xnT0_0", "xnT0_1", "any_b"] + [f"q0_{u}" for u in range(2 * G + 2)] \
    + ["xnT1_0", "xnT1_1", "logits0", "ranks", "wT0", "moe_sum0", "y0_0", "y0_1", "xnT2_0", "xnT2_1"] \
    + [f"q1_{u}" for u in range(2 * G + 2)] \
    + ["xnT3_0", "xnT3_1", "logits1", "wT1", "moe_sum1", "y1_0", "y1_1"]
ACT_STEPS = ["tanh", "root0", "xnT0_0", "xnT0_1", "energy_exp", "root1", "xnT1_0", "xnT1_1", "router0", "wT0", "yT0",
             "root2", "xnT2_0", "xnT2_1", "root3", "xnT3_0", "xnT3_1", "router1", "wT1", "yT1"]
PE_MARK = {name: i + 1 for i, name in enumerate(PE_STEPS)}
ACT_MARK = {name: i + 1 for i, name in enumerate(ACT_STEPS)}


def flamingo(nc, a, out, scratch):
    with ExitStack() as ctx:
        def sb(name, shape, dt=F32):
            return ctx.enter_context(nc.sbuf_tensor(name, shape, dt))

        def sem(name):
            return ctx.enter_context(nc.semaphore(name))

        ident = sb("ident", [128, 128])
        ident_b = sb("ident_b", [128, 128], BF16)
        head_mask = sb("head_mask", [128, J])
        head16_mask = sb("head16_mask", [128, H])
        max_mask = sb("max_mask", [128, H])
        den_sel = sb("den_sel", [128, 128])
        before = sb("before", [100, S])
        before_b = sb("before_b", [100, S], BF16)
        ones_b = sb("ones_b", [128, 128], BF16)
        ones_f = sb("ones_f", [128, 128])
        zero_b = sb("zero_b", [128, 512], BF16)
        tie_mask = sb("tie_mask", [100, 8, 8])
        gates = sb("gates", [128, 4])
        tgates = sb("tgates", [128, 4])
        wqr = [sb(f"wqr{l}", [128, G, 128]) for l in range(2)]
        wq = [sb(f"wq{l}", [128, 128]) for l in range(2)]
        wk = [sb(f"wk{l}", [128, 128]) for l in range(2)]
        wv = [sb(f"wv{l}", [128, 128]) for l in range(2)]
        wo = [sb(f"wo{l}", [128, G, 128]) for l in range(2)]
        bqr = [sb(f"bqr{l}", [128, G]) for l in range(2)]
        bq = [sb(f"bq{l}", [128, 1]) for l in range(2)]
        bk = [sb(f"bk{l}", [128, 1]) for l in range(2)]
        bv = [sb(f"bv{l}", [128, 128]) for l in range(2)]
        bo = [sb(f"bo{l}", [128, 128]) for l in range(2)]
        wr0 = sb("wr0", [128, E0])
        wr1 = sb("wr1", [128, E1])
        ebias = sb("ebias", [100, E0])

        xres = sb("xres", [100, B, D])
        xn = sb("xn", [100, B, D])
        xnT = sb("xnT", [128, TOK])
        stats = sb("stats", [100, B, 6])
        mv = sb("mv", [100, B, 2])
        rstd = sb("rstd", [100, B])
        var = sb("var", [100, B])
        fix = sb("fix", [100, B])

        mask_u = sb("mask_u", [100, NK], U8)
        maskT_u = sb("maskT_u", [KEY_TILE, KEY_TILES, S], U8)
        negq = sb("negq", [100, NK], BF16)
        any_q = sb("any_q", [100, 1])
        any_big = sb("any_big", [100, 1])
        any_diag = sb("any_diag", [100, S])
        any_b = sb("any_b", [128, S])
        negT = sb("negT", [KEY_TILE, KEY_TILES, S], BF16)
        egate = sb("egate", [KEY_TILE, B * KEY_TILES])

        ctxT = [sb(f"ctxT{i}", [128, NKP]) for i in range(2)]
        khi = sb("khi", [128, NK], F32R)
        klo = sb("klo", [128, NK], F32R)
        kst = [sb(f"kst{i}", [128, G, NK], F32R) for i in range(2)]
        vraw = [sb(f"vraw{i}", [KEY_TILE, V_PER, 128]) for i in range(2)]
        vaug = [sb(f"vaug{i}", [KEY_TILE, KEY_TILES, H * 9 + 24]) for i in range(2)]
        qsel = sb("qsel", [128, G, TOK], F32R)
        qhi = sb("qhi", [128, TOK], F32R)
        qst = [sb(f"qst{i}", [128, HQ], F32R) for i in range(2)]
        qbd = sb("qbd", [128, HQ], F32R)
        mx_part = sb("mx_part", [128, H, len(CHUNKS)])
        negm = sb("negm", [128, 128])
        junk = sb("junk", [100, 2, 512], BF16)
        probs = [sb(f"probs{i}", [KEY_TILE, HQ]) for i in range(2)]
        oraw = sb("oraw", [128, GQ])
        rden = sb("rden", [128, GQ])
        onorm = sb("onorm", [128, GQ])

        tmpf = sb("tmpf", [128, NKP])
        t2 = sb("t2", [128, 512])

        def over(host, off, shape, dt=F32):
            n = 1
            for s in shape[1:]:
                n *= s
            flat = host[:].bitcast(dt) if host.dtype != dt else host[:]
            if len(host.shape) == 3:
                flat = flat.rearrange("p a b -> p (a b)")
            v = flat[0:shape[0], off:off + n]
            if len(shape) == 3:
                v = v.rearrange("p (a b) -> p a b", b=shape[2])
            if len(shape) == 4:
                v = v.rearrange("p (a b c) -> p a b c", b=shape[2], c=shape[3])
            return v

        wts = [sb(f"wts{i}", [128, 3, 128]) for i in range(RING)]
        wb = [sb(f"wb{i}", [128, TOK]) for i in range(RING)]
        sg = [over(tmpf, v * HALF, [128, HALF]) for v in range(2)]
        tu = [over(ctxT[v], (TOK, 1024)[v], [128, HALF]) for v in range(2)]
        hh = [over(tmpf, 2 * HALF, [128, HALF]), over(t2, 0, [128, HALF])]
        yT = over(ctxT[0], 0, [128, TOK])
        rt = [over(ctxT[1], 0, [100, B * E0]), over(ctxT[1], B * E0, [100, B * E0])]
        rsc = over(probs[0], B * E0, [100, B * E0])
        rsel = over(probs[1], 0, [100, B * E0])
        rw = over(probs[1], B * E0, [100, B * E0])
        rsel_b = over(onorm, 0, [100, B, E0], BF16)
        top8 = over(tmpf, 0, [100, B * NG, 8])
        gsc = sb("gsc", [100, B * NG])
        gsel = sb("gsel", [100, B * NG])
        rsum = sb("rsum", [100, B])
        wT = over(tmpf, 512, [64, TOK])

        ps = ctx.enter_context(nc.psum_tensor("ps", [128, 4, 512], F32))
        po = ctx.enter_context(nc.psum_tensor("po", [128, 512], F32))
        pm = ctx.enter_context(nc.psum_tensor("pm", [128, 2, 512], F32))
        pc = ctx.enter_context(nc.psum_tensor("pc", [128, 512], F32))

        consts_in = sem("consts_in")
        x_in = sem("x_in")
        mask_in = sem("mask_in")
        energy_in = sem("energy_in")
        dve_done = sem("dve_done")
        act_done = sem("act_done")
        pe_done = sem("pe_done")
        pool_init = sem("pool_init")
        A = [dict((n, sem(f"{n}{l}")) for n in (
            "scores_ready", "probs_ready", "pv_done", "oraw_ready", "chunk_ready", "max_taken", "tail_ready",
            "khi_ready", "klo_ready", "vraw_ready", "v_written", "qstack_ready", "qbd_ready", "negm_ready",
            "maxrow_ready", "kproj_done", "vproj_done", "onorm_ready", "tail_step", "rowmax_step", "chunk_seen")) for l in range(2)]
        for l in range(2):
            for n in ("ctx_in", "kstack_in"):
                A[l][n] = [sem(f"{n}{l}_{i}") for i in range(2)]
        M = [dict((n, sem(f"m{n}{l}")) for n in (
            "gate_ready", "up_ready", "silu_done", "prod_done", "h_done", "down_done", "w_out")) for l in range(2)]
        for l in range(2):
            M[l]["w_in"] = [sem(f"w_in{l}_{i}") for i in range(RING)]
        out_done = sem("out_done")

        block = ctx.enter_context(nc.Block())

        marks = {}

        @block.vector
        def _(dve):
            n = [0]

            def step(ins, name=None):
                n[0] += 1
                ins.then_inc(dve_done, 1)
                dve.wait_ge(dve_done, n[0])
                if name:
                    marks[name] = n[0]

            def layer_norm(p):
                for b in range(B):
                    step(nc.vector.bn_stats(stats[:, b, :], xres[:, b, :]))
                for b in range(B):
                    step(nc.vector.bn_aggr(mv[:, b, :], stats[:, b, :]))
                step(nc.vector.tensor_scalar(var[:], mv[:, :, 1], EPS, None, ALU.add), f"var{p}")
                dve.wait_ge(act_done, ACT_MARK[f"root{p}"])
                step(nc.vector.reciprocal(rstd[:], rstd[:]))
                step(nc.vector.tensor_tensor(fix[:], rstd[:], rstd[:], ALU.mult))
                step(nc.vector.tensor_tensor(fix[:], fix[:], var[:], ALU.mult))
                step(nc.vector.tensor_scalar(fix[:], fix[:], -0.5, 1.5, ALU.mult, ALU.add))
                step(nc.vector.tensor_tensor(rstd[:], rstd[:], fix[:], ALU.mult))
                for b in range(B):
                    step(nc.vector.tensor_scalar(xn[:, b, :], xres[:, b, :], mv[:, b, 0:1], rstd[:, b:b + 1],
                                                 ALU.subtract, ALU.mult), f"xn{p}" if b == B - 1 else None)

            step(nc.vector.memset(ones_b[:], 1.0))
            step(nc.vector.memset(ones_f[:], 1.0))
            step(nc.vector.memset(zero_b[:], 0.0))
            step(nc.vector.memset(negm[:], 0.0))
            step(nc.vector.memset(mx_part[:], 0.0))
            dve.wait_ge(x_in, 16)
            layer_norm(0)

            dve.wait_ge(mask_in, 48)
            dve.wait_ge(consts_in, CONSTS * 16)
            step(nc.vector.tensor_copy(ident_b[:], ident[:]))
            step(nc.vector.tensor_copy(before_b[:], before[:]))
            step(nc.vector.tensor_reduce(any_q[:], mask_u[:], AX, ALU.max))
            step(nc.vector.tensor_scalar(any_big[:], any_q[:], BIG, None, ALU.mult))
            step(nc.vector.tensor_scalar(negq[:], mask_u[:], 1.0, any_big[:, 0:1], ALU.subtract, ALU.mult))
            step(nc.vector.tensor_scalar(any_diag[:], ident[0:S, 0:S], any_q[:, 0:1], None, ALU.mult), "any_diag")
            dve.wait_ge(pe_done, PE_MARK["any_b"])
            step(nc.vector.tensor_copy(any_b[:], pc[:, 0:S]), "any_b")
            step(nc.vector.tensor_scalar(negT[:], maskT_u[:], 1.0, BIG, ALU.subtract, ALU.mult))
            step(nc.vector.tensor_tensor(negT[:], negT[:],
                                         any_b[0:KEY_TILE, :].unsqueeze(1).broadcast_to([KEY_TILE, KEY_TILES, S]),
                                         ALU.mult), "mask_ready")

            dve.wait_ge(energy_in, 32 * B)
            en = tmpf[0:KEY_TILE, 0:B * KEY_TILES * 8].rearrange("p (t e) -> p t e", e=8)
            step(nc.vector.scalar_tensor_tensor(en, en, -1.0, en, ALU.mult, ALU.max))
            step(nc.vector.tensor_reduce(egate[:], en, AX, ALU.add))
            step(nc.vector.tensor_scalar(egate[:], egate[:], 10.0 / 8.0, -1.0, ALU.mult, ALU.add), "energy")
            dve.wait_ge(act_done, ACT_MARK["energy_exp"])
            step(nc.vector.tensor_scalar(egate[:], egate[:], 1.0, None, ALU.add))
            step(nc.vector.reciprocal(egate[:], egate[:]), "gate_ready")

            def queries(l):
                for u in range(2 * G + 2):
                    g, v = u % 5, u // 5
                    dve.wait_ge(pe_done, PE_MARK[f"q{l}_{u}"])
                    cols = slice(v * HALF, (v + 1) * HALF)
                    bias = bqr[l][:, g:g + 1] if g < G else bq[l][:, 0:1]
                    src = ps[:, u % 4, 0:HALF].rearrange("p (b q) -> p b q", q=S)
                    keep = (any_b if l == 0 else ones_f)[:, 0:S].unsqueeze(1).broadcast_to([128, HB, S])
                    dst = t2[:, 0:HALF] if g < G else qhi[:, cols]
                    step(nc.vector.scalar_tensor_tensor(dst.rearrange("p (b q) -> p b q", q=S), src, bias, keep,
                                                        ALU.add, ALU.mult), f"qread{l}_{u}")
                    if g < G:
                        step(nc.vector.tensor_copy(qsel[:, g, cols], t2[:, 0:HALF]))
                        step(nc.vector.tensor_tensor(qsel[64:96, g, cols], t2[64:96, 0:HALF], qsel[64:96, g, cols],
                                                     ALU.subtract))
                marks[f"q_ready{l}"] = n[0]

            def attention(l):
                s, blocks = A[l], MAX_BLOCKS[l]

                def k_low(b, c):
                    lo, w = CHUNKS[c]
                    dve.wait_ge(s["khi_ready"], b * 3 + (c + 1))
                    nc.vector.scalar_tensor_tensor(klo[:, lo:lo + w], pc[:, 0:w], bk[l][:, 0:1], khi[:, lo:lo + w],
                                                   ALU.add, ALU.subtract).then_inc(s["klo_ready"], 1)

                def chunk_max(b, k):
                    c, i = k // blocks, k % blocks
                    lo, w = CHUNKS[c]
                    rows = min(MAX_ROWS[l], HQ - i * MAX_ROWS[l])
                    dve.wait_ge(s["chunk_ready"], b * (3 * blocks) + (k + 1))
                    if l == 0:
                        if not (isinstance(b, int) and b == 0 and k < 2):
                            dve.wait_ge(s["max_taken"], b * (3 * blocks) + (k - 1))
                        dve.sem_inc(s["chunk_seen"], 1)
                        ins = nc.vector.tensor_tensor_reduce(junk[:, k % 2, 0:w], pm[0:S, k % 2, 0:w], negq[:, lo:lo + w],
                                                             1.0, -3e38, ALU.add, ALU.max, mx_part[0:S, i, c:c + 1])
                    else:
                        ins = nc.vector.tensor_reduce(mx_part[0:rows, i, c:c + 1], pm[0:rows, k % 2, 0:w], AX, ALU.max)
                    ins.then_inc(s["max_taken"], 1)

                def row_max(b, par):
                    rows = MAX_ROWS[l]
                    dve.wait_ge(s["max_taken"], b * (3 * blocks) + 3 * blocks)
                    nc.vector.tensor_reduce(negm[0:rows, 96:96 + blocks], mx_part[0:rows, 0:blocks, :], AX,
                                            ALU.max).then_inc(s["rowmax_step"], 1)
                    dve.wait_ge(s["rowmax_step"], b * 2 + 1)
                    nc.vector.tensor_scalar(negm[0:rows, 96:96 + blocks], negm[0:rows, 96:96 + blocks], -1.0, None,
                                            ALU.mult).then_inc(s["rowmax_step"], 1)
                    dve.wait_ge(s["maxrow_ready"], b + 1)
                    if not (isinstance(b, int) and b < 2):
                        dve.wait_ge(s["pv_done"], b * KEY_TILES - KEY_TILES)
                    for lo, hi, w in (((0, 8, S), (8, 16, S)), ((0, 7, 128), (7, 12, 128), (12, 13, HQ - 12 * 128)))[l]:
                        nc.vector.tensor_tensor(qst[par][96:128, lo * rows:lo * rows + (hi - lo) * w]
                                                .rearrange("p (h q) -> p h q", q=w),
                                                pc[96:128, 0:w].unsqueeze(1).broadcast_to([32, hi - lo, w]),
                                                max_mask[96:128, lo:hi].unsqueeze(2).broadcast_to([32, hi - lo, w]),
                                                ALU.mult).then_inc(s["negm_ready"], 1)

                def reciprocals(b, g):
                    cols = slice(g * S, (g + 1) * S)
                    dve.wait_ge(s["tail_ready"], 2 * b + 1)
                    nc.vector.reciprocal(rden[:, cols], pc[:, cols]).then_inc(s["tail_step"], 1)

                def normalise(b):
                    dve.wait_ge(s["tail_step"], b * TAIL + G)
                    dve.wait_ge(s["oraw_ready"], b + 1)
                    nc.vector.tensor_tensor(onorm[:], oraw[:], rden[:], ALU.mult).then_inc(s["onorm_ready"], 1)

                def add_out(b):
                    dve.wait_ge(s["tail_ready"], 2 * b + 2)
                    nc.vector.tensor_tensor(t2[0:S, 0:D], pc[0:S, 0:D], bo[l][0:S, :], ALU.add)\
                        .then_inc(s["tail_step"], 1)
                    dve.wait_ge(s["tail_step"], b * TAIL + OUT_TAKEN)
                    nc.vector.tensor_scalar(t2[0:S, D:2 * D], t2[0:S, 0:D], tgates[0:S, l:l + 1], None, ALU.mult)\
                        .then_inc(s["tail_step"], 1)
                    dve.wait_ge(s["tail_step"], b * TAIL + OUT_TAKEN + 1)
                    xb = xres[:, bass.ds(b, 1), :]
                    nc.vector.tensor_tensor(xb, t2[0:S, D:2 * D].unsqueeze(1), xb, ALU.add)\
                        .then_inc(s["tail_step"], 1)

                def slots(b, tail, prep, par):
                    for t in range(KEY_TILES):
                        if prep and t < 3:
                            k_low(b + 1, t)
                        extra = [lambda g=g: reciprocals(b - 1, g) for g in RECIPROCAL_SLOTS.get(t, []) if tail]
                        if tail and t == max(RECIPROCAL_SLOTS):
                            extra.append(lambda: normalise(b - 1))
                        if tail and t == OUT_SLOT:
                            extra.append(lambda: add_out(b - 1))
                        for k in MAX_SLOTS[l][t] if prep else []:
                            chunk_max(b + 1, k)
                            if extra:
                                extra.pop(0)()
                        for f in extra:
                            f()
                    if prep:
                        row_max(b + 1, 1 - par)

                slots(-1, False, True, 1)
                slots(0, False, True, 0)
                with dve.Fori(0, (B - 2) // 2) as i:
                    for k in range(2):
                        slots(i * 2 + (1 + k), True, True, 1 - k)
                slots(B - 1, True, False, 1)
                for g in range(G):
                    reciprocals(B - 1, g)
                normalise(B - 1)
                add_out(B - 1)
                dve.wait_ge(s["tail_step"], TAIL * B)

            def experts(l):
                m = M[l]

                def prod(u):
                    for v in range(2):
                        dve.wait_ge(m["silu_done"], u * 2 + (v + 1))
                        dve.wait_ge(m["up_ready"], u * 2 + (v + 1))
                        if not (isinstance(u, int) and u == 0):
                            dve.wait_ge(m["h_done"], u * 2 + (v - 1))
                        nc.vector.tensor_tensor(tu[v], ps[:, 2 + v, 0:HALF], sg[v], ALU.mult)\
                            .then_inc(m["prod_done"], 1)

                units = (UNITS0, UNITS1)[l]
                prod(0)
                with dve.Fori(0, (units - 1) // RING) as i:
                    for k in range(RING):
                        prod(i * RING + (k + 1))
                for u in range((units - 1) // RING * RING + 1, units):
                    prod(u)
                for v in range(2):
                    dve.wait_ge(pe_done, PE_MARK[f"y{l}_{v}"])
                    xh = xres[:, v * HB:(v + 1) * HB, :]
                    step(nc.vector.scalar_tensor_tensor(
                        xh, ps[0:S, v, :].rearrange("p (b d) -> p b d", d=D), tgates[0:S, 2 + l:3 + l], xh,
                        ALU.mult, ALU.add), f"moe_out{l}_{v}")

            def route0():
                t0, t1 = rt
                r3 = lambda ap: ap.rearrange("p (b e) -> p b e", e=E0)
                r4 = lambda ap: ap.rearrange("p (g e) -> p g e", e=PER_G)
                dve.wait_ge(act_done, ACT_MARK["router0"])
                step(nc.vector.tensor_scalar(t0, rsc, 1.0, None, ALU.add))
                step(nc.vector.reciprocal(rsc, t0))
                step(nc.vector.tensor_tensor(r3(t0), r3(rsc), ebias[:].unsqueeze(1).broadcast_to([100, B, E0]), ALU.add))
                for j in range(B * NG):
                    ins = nc.vector.max(top8[:, j, :], t0[:, j * PER_G:(j + 1) * PER_G])
                    n[0] += 1
                    ins.then_inc(dve_done, 1)
                dve.wait_ge(dve_done, n[0])
                step(nc.vector.tensor_tensor(gsc[:], top8[:, :, 0], top8[:, :, 1], ALU.add))
                best_of(gsc[:].rearrange("p (b g) -> p b g", g=NG), gsel[:].rearrange("p (b g) -> p b g", g=NG), TOP_G)
                step(nc.vector.tensor_tensor(r4(t1), r4(t0), gsel[:].unsqueeze(2).broadcast_to([100, B * NG, PER_G]),
                                             ALU.mult))
                for b in range(B):
                    ins = nc.vector.max(top8[:, b, :], r3(t1)[:, b, :])
                    n[0] += 1
                    ins.then_inc(dve_done, 1)
                dve.wait_ge(dve_done, n[0])
                for b in range(B):
                    ins = nc.vector.match_replace(r3(t0)[:, b, :], top8[:, b, :], r3(t1)[:, b, :], -BIG)
                    n[0] += 1
                    ins.then_inc(dve_done, 1)
                dve.wait_ge(dve_done, n[0])
                step(nc.vector.tensor_scalar(rsel, t0, -BIG, None, ALU.is_equal))
                step(nc.vector.tensor_copy(rsel_b, r3(rsel)), "chosen")
                step(nc.vector.tensor_tensor(rw, rsel, rsc, ALU.mult))
                step(nc.vector.tensor_reduce(rsum[:], r3(rw), AX, ALU.add))
                step(nc.vector.tensor_scalar(rsum[:], rsum[:], 1e-20, None, ALU.add))
                step(nc.vector.reciprocal(rsum[:], rsum[:]))
                step(nc.vector.tensor_scalar(rsum[:], rsum[:], ROUTE_SCALE, None, ALU.mult))
                step(nc.vector.tensor_tensor(r3(rw), r3(rw), rsum[:].unsqueeze(2).broadcast_to([100, B, E0]), ALU.mult))
                dve.wait_ge(pe_done, PE_MARK["ranks"])
                step(nc.vector.tensor_scalar(t1, pc[0:S, :], CAP, None, ALU.is_lt))
                step(nc.vector.tensor_tensor(rw, rw, t1, ALU.mult), "weights0")

            def best_of(vals, sel, top):
                t0, t1 = over(xn, 0, [100, B, 8, 8]), over(xn, B * 64, [100, B, 8, 8])
                for b in range(B):
                    mine = vals[:, b, :].unsqueeze(2).broadcast_to([100, 8, 8])
                    other = vals[:, b, :].unsqueeze(1).broadcast_to([100, 8, 8])
                    step(nc.vector.tensor_tensor(t0[:, b], other, mine, ALU.is_gt))
                    step(nc.vector.tensor_tensor(t1[:, b], other, mine, ALU.is_equal))
                    step(nc.vector.tensor_tensor(t1[:, b], t1[:, b], tie_mask[:], ALU.mult))
                step(nc.vector.tensor_tensor(t0, t0, t1, ALU.add))
                step(nc.vector.tensor_reduce(sel, t0, AX, ALU.add))
                step(nc.vector.tensor_scalar(sel, sel, float(top), None, ALU.is_lt))

            def route1():
                r3 = lambda ap: ap.rearrange("p (b e) -> p b e", e=E1)
                lg, ex, sl = rt[0][:, 0:B * E1], rt[0][:, 64:128], rt[0][:, 128:192]
                dve.wait_ge(pe_done, PE_MARK["logits1"])
                step(nc.vector.tensor_reduce(rsum[:], pc[0:S, 0:B * E1].rearrange("p (b e) -> p b e", e=E1), AX, ALU.max))
                step(nc.vector.tensor_tensor(r3(lg), pc[0:S, 0:B * E1].rearrange("p (b e) -> p b e", e=E1),
                                             rsum[:].unsqueeze(2).broadcast_to([100, B, E1]), ALU.subtract), "logits_sub")
                dve.wait_ge(act_done, ACT_MARK["router1"])
                step(nc.vector.tensor_reduce(rsum[:], r3(ex), AX, ALU.add))
                step(nc.vector.reciprocal(rsum[:], rsum[:]))
                step(nc.vector.tensor_tensor(r3(ex), r3(ex), rsum[:].unsqueeze(2).broadcast_to([100, B, E1]), ALU.mult))
                best_of(r3(ex), r3(sl), 2)
                step(nc.vector.tensor_tensor(rw[:, 0:B * E1], ex, sl, ALU.mult), "weights1")

            queries(0)
            attention(0)
            layer_norm(1)
            route0()
            experts(0)
            layer_norm(2)
            queries(1)
            attention(1)
            layer_norm(3)
            route1()
            experts(1)

        @block.gpsimd
        def _(pool):
            nc.gpsimd.memset(maskT_u[:, KEY_TILES - 1, :], 0).then_inc(pool_init, 1)
            nc.gpsimd.memset(tmpf[:], 1.0).then_inc(pool_init, 1)
            for i in range(2):
                nc.gpsimd.memset(ctxT[i][:, NK:NKP], 0.0).then_inc(pool_init, 1)
                nc.gpsimd.memset(vaug[i][:], 1.0).then_inc(pool_init, 1)
                pool.wait_ge(pool_init, 3 * i + 4)
                nc.gpsimd.memset(kst[i][96:128, :, :].bitcast(F32), 1.0).then_inc(pool_init, 1)
                pool.wait_ge(pool_init, 3 * i + 5)

            def attention(l):
                s = A[l]
                ops = (1, 2)[l]

                def queries(b, par):
                    if not (isinstance(b, int) and b == 0):
                        pool.wait_ge(s["chunk_ready"], b * (3 * MAX_BLOCKS[l]))
                    cols = bass.ds(b * S, S)
                    nc.gpsimd.tensor_tensor(qbd[:].rearrange("p (h q) -> p h q", q=S),
                                            qhi[:, cols].unsqueeze(1).broadcast_to([128, H, S]),
                                            head16_mask[:].unsqueeze(2).broadcast_to([128, H, S]),
                                            ALU.mult).then_inc(s["qbd_ready"], 1)
                    if not (isinstance(b, int) and b < 2):
                        pool.wait_ge(s["pv_done"], b * KEY_TILES - KEY_TILES)
                    for g in range(G):
                        nc.gpsimd.tensor_tensor(
                            qst[par][0:96, g * GQ:(g + 1) * GQ].rearrange("p (j q) -> p j q", q=S),
                            qsel[0:96, g, cols].unsqueeze(1).broadcast_to([96, J, S]),
                            head_mask[0:96, :].unsqueeze(2).broadcast_to([96, J, S]),
                            ALU.mult).then_inc(s["qstack_ready"], 1)

                def values(b, c, par):
                    pool.wait_ge(s["vraw_ready"], b * 3 + (c + 1))
                    if c == 0 and not (isinstance(b, int) and b < 2):
                        pool.wait_ge(s["pv_done"], b * KEY_TILES - KEY_TILES)
                    raw = vraw[(c + par) % 2]
                    raw4 = raw[:].rearrange("p t (h e) -> p t h e", e=DH)
                    dst = vaug[par][:, c * V_PER:(c + 1) * V_PER, 0:H * 9].rearrange("p t (h e) -> p t h e", e=9)[:, :, :, 0:DH]
                    bias = bv[l][0:KEY_TILE, :].rearrange("p (h e) -> p h e", e=DH).unsqueeze(1)\
                        .broadcast_to([KEY_TILE, V_PER, H, DH])
                    nc.gpsimd.tensor_tensor(raw4 if l else dst, raw4, bias, ALU.add).then_inc(s["v_written"], 1)
                    if l == 1:
                        pool.wait_ge(s["v_written"], b * (3 * ops) + (c * ops + 1))
                        gate = egate[:, bass.ds(b * KEY_TILES + c * V_PER, V_PER)]
                        nc.gpsimd.tensor_tensor(dst, raw4, gate.unsqueeze(2).unsqueeze(3)
                                                .broadcast_to([KEY_TILE, V_PER, H, DH]), ALU.mult)\
                            .then_inc(s["v_written"], 1)

                def prep(b, par):
                    queries(b, par)
                    for c in range(V_CHUNKS):
                        values(b, c, par)

                pool.wait_ge(dve_done, marks[f"q_ready{l}"])
                if l == 1:
                    pool.wait_ge(dve_done, marks["gate_ready"])
                prep(0, 0)
                prep(1, 1)
                with pool.Fori(0, (B - 2) // 2) as i:
                    for k in range(2):
                        prep(i * 2 + (2 + k), k)

            def experts(l):
                m = M[l]

                def weigh(u, slot):
                    pool.wait_ge(m["w_in"][slot], landed(u, slot, RING, 48))
                    for v in range(2):
                        pool.wait_ge(m["prod_done"], u * 2 + (v + 1))
                        if not (isinstance(u, int) and u == 0):
                            pool.wait_ge(m["down_done"], u * 2 + (v - 1))
                        nc.gpsimd.tensor_tensor(hh[v], tu[v], wb[slot][:, v * HALF:(v + 1) * HALF],
                                                ALU.mult).then_inc(m["h_done"], 1)

                units = (UNITS0, UNITS1)[l]
                weigh(0, 0)
                with pool.Fori(0, (units - 1) // RING) as i:
                    for k in range(RING):
                        weigh(i * RING + (k + 1), (k + 1) % RING)
                for u in range((units - 1) // RING * RING + 1, units):
                    weigh(u, u % RING)

            attention(0)
            experts(0)
            attention(1)
            experts(1)

        @block.scalar
        def _(act):
            n = [0]

            def step(ins, name):
                n[0] += 1
                ins.then_inc(act_done, 1)
                assert ACT_MARK[name] == n[0], (name, n[0])

            def transposed(p):
                act.wait_ge(dve_done, marks[f"var{p}"])
                step(nc.scalar.activation(rstd[:], var[:], ACT.Sqrt), f"root{p}")
                for v in range(2):
                    act.wait_ge(pe_done, PE_MARK[f"xnT{p}_{v}"])
                    step(nc.scalar.copy(xnT[:, v * HALF:(v + 1) * HALF].rearrange("p (b q) -> p b q", q=S),
                                        ps[:, v, :].rearrange("p (b q) -> p b q", q=128)[:, :, 0:S]), f"xnT{p}_{v}")

            def attention(l):
                s = A[l]

                def exp_half(b, t, u):
                    r = rows_of(t)
                    act.wait_ge(s["scores_ready"], b * (2 * KEY_TILES) + (2 * t + u + 1))
                    if not (isinstance(b, int) and b == 0 and t < 2):
                        act.wait_ge(s["pv_done"], b * KEY_TILES + (t - 1))
                    nc.scalar.activation(probs[t % 2][0:r, 2 * u * GQ:2 * (u + 1) * GQ].rearrange("p (g q) -> p g q", q=GQ),
                                         ps[0:r, 2 * u:2 * u + 2, 0:GQ], ACT.Exp,
                                         scale=SCALE).then_inc(s["probs_ready"], 1)

                def k_high(b, c, par):
                    lo, w = CHUNKS[c]
                    act.wait_ge(s["kproj_done"], b * 3 + (c + 1))
                    if not (isinstance(b, int) and b == 0):
                        if c == 0:
                            act.wait_ge(s["chunk_ready"], b * (3 * MAX_BLOCKS[l]))
                            act.wait_ge(s["kstack_in"][1 - par], landed(b - 1, 1 - par, 2, 192))
                    nc.scalar.activation(khi[:, lo:lo + w], pc[:, 0:w], ACT.Identity, bias=bk[l][:, 0:1])\
                        .then_inc(s["khi_ready"], 1)

                def v_raw(b, c, par):
                    act.wait_ge(s["vproj_done"], b * 3 + (c + 1))
                    if not (isinstance(b, int) and b * 3 + c < 2):
                        act.wait_ge(s["v_written"], b * (3 * (1, 2)[l]) + (c - 1) * (1, 2)[l])
                    raw = vraw[(c + par) % 2]
                    nc.scalar.copy(raw[:].rearrange("p t n -> p (t n)"), pc[0:KEY_TILE, :]).then_inc(s["vraw_ready"], 1)

                def outputs(b):
                    act.wait_ge(s["pv_done"], b * KEY_TILES + KEY_TILES)
                    if not (isinstance(b, int) and b == 0):
                        act.wait_ge(s["onorm_ready"], b)
                    nc.scalar.copy(oraw[:], po[:, 0:GQ]).then_inc(s["oraw_ready"], 1)

                def slots(b, main, after, prep, par):
                    for t in range(KEY_TILES):
                        if main:
                            exp_half(b, t, 0)
                        if prep and t < 3:
                            k_high(b + 1, t, 1 - par)
                        if prep and t in V_SLOTS:
                            v_raw(b + 1, V_SLOTS.index(t), 1 - par)
                        if main:
                            exp_half(b, t, 1)
                        if after and t == 0:
                            outputs(b - 1)

                slots(-1, False, False, True, 1)
                slots(0, True, False, True, 0)
                with act.Fori(0, (B - 2) // 2) as i:
                    for k in range(2):
                        slots(i * 2 + (1 + k), True, True, True, 1 - k)
                slots(B - 1, True, True, False, 1)
                outputs(B - 1)

            def experts(l):
                m = M[l]

                def silu(u):
                    for v in range(2):
                        act.wait_ge(m["gate_ready"], u * 2 + (v + 1))
                        if not (isinstance(u, int) and u == 0):
                            act.wait_ge(m["prod_done"], u * 2 + (v - 1))
                        nc.scalar.activation(sg[v], ps[:, v, 0:HALF], ACT.Silu).then_inc(m["silu_done"], 1)

                units = (UNITS0, UNITS1)[l]
                silu(0)
                with act.Fori(0, (units - 1) // RING) as i:
                    for k in range(RING):
                        silu(i * RING + (k + 1))
                for u in range((units - 1) // RING * RING + 1, units):
                    silu(u)
                act.wait_ge(pe_done, PE_MARK[f"moe_sum{l}"])
                step(nc.scalar.copy(yT.rearrange("p (v n) -> p v n", v=2), pm[:, :, 0:HALF]), f"yT{l}")

            act.wait_ge(consts_in, CONSTS * 16)
            step(nc.scalar.activation(tgates[:], gates[:], ACT.Tanh), "tanh")
            transposed(0)
            act.wait_ge(dve_done, marks["energy"])
            step(nc.scalar.activation(egate[:], egate[:], ACT.Exp, scale=-1.0), "energy_exp")
            attention(0)
            transposed(1)
            act.wait_ge(pe_done, PE_MARK["logits0"])
            step(nc.scalar.activation(rsc, pc[0:S, :], ACT.Exp, scale=-1.0), "router0")
            act.wait_ge(pe_done, PE_MARK["wT0"])
            step(nc.scalar.copy(wT.rearrange("p (v b q) -> p v b q", v=2, q=S),
                                ps[0:E0, 0:2, :].rearrange("p v (b q) -> p v b q", q=128)[:, :, :, 0:S]), "wT0")
            experts(0)
            transposed(2)
            attention(1)
            transposed(3)
            act.wait_ge(dve_done, marks["logits_sub"])
            step(nc.scalar.activation(rt[0][:, 64:128], rt[0][:, 0:64], ACT.Exp), "router1")
            act.wait_ge(pe_done, PE_MARK["wT1"])
            step(nc.scalar.copy(wT[0:E1, :].rearrange("p (v b q) -> p v b q", v=2, q=S),
                                ps[0:E1, 0:2, :].rearrange("p v (b q) -> p v b q", q=128)[:, :, :, 0:S]), "wT1")
            experts(1)

        @block.tensor
        def _(pe):
            n = [0]

            def step(ins, name):
                n[0] += 1
                ins.then_inc(pe_done, 1)
                assert PE_MARK[name] == n[0], (name, n[0])

            def transpose_tokens(p):
                pe.wait_ge(dve_done, marks[f"xn{p}"])
                for v in range(2):
                    for b in range(HB):
                        mm = nc.tensor.transpose(ps[:, v, b * 128:b * 128 + S], xn[:, v * HB + b, :], ident[0:S, 0:S])
                    step(mm, f"xnT{p}_{v}")

            def queries(l):
                for u in range(2 * G + 2):
                    g, v = u % 5, u // 5
                    if g == 0:
                        pe.wait_ge(act_done, ACT_MARK[f"xnT{2 * l}_{v}"])
                    if u == 0 or u == 1:
                        pe.wait_ge(act_done, ACT_MARK[f"xnT{2 * l}_1"])
                    if u >= 4:
                        pe.wait_ge(dve_done, marks[f"qread{l}_{u - 4}"])
                    w = wqr[l][:, g, :] if g < G else wq[l][:]
                    step(nc.tensor.matmul(ps[:, u % 4, 0:HALF], w, xnT[:, v * HALF:(v + 1) * HALF],
                                          start=True, stop=True), f"q{l}_{u}")

            def attention(l):
                s, blocks = A[l], MAX_BLOCKS[l]

                def k_chunk(b, c, par):
                    lo, w = CHUNKS[c]
                    if c == 0:
                        pe.wait_ge(s["ctx_in"][par], landed(b, par, 2, 16))
                        if not (isinstance(b, int) and b == 0):
                            pe.wait_ge(s["negm_ready"], b * NEGM_WRITES[l])
                    else:
                        pe.wait_ge(s["klo_ready"], b * 3 + c)
                    nc.tensor.matmul(pc[:, 0:w], wk[l][:], ctxT[par][:, lo:lo + w], start=True,
                                     stop=True).then_inc(s["kproj_done"], 1)

                def v_chunk(b, c, par, tail):
                    if c == 0:
                        if tail:
                            pe.wait_ge(s["tail_step"], b * TAIL - (2 * TAIL - OUT_TAKEN))
                        else:
                            pe.wait_ge(s["klo_ready"], b * 3 + 3)
                    else:
                        pe.wait_ge(s["vraw_ready"], b * 3 + c)
                    for i in range(V_PER):
                        t = c * V_PER + i
                        mm = nc.tensor.matmul(pc[0:KEY_TILE, i * 128:(i + 1) * 128],
                                              ctxT[par][:, t * KEY_TILE:(t + 1) * KEY_TILE], wv[l][:],
                                              start=True, stop=True)
                    mm.then_inc(s["vproj_done"], 1)

                def max_chunk(b, k):
                    c, i = k // blocks, k % blocks
                    lo, w = CHUNKS[c]
                    first = i * MAX_ROWS[l]
                    rows = min(MAX_ROWS[l], HQ - first)
                    if k == 0:
                        pe.wait_ge(s["qbd_ready"], b + 1)
                    if i == 0:
                        pe.wait_ge(s["khi_ready"], b * 3 + (c + 1))
                    if not (isinstance(b, int) and b == 0 and k < 2):
                        pe.wait_ge(s["max_taken"], b * (3 * blocks) + (k - 1))
                    nc.tensor.matmul(pm[0:rows, k % 2, 0:w], qbd[:, first:first + rows], khi[:, lo:lo + w],
                                     start=True, stop=True).then_inc(s["chunk_ready"], 1)

                def max_rows(b):
                    rows = MAX_ROWS[l]
                    pe.wait_ge(s["rowmax_step"], b * 2 + 2)
                    pe.wait_ge(s["vraw_ready"], b * 3 + 3)
                    nc.tensor.transpose(pc[:, 0:rows], negm[0:rows, :], ident[0:rows, 0:rows])\
                        .then_inc(s["maxrow_ready"], 1)

                def scores(b, t, g, par):
                    r, u = rows_of(t), g // 2
                    if t == 0 and g == 0:
                        pe.wait_ge(s["kstack_in"][par], landed(b, par, 2, 192))
                        pe.wait_ge(s["qstack_ready"], b * 4 + 4)
                    if g % 2 == 0:
                        if t == 0:
                            pe.wait_ge(s["negm_ready"], b * NEGM_WRITES[l] + (NEGM_WRITES[l] if u else 1))
                        if not (isinstance(b, int) and b == 0 and t == 0):
                            pe.wait_ge(s["probs_ready"], b * (2 * KEY_TILES) + (2 * t + u - 1))
                    mm = nc.tensor.matmul(ps[0:r, g, 0:GQ], kst[par][:, g, t * KEY_TILE:t * KEY_TILE + r],
                                          qst[par][:, g * GQ:(g + 1) * GQ], start=True, stop=(l == 1))
                    if l == 0:
                        mm = nc.tensor.matmul(ps[0:r, g, 0:GQ].rearrange("p (j q) -> p j q", q=S),
                                              ident_b[0:r, 0:r],
                                              negT[0:r, t, :].unsqueeze(1).broadcast_to([r, J, S]),
                                              start=False, stop=True)
                    if g % 2 == 1:
                        mm.then_inc(s["scores_ready"], 1)

                def weigh(b, t, u, par):
                    r = rows_of(t)
                    pe.wait_ge(s["probs_ready"], b * (2 * KEY_TILES) + (2 * t + u + 1))
                    if t == 0 and u == 0:
                        pe.wait_ge(s["v_written"], (b * 3 + 3) * (1, 2)[l])
                        if not (isinstance(b, int) and b == 0):
                            pe.wait_ge(s["oraw_ready"], b)
                    for g in range(2 * u, 2 * u + 2):
                        for j in range(J):
                            h = J * g + j
                            mm = nc.tensor.matmul(po[32 * j:32 * j + 32, g * S:(g + 1) * S],
                                                  vaug[par][0:r, t, 9 * h:9 * h + 32],
                                                  probs[t % 2][0:r, h * S:(h + 1) * S],
                                                  start=(t == 0 and g == 0), stop=(t == KEY_TILES - 1),
                                                  tile_position=(0, 32 * j), skip_group_check=True)
                    if u == 1:
                        mm.then_inc(s["pv_done"], 1)

                def den(b):
                    pe.wait_ge(s["oraw_ready"], b + 1)
                    nc.tensor.matmul(pc[:, 0:GQ], den_sel[:], oraw[:], start=True, stop=True)\
                        .then_inc(s["tail_ready"], 1)

                def project(b):
                    pe.wait_ge(s["onorm_ready"], b + 1)
                    for g in range(G):
                        mm = nc.tensor.matmul(pc[0:S, 0:D], onorm[:, g * S:(g + 1) * S], wo[l][:, g, :],
                                              start=(g == 0), stop=(g == G - 1))
                    mm.then_inc(s["tail_ready"], 1)

                def slots(b, main, after, prep, par):
                    for t in range(KEY_TILES):
                        blocks_here = list(MAX_SLOTS[l][t]) if prep else []
                        count = len(blocks_here)

                        def maxima(gap):
                            for _ in range((gap + 1) * count // 6 - gap * count // 6):
                                max_chunk(b + 1, blocks_here.pop(0))

                        def weigh_before(u):
                            if main and t >= 1:
                                weigh(b, t - 1, u, par)
                            elif after and t == 0:
                                weigh(b - 1, KEY_TILES - 1, u, 1 - par)

                        if main:
                            scores(b, t, 0, par)
                        maxima(0)
                        if main:
                            scores(b, t, 1, par)
                        if prep and t < 3:
                            k_chunk(b + 1, t, 1 - par)
                        if prep and t in V_SLOTS:
                            v_chunk(b + 1, V_SLOTS.index(t), 1 - par, after)
                        if after and t == DEN_SLOT:
                            if prep:
                                pe.wait_ge(s["klo_ready"], b * 3 + 6)
                            else:
                                pe.wait_ge(s["negm_ready"], (b + 1) * NEGM_WRITES[l])
                            den(b - 1)
                        if after and t == OUT_SLOT:
                            project(b - 1)
                        maxima(1)
                        weigh_before(0)
                        maxima(2)
                        if prep and t == KEY_TILES - 1:
                            max_rows(b + 1)
                        if main:
                            scores(b, t, 2, par)
                        maxima(3)
                        if main:
                            scores(b, t, 3, par)
                        maxima(4)
                        weigh_before(1)
                        maxima(5)

                slots(-1, False, False, True, 1)
                slots(0, True, False, True, 0)
                with pe.Fori(0, (B - 2) // 2) as i:
                    for k in range(2):
                        slots(i * 2 + (1 + k), True, True, True, 1 - k)
                slots(B - 1, True, True, False, 1)
                for u in range(2):
                    weigh(B - 1, KEY_TILES - 1, u, 1)
                pe.wait_ge(s["tail_step"], TAIL * (B - 1))
                den(B - 1)
                project(B - 1)

            def experts(l):
                m = M[l]
                units = (UNITS0, UNITS1)[l]

                def gate_up(u, slot):
                    pe.wait_ge(m["w_in"][slot], landed(u, slot, RING, 48))
                    for v in range(2):
                        cols = slice(v * HALF, (v + 1) * HALF)
                        if not (isinstance(u, int) and u == 0):
                            pe.wait_ge(m["prod_done"], u * 2 + (v - 1))
                        nc.tensor.matmul(ps[:, v, 0:HALF], wts[slot][:, 0, :], xnT[:, cols], start=True,
                                         stop=True).then_inc(m["gate_ready"], 1)
                        nc.tensor.matmul(ps[:, 2 + v, 0:HALF], wts[slot][:, 1, :], xnT[:, cols], start=True,
                                         stop=True).then_inc(m["up_ready"], 1)

                def down(u, slot):
                    for v in range(2):
                        pe.wait_ge(m["h_done"], u * 2 + (v + 1))
                        nc.tensor.matmul(pm[:, v, 0:HALF], wts[slot][:, 2, :], hh[v], start=False, stop=False,
                                         skip_group_check=True).then_inc(m["down_done"], 1)

                for v in range(2):
                    nc.tensor.matmul(pm[:, v, 0:HALF], zero_b[:, 0:128], zero_b[:, 0:HALF], start=True, stop=False,
                                     skip_group_check=True)
                gate_up(0, 0)
                with pe.Fori(0, (units - 1) // RING) as i:
                    for k in range(RING):
                        gate_up(i * RING + (k + 1), (k + 1) % RING)
                        down(i * RING + k, k)
                for u in range((units - 1) // RING * RING, units):
                    if u + 1 < units:
                        gate_up(u + 1, (u + 1) % RING)
                    down(u, u % RING)
                for v in range(2):
                    mm = nc.tensor.matmul(pm[:, v, 0:HALF], zero_b[:, 0:128], zero_b[:, 0:HALF], start=False, stop=True,
                                          skip_group_check=True)
                step(mm, f"moe_sum{l}")
                pe.wait_ge(act_done, ACT_MARK[f"yT{l}"])
                for v in range(2):
                    for b in range(HB):
                        mm = nc.tensor.transpose(ps[0:S, v, b * D:(b + 1) * D], yT[:, (v * HB + b) * S:(v * HB + b + 1) * S],
                                                 ident[:])
                    step(mm, f"y{l}_{v}")

            def logits(l, w, e):
                pe.wait_ge(act_done, ACT_MARK[f"xnT{2 * l + 1}_1"])
                for b in range(B):
                    mm = nc.tensor.matmul(pc[0:S, b * e:(b + 1) * e], xnT[:, b * S:(b + 1) * S], w[:],
                                          start=True, stop=True)
                step(mm, f"logits{l}")

            def weights_across(l, e):
                pe.wait_ge(dve_done, marks[f"weights{l}"])
                w3 = rw[:, 0:B * e].rearrange("p (b e) -> p b e", e=e)
                for b in range(B):
                    mm = nc.tensor.transpose(ps[0:e, b // HB, (b % HB) * 128:(b % HB) * 128 + S], w3[:, b, :],
                                             ident[0:S, 0:S])
                step(mm, f"wT{l}")

            pe.wait_ge(consts_in, CONSTS * 16)
            pe.wait_ge(pool_init, 8)
            transpose_tokens(0)
            pe.wait_ge(dve_done, marks["any_diag"])
            step(nc.tensor.matmul(pc[:, 0:S], ones_f[0:S, :], any_diag[:], start=True, stop=True), "any_b")
            queries(0)
            pe.wait_ge(dve_done, marks["q_ready0"])
            attention(0)
            transpose_tokens(1)
            logits(0, wr0, E0)
            pe.wait_ge(dve_done, marks["chosen"])
            for b in range(B):
                for c in range(b + 1):
                    mm = nc.tensor.matmul(pc[0:S, b * E0:(b + 1) * E0], (before_b[:] if c == b else ones_b[0:S, 0:S]),
                                          rsel_b[:, c, :], start=(c == 0), stop=(c == b))
            step(mm, "ranks")
            weights_across(0, E0)
            experts(0)
            transpose_tokens(2)
            queries(1)
            pe.wait_ge(dve_done, marks["q_ready1"])
            attention(1)
            transpose_tokens(3)
            logits(1, wr1, E1)
            weights_across(1, E1)
            experts(1)

        @block.sync
        def _(sp):
            sp.dma_start(xres[:], a["x"].rearrange("b q d -> q b d")).then_inc(x_in, 16)

            def context(l, b, par):
                s = A[l]
                if not (isinstance(b, int) and b < 2):
                    sp.wait_ge(s["vproj_done"], b * 3 - 3)
                sp.dma_start(ctxT[par][:, 0:NK], a["ctxT"][bass.ds(b, 1)].rearrange("a p n -> p (a n)"))\
                    .then_inc(s["ctx_in"][par], 16)

            def stack(l, b, par):
                s = A[l]
                sp.wait_ge(s["klo_ready"], b * 3 + 3)
                if not (isinstance(b, int) and b < 2):
                    sp.wait_ge(s["pv_done"], b * KEY_TILES - KEY_TILES)
                for g in range(G):
                    for i, part in enumerate((khi, klo, khi)):
                        sp.dma_start(kst[par][32 * i:32 * i + 32, g, :].bitcast(F32),
                                     part[32 * g:32 * g + 32, :].bitcast(F32)).then_inc(s["kstack_in"][par], 16)

            context(0, 0, 0)
            for name, tile in (("ident", ident), ("head_mask", head_mask), ("head16_mask", head16_mask),
                               ("max_mask", max_mask), ("den_sel", den_sel), ("before", before),
                               ("tie_mask", tie_mask), ("gates", gates), ("wr0", wr0), ("wr1", wr1), ("ebias", ebias)):
                sp.dma_start(tile[:], a[name]).then_inc(consts_in, 16)
            for l in range(2):
                for name, tiles in (("wqr", wqr), ("wq", wq), ("wk", wk), ("wv", wv), ("wo", wo), ("bqr", bqr),
                                    ("bq", bq), ("bk", bk), ("bv", bv), ("bo", bo)):
                    sp.dma_start(tiles[l][:], a[f"{name}{l}"]).then_inc(consts_in, 16)
            sp.dma_start(mask_u[:], a["mask"]).then_inc(mask_in, 16)
            sp.wait_ge(pool_init, 1)
            full = (KEY_TILES - 1) * KEY_TILE
            sp.dma_start(maskT_u[:, 0:KEY_TILES - 1, :], a["maskT"][0:full].rearrange("(t p) q -> p t q", p=KEY_TILE))\
                .then_inc(mask_in, 16)
            sp.dma_start(maskT_u[0:LAST_ROWS, KEY_TILES - 1, :], a["maskT"][full:NK]).then_inc(mask_in, 16)
            sp.wait_ge(pool_init, 2)
            en = tmpf[0:KEY_TILE, 0:B * KEY_TILES * 8].rearrange("p (b t e) -> p b t e", b=B, e=8)
            for b in range(B):
                sp.dma_start(en[:, b, 0:KEY_TILES - 1, :],
                             a["ctxb"][b, 0:full].rearrange("(t p) e -> p t e", p=KEY_TILE)).then_inc(energy_in, 16)
                sp.dma_start(en[0:LAST_ROWS, b, KEY_TILES - 1, :], a["ctxb"][b, full:NK]).then_inc(energy_in, 16)

            def attention(l, first):
                if not first:
                    context(l, 0, 0)
                context(l, 1, 1)
                stack(l, 0, 0)
                context(l, 2, 0)
                stack(l, 1, 1)
                context(l, 3, 1)
                with sp.Fori(0, (B - 4) // 2) as i:
                    for k in range(2):
                        stack(l, i * 2 + (2 + k), k)
                        context(l, i * 2 + (4 + k), k)
                stack(l, B - 2, 0)
                stack(l, B - 1, 1)

            def experts(l):
                m = M[l]
                units = (UNITS0, UNITS1)[l]

                def load(u, slot):
                    if not (isinstance(u, int) and u < RING):
                        sp.wait_ge(m["down_done"], u * 2 - (2 * RING - 2))
                    sp.dma_start(wts[slot][:], a[f"experts{l}"][bass.ds(u, 1)].rearrange("a p c n -> p (a c) n"))\
                        .then_inc(m["w_in"][slot], 16)
                    for i in range(2):
                        row = scratch[l][bass.ds(u * 2 + i, 1), :]
                        sp.dma_start(wb[slot][64 * i:64 * i + 64, :], row.broadcast_to([64, TOK]))\
                            .then_inc(m["w_in"][slot], 16)

                sp.wait_ge(act_done, ACT_MARK[f"wT{l}"])
                if l == 0:
                    sp.dma_start(scratch[0][0:E0, :], wT).then_inc(m["w_out"], 16)
                    sp.dma_start(scratch[0][E0:E0 + 2, :].rearrange("a (b n) -> a b n", n=100),
                                 ones_f[0:2, 0:100].unsqueeze(1).broadcast_to([2, 8, 100])).then_inc(m["w_out"], 16)
                    sp.wait_ge(m["w_out"], 32)
                else:
                    rows = scratch[1].rearrange("(e s) t -> s e t", s=2 * SPLIT1)
                    for i in range(2 * SPLIT1):
                        sp.dma_start(rows[i], wT[0:E1, :]).then_inc(m["w_out"], 16)
                    sp.wait_ge(m["w_out"], 16 * 2 * SPLIT1)
                for u in range(RING):
                    load(u, u)
                with sp.Fori(0, (units - RING) // RING) as i:
                    for k in range(RING):
                        load(i * RING + (RING + k), k)
                for u in range(units // RING * RING, units):
                    load(u, u % RING)

            attention(0, True)
            experts(0)
            sp.wait_ge(dve_done, marks["moe_out0_1"])
            attention(1, False)
            experts(1)
            sp.wait_ge(dve_done, marks["moe_out1_1"])
            sp.dma_start(out.rearrange("b q d -> q b d"), xres[:]).then_inc(out_done, 16)
            sp.wait_ge(out_done, 16)


_IN = ["x", "ctxT", "ctxb", "mask", "maskT", "ident", "head_mask", "head16_mask", "max_mask", "den_sel", "before",
       "tie_mask", "gates", "wr0", "wr1", "ebias", "experts0", "experts1"] + [
    f"{n}{l}" for l in range(2) for n in ("wqr", "wq", "wk", "wv", "wo", "bqr", "bq", "bk", "bv", "bo")]


def kernel(**inputs):
    import numpy as np
    import concourse.bacc as bacc
    from concourse.bass_utils import run_bass_kernel_spmd

    i = {k: np.asarray(v) for k, v in inputs.items()}
    a = {"x": i["x"], "ctxT": i["ctx_1024"].transpose(0, 2, 1), "ctxb": i["ctxb_2048x8"]}
    mask = i["mask_1x1xSxS2_bk0"][0, 0]
    a["mask"], a["maskT"] = mask, mask.T

    f = np.float32
    row = np.arange(128)
    a["ident"] = np.eye(128, dtype=f)
    a["head_mask"] = ((row[:, None] % 32 // DH == np.arange(J)) & (row[:, None] < 96)).astype(f)
    a["head16_mask"] = (row[:, None] // DH == np.arange(H)).astype(f)
    a["max_mask"] = (row[:, None] - 96 == np.arange(H)).astype(f)
    a["den_sel"] = (row[:, None] == row // 32 * 32 + DH).astype(f)
    a["before"] = (row[:S, None] < row[:S]).astype(f)
    a["tie_mask"] = np.ascontiguousarray(np.broadcast_to((np.arange(8) < np.arange(8)[:, None]).astype(f), (S, 8, 8)))

    a["gates"] = np.broadcast_to(np.concatenate([i["g_xattn"], i["g_ffn"]]), (128, 4))
    for l in range(2):
        w = {n: i[f"L{l}_xattn_W{n}"] for n in "qkvo"}
        if l == 0:
            w = {n: m.T for n, m in w.items()}
        b = {n: i[f"L{l}_xattn_b{n}"] for n in "qkvo"}
        a[f"wqr{l}"] = np.tile(w["q"].reshape(128, G, 1, 32), (1, 1, 4, 1)).reshape(128, G, 128)
        a[f"wq{l}"], a[f"wk{l}"], a[f"wv{l}"] = w["q"], w["k"], w["v"]
        wo = np.zeros((J, 32, G, D), f)
        wo[:, 0:DH] = w["o"].reshape(G, J, DH, D).transpose(1, 2, 0, 3)
        a[f"wo{l}"] = wo.reshape(128, G, D)
        a[f"bqr{l}"] = np.tile(b["q"].reshape(G, 32), (1, 4)).T
        a[f"bq{l}"], a[f"bk{l}"] = b["q"][:, None], b["k"][:, None]
        a[f"bv{l}"], a[f"bo{l}"] = np.broadcast_to(b["v"], (128, 128)), np.broadcast_to(b["o"], (128, 128))
    a["wr0"], a["wr1"] = i["L0_ffn_gate_weight"].T, i["L1_ffn_router_w"].T
    a["ebias"] = np.broadcast_to(i["L0_ffn_e_bias"], (S, E0))

    ex = np.zeros((UNITS0, 128, 3, 128), f)
    ex[:-1, :, 0] = i["L0_ffn_w1"].reshape(-1, 128, D).transpose(0, 2, 1)
    ex[:-1, :, 1] = i["L0_ffn_w3"].reshape(-1, 128, D).transpose(0, 2, 1)
    ex[:-1, :, 2] = i["L0_ffn_w2"].transpose(0, 2, 1).reshape(-1, 128, D)
    ex[-1, :, 0], ex[-1, :, 1], ex[-1, :, 2] = (i["L0_ffn_shared_gate"].T, i["L0_ffn_shared_up"].T,
                                                i["L0_ffn_shared_down"].T)
    a["experts0"] = ex
    part = I1 // SPLIT1 + 1
    ex = np.zeros((E1, SPLIT1, 128, 3, 128), f)
    for k in range(SPLIT1):
        lo, hi = k * part, min((k + 1) * part, I1)
        ex[:, k, :, 0, :hi - lo] = i["L1_ffn_gate_w"][:, lo:hi].transpose(0, 2, 1)
        ex[:, k, :, 1, :hi - lo] = i["L1_ffn_up_w"][:, lo:hi].transpose(0, 2, 1)
        ex[:, k, :hi - lo, 2] = i["L1_ffn_down_w"][:, :, lo:hi].transpose(0, 2, 1)
    a["experts1"] = ex.reshape(UNITS1, 128, 3, 128)

    nc = bacc.Bacc("TRN2", target_bir_lowering=False, num_devices=1)
    arrays, aps = {}, {}
    for name in _IN:
        arr = np.ascontiguousarray(a[name])
        arrays[f"in_{name}"] = arr
        aps[name] = nc.dram_tensor(f"in_{name}", arr.shape, mybir.dt.from_np(arr.dtype), kind="ExternalInput").ap()
    out = nc.dram_tensor("out_dram", (B, S, D), F32, kind="ExternalOutput").ap()
    scratch = [nc.dram_tensor(f"routing{l}", (2 * (UNITS0, UNITS1)[l], TOK), F32, kind="Internal").ap() for l in range(2)]
    flamingo(nc, aps, out, scratch)
    r = run_bass_kernel_spmd(nc, [arrays], core_ids=[0])
    return r.results[0]["out_dram"]
```

```python
from contextlib import ExitStack

import concourse.bass as bass
from concourse import mybir

F32 = mybir.dt.float32
F32R = mybir.dt.float32r
BF16 = mybir.dt.bfloat16
U8 = mybir.dt.uint8
ALU = mybir.AluOpType
ACT = mybir.ActivationFunctionType
AX = mybir.AxisListType.X

B, S, D = 8, 100, 128
NK = 1444
KEY_TILE = 121
KEY_TILES = -(-NK // KEY_TILE)
LAST_ROWS = NK - (KEY_TILES - 1) * KEY_TILE
NKP = KEY_TILES * KEY_TILE
H, DH, G, J = 16, 8, 4, 4
HQ = H * S
GQ = J * S
CHUNKS = [(0, 482), (482, 482), (964, 480)]
V_CHUNKS = 3
V_PER = KEY_TILES // V_CHUNKS
SCALE = float(DH) ** -0.5
BIG = 1e30
EPS = 1e-5
TOK = B * S
HALF = TOK // 2
HB = B // 2

E0, F0 = 64, 64
NG, PER_G, TOP_G, TOP_E = 8, 8, 4, 8
CAP = 128.0
ROUTE_SCALE = 2.5
UNITS0 = E0 // 2 + 1
E1, I1 = 8, 352
UNITS1 = E1 * I1 // 128
STRETCHES = [128 // F0, 4]
RING = 4

MAX_ROWS = [S, 128]
MAX_BLOCKS = [H, -(-HQ // 128)]
MAX_PER_SLOT = [[1, 4, 4, 4, 4, 4, 4, 5, 6, 6, 6, 0], [0, 4, 4, 3, 3, 3, 3, 4, 5, 5, 5, 0]]
MAX_SLOTS = [[range(sum(m[:t]), sum(m[:t + 1])) for t in range(KEY_TILES)] for m in MAX_PER_SLOT]
V_SLOTS = [8, 9, 10]
DEN_SLOT, OUT_SLOT = 3, 7
RECIPROCAL_SLOTS = {3: [0], 4: [1], 5: [2], 6: [3]}
BESIDE_AFTER = {1: 1, 2: 1, DEN_SLOT: 2}
SCORES_WORK, WEIGH_WORK, K_WORK, V_WORK, DEN_WORK, OUT_WORK, TURN_WORK = (34, 17), 30, 80, 100, 67, 100, 10
NEGM_WRITES = [[(J * g, J * g + J, S) for g in range(G)], [(0, 4, 128), (4, 7, 128), (7, 10, 128), (10, 12, 128),
                                                           (12, 13, HQ - 12 * 128)]]
IN_FLIGHT, IN_FLIGHT_FIRST = 2, 4
TAIL = G + 3
OUT_TAKEN = G + 1
PARTS = {"a": (0, 6), "b": (6, 8)}
TURN_SLOT, LOGITS_SLOT = 4, 6


def rows_of(t):
    return KEY_TILE if t < KEY_TILES - 1 else LAST_ROWS


def landed(n, slot, ring, each):
    return n * (each // ring) + (each - slot * (each // ring))


CONSTS_EARLY = ["wk0", "bk0", "wv0", "ident", "wq0", "bq0", "head16_mask"]
CONSTS_LATE = ["head_mask", "bv0", "max_mask", "den_sel", "gates", "wo0", "bo0", "before", "tie_mask", "wr0", "ebias",
               "wk1", "bk1", "wv1", "wq1", "bq1", "bv1", "wo1", "bo1", "wr1"]
PE_STEPS = ["xnT0_0", "xnT0_1", "any_b", "q0_0", "q0_1",
            "xnT1a_0", "xnT1a_1", "logits0a", "xnT1b", "logits0b", "ranks", "wT0", "moe_sum0", "y0_0", "y0_1", "xnT2_0", "xnT2_1", "q1_0", "q1_1",
            "xnT3a_0", "xnT3a_1", "logits1a", "xnT3b", "logits1b", "wT1", "moe_sum1", "y1_0", "y1_1"]
ACT_STEPS = ["root0", "xnT0_0", "xnT0_1", "tanh", "energy_exp",
             "root1a", "xnT1a_0", "xnT1a_1", "router0a", "root1b", "xnT1b", "router0b", "wT0", "yT0",
             "root2", "xnT2_0", "xnT2_1",
             "root3a", "xnT3a_0", "xnT3a_1", "root3b", "xnT3b", "router1", "wT1", "yT1"]
PE_MARK = {name: i + 1 for i, name in enumerate(PE_STEPS)}
ACT_MARK = {name: i + 1 for i, name in enumerate(ACT_STEPS)}


def flamingo(nc, a, out, scratch):
    with ExitStack() as ctx:
        def sb(name, shape, dt=F32):
            return ctx.enter_context(nc.sbuf_tensor(name, shape, dt))

        def sem(name):
            return ctx.enter_context(nc.semaphore(name))

        ident = sb("ident", [128, 128])
        ident_b = sb("ident_b", [128, 128], BF16)
        head_mask = sb("head_mask", [128, J])
        head16_mask = sb("head16_mask", [128, H])
        max_mask = sb("max_mask", [128, H])
        den_sel = sb("den_sel", [128, 128])
        before = sb("before", [100, S])
        before_b = sb("before_b", [100, S], BF16)
        ones_b = sb("ones_b", [128, 128], BF16)
        ones_f = sb("ones_f", [128, 128])
        zero_b = sb("zero_b", [128, 512], BF16)
        tie_mask = sb("tie_mask", [100, 8, 8])
        gates = sb("gates", [128, 4])
        tgates = sb("tgates", [128, 4])
        wq = [sb(f"wq{l}", [128, 128]) for l in range(2)]
        wk = [sb(f"wk{l}", [128, 128]) for l in range(2)]
        wv = [sb(f"wv{l}", [128, 128]) for l in range(2)]
        wo = [sb(f"wo{l}", [128, G, 128]) for l in range(2)]
        bq = [sb(f"bq{l}", [128, 1]) for l in range(2)]
        bk = [sb(f"bk{l}", [128, 1]) for l in range(2)]
        bv = [sb(f"bv{l}", [128, 128]) for l in range(2)]
        bo = [sb(f"bo{l}", [128, 128]) for l in range(2)]
        wr0 = sb("wr0", [128, E0])
        wr1 = sb("wr1", [128, E1])
        ebias = sb("ebias", [100, E0])

        xres = sb("xres", [100, B, D])
        xn = sb("xn", [100, B, D])
        xnT = sb("xnT", [128, TOK])
        stats = sb("stats", [100, B, 6])
        mv = sb("mv", [100, B, 2])
        rstd = sb("rstd", [100, B])
        var = sb("var", [100, B])
        fix = sb("fix", [100, B])

        mask_u = sb("mask_u", [100, NK], U8)
        maskT_u = sb("maskT_u", [KEY_TILE, KEY_TILES, S], U8)
        negq = sb("negq", [100, NK], BF16)
        any_q = sb("any_q", [100, 1])
        any_big = sb("any_big", [100, 1])
        any_diag = sb("any_diag", [100, S])
        any_b = sb("any_b", [128, S])
        negT = sb("negT", [KEY_TILE, KEY_TILES, S], BF16)
        egate = sb("egate", [KEY_TILE, B * KEY_TILES])

        ctxT = [sb(f"ctxT{i}", [128, NKP]) for i in range(2)]
        khi = sb("khi", [128, NK], F32R)
        klo = sb("klo", [128, NK], F32R)
        kst = [sb(f"kst{i}", [128, G, NK], F32R) for i in range(2)]
        vraw = [sb(f"vraw{i}", [KEY_TILE, V_PER, 128]) for i in range(2)]
        vaug = [sb(f"vaug{i}", [128, KEY_TILES, H * 9 + 24]) for i in range(2)]
        qsel = sb("qsel", [128, G, TOK], F32R)
        qhi = sb("qhi", [128, TOK], F32R)
        qlo = sb("qlo", [128, TOK], F32R)
        qst = [sb(f"qst{i}", [128, HQ], F32R) for i in range(2)]
        qbd = sb("qbd", [128, HQ], F32R)
        mx_part = sb("mx_part", [128, H, len(CHUNKS)])
        negm = sb("negm", [128, 128])
        junk = sb("junk", [100, 2, 512], BF16)
        probs = [sb(f"probs{i}", [KEY_TILE, HQ]) for i in range(2)]
        oraw = sb("oraw", [128, GQ])
        rden = sb("rden", [128, GQ])
        onorm = sb("onorm", [128, GQ])

        tmpf = sb("tmpf", [128, NKP])
        t2 = sb("t2", [128, 512])
        q_f32 = [t2[:, 0:HALF], tmpf[:, 2 * HALF:3 * HALF]]

        def over(host, off, shape, dt=F32):
            n = 1
            for s in shape[1:]:
                n *= s
            flat = host[:].bitcast(dt) if host.dtype != dt else host[:]
            if len(host.shape) == 3:
                flat = flat.rearrange("p a b -> p (a b)")
            v = flat[0:shape[0], off:off + n]
            if len(shape) == 3:
                v = v.rearrange("p (a b) -> p a b", b=shape[2])
            if len(shape) == 4:
                v = v.rearrange("p (a b c) -> p a b c", b=shape[2], c=shape[3])
            return v

        wts = [sb(f"wts{i}", [128, 3, 128]) for i in range(RING)]
        wb = [sb(f"wb{i}", [128, TOK]) for i in range(RING)]
        sg = [over(tmpf, v * HALF, [128, HALF]) for v in range(2)]
        tu = [over(vaug[0], TOK + v * HALF, [128, HALF]) for v in range(2)]
        hw = [over(tmpf, 2 * HALF, [128, HALF]), over(t2, 0, [128, HALF])]
        x_hi, x_lo = over(qsel, 0, [128, TOK], F32R), over(qsel, TOK, [128, TOK], F32R)
        h_hi = [over(qsel, 2 * TOK + v * HALF, [128, HALF], F32R) for v in range(2)]
        h_lo = [over(qsel, 3 * TOK + v * HALF, [128, HALF], F32R) for v in range(2)]
        w_hi = [over(qst[k // 2], k % 2 * 768, [128, 3, 128], F32R) for k in range(RING)]
        w_lo = [over(qst[k // 2], k % 2 * 768 + 384, [128, 3, 128], F32R) for k in range(RING)]
        yT = over(vaug[0], 0, [128, TOK])
        rt = [over(ctxT[0], 0, [100, B * E0]), over(ctxT[0], B * E0, [100, B * E0])]
        rsc = over(ctxT[1], 0, [100, B * E0])
        rw = over(ctxT[1], B * E0, [100, B * E0])
        rsel = over(vaug[0], 0, [100, B * E0])
        rsel_b = over(junk, 0, [100, B, E0], BF16)
        top8 = over(vaug[0], B * E0, [100, B * NG, 8])
        gsc = sb("gsc", [100, B * NG])
        gsel = sb("gsel", [100, B * NG])
        rsum = sb("rsum", [100, B])
        wT = over(vaug[1], 0, [64, TOK])

        ps = ctx.enter_context(nc.psum_tensor("ps", [128, 4, 512], F32))
        po = ctx.enter_context(nc.psum_tensor("po", [128, 512], F32))
        pm = ctx.enter_context(nc.psum_tensor("pm", [128, 2, 512], F32))
        pc = ctx.enter_context(nc.psum_tensor("pc", [128, 512], F32))

        first_k_bank = [pc[:], ps[:, 2, :], ps[:, 3, :]]
        first_v_bank = [pm[:, 0, :], pm[:, 1, :], po[:]]

        def max_bank(b, k):
            if isinstance(b, int) and b == 0:
                return (pm[:, 0, :], pm[:, 1, :], ps[:, 2, :], ps[:, 3, :])[k % IN_FLIGHT_FIRST]
            return pm[:, k % IN_FLIGHT, :]

        logits_of = {"a": pm[:, 0, :], "b": pm[:, 1, :]}
        logits_at = pm[:, 0, :]

        consts_early = sem("consts_early")
        consts_late = sem("consts_late")
        x_in = sem("x_in")
        mask_in = sem("mask_in")
        energy_in = sem("energy_in")
        dve_done = sem("dve_done")
        act_done = sem("act_done")
        pe_done = sem("pe_done")
        pool_init = sem("pool_init")
        A = [dict((n, sem(f"{n}{l}")) for n in (
            "scores_ready", "probs_ready", "pv_done", "oraw_ready", "chunk_ready", "max_taken", "tail_ready",
            "khi_ready", "klo_ready", "vraw_ready", "v_written", "qstack_ready", "qbd_ready", "negm_ready",
            "maxrow_ready", "kproj_done", "vproj_done", "onorm_ready", "tail_step", "rowmax_step", "chunk_seen")) for l in range(2)]
        for l in range(2):
            for n in ("ctx_in", "kstack_in"):
                A[l][n] = [sem(f"{n}{l}_{i}") for i in range(2)]
            A[l]["qsel_in"] = sem(f"qsel_in{l}")
        M = [dict((n, sem(f"m{n}{l}")) for n in (
            "gate_ready", "up_ready", "silu_done", "prod_done", "weighted", "h_high", "h_low", "w_high", "w_low",
            "down_done", "w_out")) for l in range(2)]
        for l in range(2):
            M[l]["w_in"] = [sem(f"w_in{l}_{i}") for i in range(RING)]
            M[l]["wb_in"] = [sem(f"wb_in{l}_{i}") for i in range(RING)]
        out_done = sem("out_done")

        block = ctx.enter_context(nc.Block())

        marks = {}

        @block.vector
        def _(dve):
            n = [0]

            def step(ins, name=None):
                n[0] += 1
                ins.then_inc(dve_done, 1)
                dve.wait_ge(dve_done, n[0])
                if name:
                    marks[name] = n[0]

            def several(instructions, name=None):
                for ins in instructions:
                    n[0] += 1
                    ins.then_inc(dve_done, 1)
                dve.wait_ge(dve_done, n[0])
                if name:
                    marks[name] = n[0]

            def layer_norm(p, part=""):
                b0, b1 = PARTS.get(part, (0, B))
                several(nc.vector.bn_stats(stats[:, b, :], xres[:, b, :]) for b in range(b0, b1))
                several(nc.vector.bn_aggr(mv[:, b, :], stats[:, b, :]) for b in range(b0, b1))
                v, r, f = var[:, b0:b1], rstd[:, b0:b1], fix[:, b0:b1]
                step(nc.vector.tensor_scalar(v, mv[:, b0:b1, 1], EPS, None, ALU.add), f"var{p}{part}")
                dve.wait_ge(act_done, ACT_MARK[f"root{p}{part}"])
                step(nc.vector.reciprocal(r, r))
                step(nc.vector.tensor_tensor(f, r, r, ALU.mult))
                step(nc.vector.tensor_tensor(f, f, v, ALU.mult))
                step(nc.vector.tensor_scalar(f, f, -0.5, 1.5, ALU.mult, ALU.add))
                step(nc.vector.tensor_tensor(r, r, f, ALU.mult))
                for lo in range(b0, b1, HB):
                    several((nc.vector.tensor_scalar(xn[:, b, :], xres[:, b, :], mv[:, b, 0:1], rstd[:, b:b + 1],
                                                     ALU.subtract, ALU.mult) for b in range(lo, min(lo + HB, b1))),
                            f"xn{p}{part}_{(lo - b0) // HB}")

            def first_k_low(l):
                for c, (lo, w) in enumerate(CHUNKS):
                    dve.wait_ge(A[l]["khi_ready"], c + 1)
                    nc.vector.scalar_tensor_tensor(klo[:, lo:lo + w], first_k_bank[c][:, 0:w], bk[l][:, 0:1],
                                                   khi[:, lo:lo + w], ALU.add, ALU.subtract)\
                        .then_inc(A[l]["klo_ready"], 1)

            def mask_rows():
                dve.wait_ge(mask_in, 48)
                step(nc.vector.tensor_reduce(any_q[:], mask_u[:], AX, ALU.max))
                several([nc.vector.tensor_scalar(any_big[:], any_q[:], BIG, None, ALU.mult),
                         nc.vector.tensor_scalar(any_diag[:], ident[0:S, 0:S], any_q[:, 0:1], None, ALU.mult)], "any_diag")
                dve.wait_ge(pe_done, PE_MARK["any_b"])
                step(nc.vector.tensor_copy(any_b[:], pc[:, 0:S]), "any_b")

            def mask_fill():
                several([nc.vector.tensor_scalar(negq[:], mask_u[:], 1.0, any_big[:, 0:1], ALU.subtract, ALU.mult),
                         nc.vector.tensor_copy(ident_b[:], ident[:])])

            def queries(l):
                for v in range(2):
                    cols = slice(v * HALF, (v + 1) * HALF)
                    keep = (any_b if l == 0 else ones_f)[:, 0:S].unsqueeze(1).broadcast_to([128, HB, S])
                    dve.wait_ge(pe_done, PE_MARK[f"q{l}_{v}"])
                    step(nc.vector.scalar_tensor_tensor(q_f32[v].rearrange("p (b q) -> p b q", q=S),
                                                        ps[:, v, 0:HALF].rearrange("p (b q) -> p b q", q=S),
                                                        bq[l][:, 0:1], keep, ALU.add, ALU.mult))
                    step(nc.vector.tensor_copy(qhi[:, cols], q_f32[v]), f"qhi{l}")
                several((nc.vector.tensor_tensor(qlo[:, v * HALF:(v + 1) * HALF], q_f32[v],
                                                 qhi[:, v * HALF:(v + 1) * HALF], ALU.subtract) for v in range(2)),
                        f"q_ready{l}")

            def energy_gates():
                dve.wait_ge(energy_in, 32 * B)
                en = tmpf[0:KEY_TILE, 0:B * KEY_TILES * 8].rearrange("p (t e) -> p t e", e=8)
                step(nc.vector.scalar_tensor_tensor(en, en, -1.0, en, ALU.mult, ALU.max))
                step(nc.vector.tensor_reduce(egate[:], en, AX, ALU.add))
                step(nc.vector.tensor_scalar(egate[:], egate[:], 10.0 / 8.0, -1.0, ALU.mult, ALU.add), "energy")
                dve.wait_ge(act_done, ACT_MARK["energy_exp"])
                step(nc.vector.tensor_scalar(egate[:], egate[:], 1.0, None, ALU.add))
                step(nc.vector.reciprocal(egate[:], egate[:]), "gate_ready")

            several([nc.vector.memset(ones_b[:], 1.0), nc.vector.memset(ones_f[:], 1.0), nc.vector.memset(zero_b[:], 0.0),
                     nc.vector.memset(negm[:], 0.0), nc.vector.memset(mx_part[:], 0.0)])
            dve.wait_ge(x_in, 16)
            layer_norm(0)

            def attention(l):
                s, blocks = A[l], MAX_BLOCKS[l]

                def k_low(b, c):
                    lo, w = CHUNKS[c]
                    dve.wait_ge(s["khi_ready"], b * 3 + (c + 1))
                    nc.vector.scalar_tensor_tensor(klo[:, lo:lo + w], pc[:, 0:w], bk[l][:, 0:1], khi[:, lo:lo + w],
                                                   ALU.add, ALU.subtract).then_inc(s["klo_ready"], 1)

                def chunk_max(b, k):
                    c, i = k // blocks, k % blocks
                    lo, w = CHUNKS[c]
                    rows = min(MAX_ROWS[l], HQ - i * MAX_ROWS[l])
                    dve.wait_ge(s["chunk_ready"], b * (3 * blocks) + (k + 1))
                    if l == 0:
                        if not (isinstance(b, int) and b == 0 and k < 2):
                            dve.wait_ge(s["max_taken"], b * (3 * blocks) + (k - 1))
                        dve.sem_inc(s["chunk_seen"], 1)
                        ins = nc.vector.tensor_tensor_reduce(junk[:, k % 2, 0:w], max_bank(b, k)[0:S, 0:w], negq[:, lo:lo + w],
                                                             1.0, -3e38, ALU.add, ALU.max, mx_part[0:S, i, c:c + 1])
                    else:
                        ins = nc.vector.tensor_reduce(mx_part[0:rows, i, c:c + 1], max_bank(b, k)[0:rows, 0:w], AX, ALU.max)
                    ins.then_inc(s["max_taken"], 1)

                def row_max(b, par):
                    rows = MAX_ROWS[l]
                    dve.wait_ge(s["max_taken"], b * (3 * blocks) + 3 * blocks)
                    nc.vector.tensor_reduce(negm[0:rows, 96:96 + blocks], mx_part[0:rows, 0:blocks, :], AX,
                                            ALU.max).then_inc(s["rowmax_step"], 1)
                    dve.wait_ge(s["rowmax_step"], b * 2 + 1)
                    nc.vector.tensor_scalar(negm[0:rows, 96:96 + blocks], negm[0:rows, 96:96 + blocks], -1.0, None,
                                            ALU.mult).then_inc(s["rowmax_step"], 1)
                    dve.wait_ge(s["maxrow_ready"], b + 1)
                    if not (isinstance(b, int) and b < 2):
                        dve.wait_ge(s["pv_done"], b * KEY_TILES - KEY_TILES)
                    for lo, hi, w in NEGM_WRITES[l]:
                        nc.vector.tensor_tensor(qst[par][96:128, lo * rows:lo * rows + (hi - lo) * w]
                                                .rearrange("p (h q) -> p h q", q=w),
                                                pc[96:128, 0:w].unsqueeze(1).broadcast_to([32, hi - lo, w]),
                                                max_mask[96:128, lo:hi].unsqueeze(2).broadcast_to([32, hi - lo, w]),
                                                ALU.mult).then_inc(s["negm_ready"], 1)

                def reciprocals(b, g):
                    cols = slice(g * S, (g + 1) * S)
                    dve.wait_ge(s["tail_ready"], 2 * b + 1)
                    nc.vector.reciprocal(rden[:, cols], pc[:, cols]).then_inc(s["tail_step"], 1)

                def normalise(b):
                    dve.wait_ge(s["tail_step"], b * TAIL + G)
                    dve.wait_ge(s["oraw_ready"], b + 1)
                    nc.vector.tensor_tensor(onorm[:], oraw[:], rden[:], ALU.mult).then_inc(s["onorm_ready"], 1)

                def add_out(b):
                    dve.wait_ge(s["tail_ready"], 2 * b + 2)
                    nc.vector.tensor_tensor(t2[0:S, 0:D], pc[0:S, 0:D], bo[l][0:S, :], ALU.add)\
                        .then_inc(s["tail_step"], 1)
                    dve.wait_ge(s["tail_step"], b * TAIL + OUT_TAKEN)
                    nc.vector.tensor_scalar(t2[0:S, D:2 * D], t2[0:S, 0:D], tgates[0:S, l:l + 1], None, ALU.mult)\
                        .then_inc(s["tail_step"], 1)
                    dve.wait_ge(s["tail_step"], b * TAIL + OUT_TAKEN + 1)
                    xb = xres[:, bass.ds(b, 1), :]
                    nc.vector.tensor_tensor(xb, t2[0:S, D:2 * D].unsqueeze(1), xb, ALU.add)\
                        .then_inc(s["tail_step"], 1)

                def beside(b, t, main, tail):
                    if main and 0 < t < 3:
                        k_low(b + 1, t)
                    if tail:
                        for g in RECIPROCAL_SLOTS.get(t, []):
                            reciprocals(b - 1, g)

                def slots(b, main, tail, par):
                    for t in range(KEY_TILES):
                        if main and t == 0:
                            k_low(b + 1, 0)
                        for i, k in enumerate(MAX_SLOTS[l][t]):
                            chunk_max(b + 1, k)
                            if i == BESIDE_AFTER.get(t, 0):
                                beside(b, t, main, tail)
                            if tail and t == max(RECIPROCAL_SLOTS) and i == 1:
                                normalise(b - 1)
                        if tail and t == OUT_SLOT:
                            add_out(b - 1)
                    row_max(b + 1, 1 - par)

                slots(-1, False, False, 1)
                slots(0, True, False, 0)
                if l == 0:
                    energy_gates()
                with dve.Fori(0, (B - 2) // 2) as i:
                    for k in range(2):
                        slots(i * 2 + (1 + k), True, True, 1 - k)
                layer_norm(2 * l + 1, "a")
                for g in range(G):
                    reciprocals(B - 2, g)
                normalise(B - 2)
                dve.wait_ge(s["vproj_done"], V_CHUNKS * B)
                dve.wait_ge(s["qstack_ready"], G * B)
                dve.wait_ge(s["pv_done"], KEY_TILES * (B - 1))
                split_tokens(l, "a")
                if l == 0:
                    route0("a")
                add_out(B - 2)
                for g in range(G):
                    reciprocals(B - 1, g)
                normalise(B - 1)
                add_out(B - 1)
                dve.wait_ge(s["tail_step"], TAIL * B)

            def weights_low(l, u, slot):
                dve.wait_ge(M[l]["w_high"], u + 1)
                nc.vector.tensor_tensor(w_lo[slot], wts[slot][:], w_hi[slot], ALU.subtract).then_inc(M[l]["w_low"], 1)

            def experts(l):
                m = M[l]

                def hidden_low(u, v):
                    dve.wait_ge(m["h_high"], u * 2 + (v + 1))
                    nc.vector.tensor_tensor(h_lo[v], hw[v], h_hi[v], ALU.subtract).then_inc(m["h_low"], 1)

                def prod(u, v):
                    dve.wait_ge(m["silu_done"], u * 2 + (v + 1))
                    dve.wait_ge(m["up_ready"], u * 2 + (v + 1))
                    if not (isinstance(u, int) and u == 0):
                        dve.wait_ge(m["weighted"], u * 2 + (v - 1))
                    nc.vector.tensor_tensor(tu[v], ps[:, 2 + v, 0:HALF], sg[v], ALU.mult)\
                        .then_inc(m["prod_done"], 1)

                units = (UNITS0, UNITS1)[l]

                def unit(u, slot):
                    for v in range(2):
                        if not (isinstance(u, int) and u == 0):
                            hidden_low(u - 1, v)
                        prod(u, v)
                    if not (isinstance(u, int) and u + 2 >= units):
                        weights_low(l, u + 2, (slot + 2) % RING)

                unit(0, 0)
                unit(1, 1)
                with dve.Fori(0, (units - 4) // RING) as i:
                    for k in range(RING):
                        unit(i * RING + (k + 2), (k + 2) % RING)
                for u in range((units - 4) // RING * RING + 2, units):
                    unit(u, u % RING)
                for v in range(2):
                    hidden_low(units - 1, v)
                for v in range(2):
                    dve.wait_ge(pe_done, PE_MARK[f"y{l}_{v}"])
                    xh = xres[:, v * HB:(v + 1) * HB, :]
                    step(nc.vector.scalar_tensor_tensor(
                        xh, ps[0:S, v, :].rearrange("p (b d) -> p b d", d=D), tgates[0:S, 2 + l:3 + l], xh,
                        ALU.mult, ALU.add), f"moe_out{l}_{v}")

            def split_tokens(l, part):
                b0, b1 = PARTS[part]
                cols = slice(b0 * S, b1 * S)
                dve.wait_ge(act_done, ACT_MARK[f"xnT{2 * l + 1}{part}" + ("_1" if part == "a" else "")])
                step(nc.vector.tensor_copy(x_hi[:, cols], xnT[:, cols]))
                step(nc.vector.tensor_tensor(x_lo[:, cols], xnT[:, cols], x_hi[:, cols], ALU.subtract), f"tokens{l}{part}")

            def route0(part):
                b0, b1 = PARTS[part]
                nb = b1 - b0
                t0, t1, sc, sel, w = (x[:, b0 * E0:b1 * E0] for x in (rt[0], rt[1], rsc, rsel, rw))
                r3 = lambda ap: ap.rearrange("p (b e) -> p b e", e=E0)
                r4 = lambda ap: ap.rearrange("p (g e) -> p g e", e=PER_G)
                groups = slice(b0 * NG, b1 * NG)
                g3 = lambda ap: ap[:, groups].rearrange("p (b g) -> p b g", g=NG)
                dve.wait_ge(act_done, ACT_MARK[f"router0{part}"])
                step(nc.vector.tensor_scalar(t0, sc, 1.0, None, ALU.add))
                step(nc.vector.reciprocal(sc, t0))
                step(nc.vector.tensor_tensor(r3(t0), r3(sc), ebias[:].unsqueeze(1).broadcast_to([100, nb, E0]), ALU.add))
                several(nc.vector.max(top8[:, b0 * NG + j, :], t0[:, j * PER_G:(j + 1) * PER_G]) for j in range(nb * NG))
                step(nc.vector.tensor_tensor(gsc[:, groups], top8[:, groups, 0], top8[:, groups, 1], ALU.add))
                best_of(g3(gsc), g3(gsel), TOP_G, b0, nb)
                step(nc.vector.tensor_tensor(r4(t1), r4(t0), gsel[:, groups].unsqueeze(2)
                                             .broadcast_to([100, nb * NG, PER_G]), ALU.mult))
                several(nc.vector.max(top8[:, b0 * NG + b, :], r3(t1)[:, b, :]) for b in range(nb))
                several(nc.vector.match_replace(r3(t0)[:, b, :], top8[:, b0 * NG + b, :], r3(t1)[:, b, :], -BIG)
                        for b in range(nb))
                step(nc.vector.tensor_scalar(sel, t0, -BIG, None, ALU.is_equal))
                several([nc.vector.tensor_copy(rsel_b[:, b0:b1, :], r3(sel)),
                         nc.vector.tensor_tensor(w, sel, sc, ALU.mult)], f"chosen{part}")

            def weights0():
                r3 = lambda ap: ap.rearrange("p (b e) -> p b e", e=E0)
                step(nc.vector.tensor_reduce(rsum[:], r3(rw), AX, ALU.add))
                step(nc.vector.tensor_scalar(rsum[:], rsum[:], 1e-20, None, ALU.add))
                step(nc.vector.reciprocal(rsum[:], rsum[:]))
                step(nc.vector.tensor_scalar(rsum[:], rsum[:], ROUTE_SCALE, None, ALU.mult))
                step(nc.vector.tensor_tensor(r3(rw), r3(rw), rsum[:].unsqueeze(2).broadcast_to([100, B, E0]), ALU.mult))
                dve.wait_ge(pe_done, PE_MARK["ranks"])
                step(nc.vector.tensor_scalar(rt[1], pc[0:S, :], CAP, None, ALU.is_lt))
                step(nc.vector.tensor_tensor(rw, rw, rt[1], ALU.mult), "weights0")

            def best_of(vals, sel, top, b0, nb):
                shape = [100, nb, 8, 8]
                t0, t1 = over(xn, b0 * D, shape), over(xn, b0 * D + nb * 64, shape)
                mine, other = vals.unsqueeze(3).broadcast_to(shape), vals.unsqueeze(2).broadcast_to(shape)
                several([nc.vector.tensor_tensor(t0, other, mine, ALU.is_gt),
                         nc.vector.tensor_tensor(t1, other, mine, ALU.is_equal)])
                step(nc.vector.tensor_tensor(t1, t1, tie_mask[:].unsqueeze(1).broadcast_to(shape), ALU.mult))
                step(nc.vector.tensor_tensor(t0, t0, t1, ALU.add))
                step(nc.vector.tensor_reduce(sel, t0, AX, ALU.add))
                step(nc.vector.tensor_scalar(sel, sel, float(top), None, ALU.is_lt))

            def route1():
                r3 = lambda ap: ap.rearrange("p (b e) -> p b e", e=E1)
                lg, ex, sl = rt[0][:, 0:B * E1], rt[0][:, 64:128], rt[0][:, 128:192]
                dve.wait_ge(pe_done, PE_MARK["logits1b"])
                step(nc.vector.tensor_reduce(rsum[:], logits_at[0:S, 0:B * E1].rearrange("p (b e) -> p b e", e=E1), AX, ALU.max))
                step(nc.vector.tensor_tensor(r3(lg), logits_at[0:S, 0:B * E1].rearrange("p (b e) -> p b e", e=E1),
                                             rsum[:].unsqueeze(2).broadcast_to([100, B, E1]), ALU.subtract), "logits_sub")
                dve.wait_ge(act_done, ACT_MARK["router1"])
                step(nc.vector.tensor_reduce(rsum[:], r3(ex), AX, ALU.add))
                step(nc.vector.reciprocal(rsum[:], rsum[:]))
                step(nc.vector.tensor_tensor(r3(ex), r3(ex), rsum[:].unsqueeze(2).broadcast_to([100, B, E1]), ALU.mult))
                best_of(r3(ex), r3(sl), 2, 0, B)
                step(nc.vector.tensor_tensor(rw[:, 0:B * E1], ex, sl, ALU.mult), "weights1")

            dve.wait_ge(consts_early, len(CONSTS_EARLY) * 16)
            dve.wait_ge(pool_init, 2)
            first_k_low(0)
            mask_rows()
            queries(0)
            mask_fill()
            dve.wait_ge(consts_late, len(CONSTS_LATE) * 16)
            step(nc.vector.tensor_copy(before_b[:], before[:]))
            attention(0)
            layer_norm(1, "b")
            split_tokens(0, "b")
            weights_low(0, 0, 0)
            weights_low(0, 1, 1)
            route0("b")
            weights0()
            experts(0)
            layer_norm(2)
            first_k_low(1)
            queries(1)
            attention(1)
            layer_norm(3, "b")
            split_tokens(1, "b")
            weights_low(1, 0, 0)
            weights_low(1, 1, 1)
            route1()
            experts(1)

        @block.gpsimd
        def _(pool):
            nc.gpsimd.memset(maskT_u[:, KEY_TILES - 1, :], 0).then_inc(pool_init, 1)
            nc.gpsimd.memset(tmpf[:], 1.0).then_inc(pool_init, 1)
            for i in range(2):
                nc.gpsimd.memset(ctxT[i][:, NK:NKP], 0.0).then_inc(pool_init, 1)
                nc.gpsimd.memset(vaug[i][:], 1.0).then_inc(pool_init, 1)
                pool.wait_ge(pool_init, 3 * i + 4)
                nc.gpsimd.memset(kst[i][96:128, :, :].bitcast(F32), 1.0).then_inc(pool_init, 1)
                pool.wait_ge(pool_init, 3 * i + 5)

            def attention(l):
                s = A[l]
                ops = (1, 2)[l]

                def max_queries(b):
                    if not (isinstance(b, int) and b == 0):
                        pool.wait_ge(s["chunk_ready"], b * (3 * MAX_BLOCKS[l]))
                    nc.gpsimd.tensor_tensor(qbd[:].rearrange("p (h q) -> p h q", q=S),
                                            qhi[:, bass.ds(b * S, S)].unsqueeze(1).broadcast_to([128, H, S]),
                                            head16_mask[:].unsqueeze(2).broadcast_to([128, H, S]),
                                            ALU.mult).then_inc(s["qbd_ready"], 1)

                def score_queries(b, par):
                    if not (isinstance(b, int) and b < 2):
                        pool.wait_ge(s["pv_done"], b * KEY_TILES - KEY_TILES)
                    for g in range(G):
                        nc.gpsimd.tensor_tensor(
                            qst[par][0:96, g * GQ:(g + 1) * GQ].rearrange("p (j q) -> p j q", q=S),
                            qsel[0:96, g, bass.ds(b * S, S)].unsqueeze(1).broadcast_to([96, J, S]),
                            head_mask[0:96, :].unsqueeze(2).broadcast_to([96, J, S]),
                            ALU.mult).then_inc(s["qstack_ready"], 1)

                def values(b, c, par):
                    pool.wait_ge(s["vraw_ready"], b * 3 + (c + 1))
                    if c == 0 and not (isinstance(b, int) and b < 2):
                        pool.wait_ge(s["pv_done"], b * KEY_TILES - KEY_TILES)
                    raw = vraw[(c + par) % 2]
                    raw4 = raw[:].rearrange("p t (h e) -> p t h e", e=DH)
                    dst = vaug[par][0:KEY_TILE, c * V_PER:(c + 1) * V_PER, 0:H * 9].rearrange("p t (h e) -> p t h e", e=9)[:, :, :, 0:DH]
                    bias = bv[l][0:KEY_TILE, :].rearrange("p (h e) -> p h e", e=DH).unsqueeze(1)\
                        .broadcast_to([KEY_TILE, V_PER, H, DH])
                    nc.gpsimd.tensor_tensor(raw4 if l else dst, raw4, bias, ALU.add).then_inc(s["v_written"], 1)
                    if l == 1:
                        pool.wait_ge(s["v_written"], b * (3 * ops) + (c * ops + 1))
                        gate = egate[:, bass.ds(b * KEY_TILES + c * V_PER, V_PER)]
                        nc.gpsimd.tensor_tensor(dst, raw4, gate.unsqueeze(2).unsqueeze(3)
                                                .broadcast_to([KEY_TILE, V_PER, H, DH]), ALU.mult)\
                            .then_inc(s["v_written"], 1)

                def prep(b, par):
                    max_queries(b)
                    score_queries(b, par)
                    for c in range(V_CHUNKS):
                        values(b, c, par)

                if l == 1:
                    pool.wait_ge(pe_done, PE_MARK["y0_1"])
                    for i in range(2):
                        nc.gpsimd.memset(vaug[i][:], 1.0).then_inc(pool_init, 1)
                    pool.wait_ge(pool_init, 12)
                pool.wait_ge(consts_early, len(CONSTS_EARLY) * 16)
                pool.wait_ge(dve_done, marks[f"qhi{l}"])
                max_queries(0)
                if l == 0:
                    pool.wait_ge(consts_late, len(CONSTS_LATE) * 16)
                else:
                    pool.wait_ge(dve_done, marks["gate_ready"])
                for c in range(V_CHUNKS):
                    values(0, c, 0)
                pool.wait_ge(s["qsel_in"], 3 * G * 16)
                score_queries(0, 0)
                if l == 0:
                    pool.wait_ge(mask_in, 48)
                    pool.wait_ge(dve_done, marks["any_b"])
                    nc.gpsimd.tensor_scalar(negT[:], maskT_u[:], 1.0, BIG, ALU.subtract, ALU.mult).then_inc(pool_init, 1)
                    pool.wait_ge(pool_init, 9)
                    nc.gpsimd.tensor_tensor(negT[:], negT[:], any_b[0:KEY_TILE, :].unsqueeze(1)
                                            .broadcast_to([KEY_TILE, KEY_TILES, S]), ALU.mult).then_inc(pool_init, 1)
                prep(1, 1)
                with pool.Fori(0, (B - 2) // 2) as i:
                    for k in range(2):
                        prep(i * 2 + (2 + k), k)

            def experts(l):
                m = M[l]

                def weigh(u, slot):
                    pool.wait_ge(m["wb_in"][slot], landed(u, slot, RING, 16))
                    for v in range(2):
                        pool.wait_ge(m["prod_done"], u * 2 + (v + 1))
                        if not (isinstance(u, int) and u == 0):
                            pool.wait_ge(m["h_low"], u * 2 + (v - 1))
                        nc.gpsimd.tensor_tensor(hw[v], tu[v], wb[slot][:, v * HALF:(v + 1) * HALF],
                                                ALU.mult).then_inc(m["weighted"], 1)

                units = (UNITS0, UNITS1)[l]
                weigh(0, 0)
                with pool.Fori(0, (units - 1) // RING) as i:
                    for k in range(RING):
                        weigh(i * RING + (k + 1), (k + 1) % RING)
                for u in range((units - 1) // RING * RING + 1, units):
                    weigh(u, u % RING)

            attention(0)
            experts(0)
            attention(1)
            experts(1)

        @block.scalar
        def _(act):
            n = [0]

            def step(ins, name):
                n[0] += 1
                ins.then_inc(act_done, 1)
                assert ACT_MARK[name] == n[0], (name, n[0])

            def root_all(p):
                act.wait_ge(dve_done, marks[f"var{p}"])
                step(nc.scalar.activation(rstd[:], var[:], ACT.Sqrt), f"root{p}")

            def transposed(p):
                for v in range(2):
                    act.wait_ge(pe_done, PE_MARK[f"xnT{p}_{v}"])
                    step(nc.scalar.copy(xnT[:, v * HALF:(v + 1) * HALF].rearrange("p (b q) -> p b q", q=S),
                                        ps[:, v, :].rearrange("p (b q) -> p b q", q=128)[:, :, 0:S]), f"xnT{p}_{v}")

            def part_turned(p, v):
                act.wait_ge(pe_done, PE_MARK[f"xnT{p}a_{v}"])
                b0, b1 = v * HB, min((v + 1) * HB, PARTS["a"][1])
                step(nc.scalar.copy(xnT[:, b0 * S:b1 * S].rearrange("p (b q) -> p b q", q=S),
                                    pm[:, v, 0:(b1 - b0) * 128].rearrange("p (b q) -> p b q", q=128)[:, :, 0:S]),
                     f"xnT{p}a_{v}")

            def root(p, part):
                b0, b1 = PARTS[part]
                act.wait_ge(dve_done, marks[f"var{p}{part}"])
                step(nc.scalar.activation(rstd[:, b0:b1], var[:, b0:b1], ACT.Sqrt), f"root{p}{part}")

            def rest_turned(p):
                root(p, "b")
                weights_high(p // 2, 0, 0)
                weights_high(p // 2, 1, 1)
                act.wait_ge(pe_done, PE_MARK[f"xnT{p}b"])
                b0, b1 = PARTS["b"]
                step(nc.scalar.copy(xnT[:, b0 * S:b1 * S].rearrange("p (b q) -> p b q", q=S),
                                    ps[:, 0, 0:(b1 - b0) * 128].rearrange("p (b q) -> p b q", q=128)[:, :, 0:S]),
                     f"xnT{p}b")

            def router0(part):
                b0, b1 = PARTS[part]
                act.wait_ge(pe_done, PE_MARK[f"logits0{part}"])
                step(nc.scalar.activation(rsc[:, b0 * E0:b1 * E0], logits_of[part][0:S, 0:(b1 - b0) * E0], ACT.Exp,
                                          scale=-1.0), f"router0{part}")

            def attention(l):
                s = A[l]

                def exp_half(b, t, u):
                    r = rows_of(t)
                    act.wait_ge(s["scores_ready"], b * (2 * KEY_TILES) + (2 * t + u + 1))
                    if not (isinstance(b, int) and b == 0 and t < 2):
                        act.wait_ge(s["pv_done"], b * KEY_TILES + (t - 1))
                    nc.scalar.activation(probs[t % 2][0:r, 2 * u * GQ:2 * (u + 1) * GQ].rearrange("p (g q) -> p g q", q=GQ),
                                         ps[0:r, 2 * u:2 * u + 2, 0:GQ], ACT.Exp,
                                         scale=SCALE).then_inc(s["probs_ready"], 1)

                def k_high(b, c, par):
                    lo, w = CHUNKS[c]
                    act.wait_ge(s["kproj_done"], b * 3 + (c + 1))
                    if not (isinstance(b, int) and b == 0):
                        if c == 0:
                            act.wait_ge(s["chunk_ready"], b * (3 * MAX_BLOCKS[l]))
                            act.wait_ge(s["kstack_in"][1 - par], landed(b - 1, 1 - par, 2, 192))
                    nc.scalar.activation(khi[:, lo:lo + w], pc[:, 0:w], ACT.Identity, bias=bk[l][:, 0:1])\
                        .then_inc(s["khi_ready"], 1)

                def v_raw(b, c, par):
                    act.wait_ge(s["vproj_done"], b * 3 + (c + 1))
                    if not (isinstance(b, int) and b * 3 + c < 2):
                        act.wait_ge(s["v_written"], b * (3 * (1, 2)[l]) + (c - 1) * (1, 2)[l])
                    raw = vraw[(c + par) % 2]
                    nc.scalar.copy(raw[:].rearrange("p t n -> p (t n)"), pc[0:KEY_TILE, :]).then_inc(s["vraw_ready"], 1)

                def outputs(b):
                    act.wait_ge(s["pv_done"], b * KEY_TILES + KEY_TILES)
                    if not (isinstance(b, int) and b == 0):
                        act.wait_ge(s["onorm_ready"], b)
                    nc.scalar.copy(oraw[:], po[:, 0:GQ]).then_inc(s["oraw_ready"], 1)

                def slots(b, main, after, prep, par):
                    for t in range(KEY_TILES):
                        if main:
                            exp_half(b, t, 0)
                        if prep and t < 3:
                            k_high(b + 1, t, 1 - par)
                        if prep and t in V_SLOTS:
                            v_raw(b + 1, V_SLOTS.index(t), 1 - par)
                        if main:
                            exp_half(b, t, 1)
                        if after and t == 0:
                            outputs(b - 1)
                        if main and not prep:
                            if t == 0:
                                root(2 * l + 1, "a")
                            if t == TURN_SLOT:
                                part_turned(2 * l + 1, 0)
                                part_turned(2 * l + 1, 1)
                            if t == LOGITS_SLOT and l == 0:
                                router0("a")

                slots(0, True, False, True, 0)
                if l == 0:
                    act.wait_ge(dve_done, marks["energy"])
                    step(nc.scalar.activation(egate[:], egate[:], ACT.Exp, scale=-1.0), "energy_exp")
                with act.Fori(0, (B - 2) // 2) as i:
                    for k in range(2):
                        slots(i * 2 + (1 + k), True, True, True, 1 - k)
                slots(B - 1, True, True, False, 1)
                outputs(B - 1)

            def weights_high(l, u, slot):
                m = M[l]
                act.wait_ge(m["w_in"][slot], landed(u, slot, RING, 16))
                if not (isinstance(u, int) and u < RING):
                    act.wait_ge(m["down_done"], u * 2 - (2 * RING - 2))
                nc.scalar.copy(w_hi[slot], wts[slot][:]).then_inc(m["w_high"], 1)

            def silu(l, u, v):
                m = M[l]
                act.wait_ge(m["gate_ready"], u * 2 + (v + 1))
                if not (isinstance(u, int) and u == 0):
                    act.wait_ge(m["prod_done"], u * 2 + (v - 1))
                nc.scalar.activation(sg[v], ps[:, v, 0:HALF], ACT.Silu).then_inc(m["silu_done"], 1)

            def experts(l):
                m = M[l]

                def hidden_high(u, v):
                    act.wait_ge(m["weighted"], u * 2 + (v + 1))
                    if not (isinstance(u, int) and u == 0):
                        act.wait_ge(m["down_done"], u * 2 + (v - 1))
                    nc.scalar.copy(h_hi[v], hw[v]).then_inc(m["h_high"], 1)

                units = (UNITS0, UNITS1)[l]

                def unit(u, slot):
                    for v in range(2):
                        if not (isinstance(u, int) and u == 0):
                            hidden_high(u - 1, v)
                        if not (isinstance(u, int) and u == 0):
                            silu(l, u, v)
                    if not (isinstance(u, int) and u + 2 >= units):
                        weights_high(l, u + 2, (slot + 2) % RING)

                unit(0, 0)
                unit(1, 1)
                with act.Fori(0, (units - 4) // RING) as i:
                    for k in range(RING):
                        unit(i * RING + (k + 2), (k + 2) % RING)
                for u in range((units - 4) // RING * RING + 2, units):
                    unit(u, u % RING)
                for v in range(2):
                    hidden_high(units - 1, v)
                act.wait_ge(pe_done, PE_MARK[f"moe_sum{l}"])
                step(nc.scalar.copy(yT.rearrange("p (v n) -> p v n", v=2), pm[:, :, 0:HALF]), f"yT{l}")

            def first_k(l):
                for c, (lo, w) in enumerate(CHUNKS):
                    act.wait_ge(A[l]["kproj_done"], c + 1)
                    nc.scalar.activation(khi[:, lo:lo + w], first_k_bank[c][:, 0:w], ACT.Identity, bias=bk[l][:, 0:1])\
                        .then_inc(A[l]["khi_ready"], 1)

            def first_v(l):
                s = A[l]
                for c in range(V_CHUNKS):
                    act.wait_ge(s["vproj_done"], c + 1)
                    if c == 2:
                        act.wait_ge(s["v_written"], (1, 2)[l])
                    nc.scalar.copy(vraw[c % 2][:].rearrange("p t n -> p (t n)"), first_v_bank[c][0:KEY_TILE, :])\
                        .then_inc(s["vraw_ready"], 1)

            root_all(0)
            act.wait_ge(consts_early, len(CONSTS_EARLY) * 16)
            first_k(0)
            transposed(0)
            act.wait_ge(consts_late, len(CONSTS_LATE) * 16)
            step(nc.scalar.activation(tgates[:], gates[:], ACT.Tanh), "tanh")
            first_v(0)
            attention(0)
            rest_turned(1)
            router0("b")
            silu(0, 0, 0)
            silu(0, 0, 1)
            act.wait_ge(pe_done, PE_MARK["wT0"])
            step(nc.scalar.copy(wT.rearrange("p (v b q) -> p v b q", v=2, q=S),
                                pm[0:E0, 0:2, :].rearrange("p v (b q) -> p v b q", q=128)[:, :, :, 0:S]), "wT0")
            experts(0)
            first_k(1)
            root_all(2)
            transposed(2)
            first_v(1)
            attention(1)
            rest_turned(3)
            act.wait_ge(dve_done, marks["logits_sub"])
            step(nc.scalar.activation(rt[0][:, 64:128], rt[0][:, 0:64], ACT.Exp), "router1")
            silu(1, 0, 0)
            silu(1, 0, 1)
            act.wait_ge(pe_done, PE_MARK["wT1"])
            step(nc.scalar.copy(wT[0:E1, :].rearrange("p (v b q) -> p v b q", v=2, q=S),
                                pm[0:E1, 0:2, :].rearrange("p v (b q) -> p v b q", q=128)[:, :, :, 0:S]), "wT1")
            experts(1)

        @block.tensor
        def _(pe):
            n = [0]

            def step(ins, name):
                n[0] += 1
                ins.then_inc(pe_done, 1)
                assert PE_MARK[name] == n[0], (name, n[0])

            def transpose_tokens(p):
                for v in range(2):
                    pe.wait_ge(dve_done, marks[f"xn{p}_{v}"])
                    for b in range(HB):
                        mm = nc.tensor.transpose(ps[:, v, b * 128:b * 128 + S], xn[:, v * HB + b, :], ident[0:S, 0:S])
                    step(mm, f"xnT{p}_{v}")

            def queries(l):
                for v in range(2):
                    pe.wait_ge(act_done, ACT_MARK[f"xnT{2 * l}_{v}"])
                    step(nc.tensor.matmul(ps[:, v, 0:HALF], wq[l][:], xnT[:, v * HALF:(v + 1) * HALF],
                                          start=True, stop=True), f"q{l}_{v}")

            def first_k(l):
                s = A[l]
                pe.wait_ge(s["ctx_in"][0], 16)
                for c, (lo, w) in enumerate(CHUNKS):
                    nc.tensor.matmul(first_k_bank[c][:, 0:w], wk[l][:], ctxT[0][:, lo:lo + w], start=True,
                                     stop=True).then_inc(s["kproj_done"], 1)

            def first_v(l):
                s = A[l]
                for c in range(V_CHUNKS):
                    for i in range(V_PER):
                        t = c * V_PER + i
                        mm = nc.tensor.matmul(first_v_bank[c][0:KEY_TILE, i * 128:(i + 1) * 128],
                                              ctxT[0][:, t * KEY_TILE:(t + 1) * KEY_TILE], wv[l][:],
                                              start=True, stop=True)
                    mm.then_inc(s["vproj_done"], 1)

            def turn(p, part):
                b0, b1 = PARTS[part]
                for lo in range(b0, b1, HB):
                    v = (lo - b0) // HB
                    pe.wait_ge(dve_done, marks[f"xn{p}{part}_{v}"])
                    for b in range(lo, min(lo + HB, b1)):
                        dst = pm[:, v, :] if part == "a" else ps[:, 0, :]
                        mm = nc.tensor.transpose(dst[:, (b - lo) * 128:(b - lo) * 128 + S], xn[:, b, :], ident[0:S, 0:S])
                    step(mm, f"xnT{p}{part}" + (f"_{v}" if part == "a" else ""))

            def logits(l, part):
                w, e = ((wr0, E0), (wr1, E1))[l]
                b0, b1 = PARTS[part]
                pe.wait_ge(act_done, ACT_MARK[f"xnT{2 * l + 1}{part}" + ("_1" if part == "a" else "")])
                for b in range(b0, b1):
                    dst, i = (logits_of[part], b - b0) if l == 0 else (logits_at, b)
                    mm = nc.tensor.matmul(dst[0:S, i * e:(i + 1) * e], xnT[:, b * S:(b + 1) * S], w[:],
                                          start=True, stop=True)
                step(mm, f"logits{l}{part}")

            def attention(l):
                s, blocks = A[l], MAX_BLOCKS[l]

                def k_chunk(b, c, par):
                    lo, w = CHUNKS[c]
                    if c == 0:
                        pe.wait_ge(s["ctx_in"][par], landed(b, par, 2, 16))
                        if not (isinstance(b, int) and b == 0):
                            pe.wait_ge(s["negm_ready"], b * len(NEGM_WRITES[l]))
                    else:
                        pe.wait_ge(s["klo_ready"], b * 3 + c)
                    nc.tensor.matmul(pc[:, 0:w], wk[l][:], ctxT[par][:, lo:lo + w], start=True,
                                     stop=True).then_inc(s["kproj_done"], 1)

                def v_chunk(b, c, half, par, tail):
                    if half == 1:
                        pass
                    elif c == 0:
                        if tail:
                            pe.wait_ge(s["tail_step"], b * TAIL - (2 * TAIL - OUT_TAKEN))
                        else:
                            pe.wait_ge(s["klo_ready"], b * 3 + 3)
                    else:
                        pe.wait_ge(s["vraw_ready"], b * 3 + c)
                    for i in range(half * V_PER // 2, (half + 1) * V_PER // 2):
                        t = c * V_PER + i
                        mm = nc.tensor.matmul(pc[0:KEY_TILE, i * 128:(i + 1) * 128],
                                              ctxT[par][:, t * KEY_TILE:(t + 1) * KEY_TILE], wv[l][:],
                                              start=True, stop=True)
                    if half == 1:
                        mm.then_inc(s["vproj_done"], 1)

                def max_chunk(b, k):
                    c, i = k // blocks, k % blocks
                    lo, w = CHUNKS[c]
                    first = i * MAX_ROWS[l]
                    rows = min(MAX_ROWS[l], HQ - first)
                    if k == 0:
                        pe.wait_ge(s["qbd_ready"], b + 1)
                    if isinstance(b, int) and b == 0 and k == 0:
                        pe.wait_ge(s["vraw_ready"], 2)
                        pe.wait_ge(s["klo_ready"], 3)
                    if i == 0:
                        pe.wait_ge(s["khi_ready"], b * 3 + (c + 1))
                    if isinstance(b, int) and b == 0:
                        if k >= IN_FLIGHT_FIRST:
                            pe.wait_ge(s["max_taken"], k - (IN_FLIGHT_FIRST - 1))
                    else:
                        pe.wait_ge(s["max_taken"], b * (3 * blocks) + (k - 1))
                    nc.tensor.matmul(max_bank(b, k)[0:rows, 0:w], qbd[:, first:first + rows], khi[:, lo:lo + w],
                                     start=True, stop=True).then_inc(s["chunk_ready"], 1)

                def max_rows(b):
                    rows = MAX_ROWS[l]
                    pe.wait_ge(s["rowmax_step"], b * 2 + 2)
                    pe.wait_ge(s["vraw_ready"], b * 3 + 3)
                    nc.tensor.transpose(pc[:, 0:rows], negm[0:rows, :], ident[0:rows, 0:rows])\
                        .then_inc(s["maxrow_ready"], 1)

                def scores(b, t, g, par):
                    r, u = rows_of(t), g // 2
                    if t == 0 and g == 0:
                        if l == 0 and isinstance(b, int) and b == 0:
                            pe.wait_ge(pool_init, 10)
                        pe.wait_ge(s["kstack_in"][par], landed(b, par, 2, 192))
                        pe.wait_ge(s["qstack_ready"], b * 4 + 4)
                    if t == 0:
                        writes = len(NEGM_WRITES[l])
                        pe.wait_ge(s["negm_ready"], b * writes + (g + 1 if g < G - 1 else writes))
                    if g % 2 == 0:
                        if not (isinstance(b, int) and b == 0 and t == 0):
                            pe.wait_ge(s["probs_ready"], b * (2 * KEY_TILES) + (2 * t + u - 1))
                    mm = nc.tensor.matmul(ps[0:r, g, 0:GQ], kst[par][:, g, t * KEY_TILE:t * KEY_TILE + r],
                                          qst[par][:, g * GQ:(g + 1) * GQ], start=True, stop=(l == 1))
                    if l == 0:
                        mm = nc.tensor.matmul(ps[0:r, g, 0:GQ].rearrange("p (j q) -> p j q", q=S),
                                              ident_b[0:r, 0:r],
                                              negT[0:r, t, :].unsqueeze(1).broadcast_to([r, J, S]),
                                              start=False, stop=True)
                    if g % 2 == 1:
                        mm.then_inc(s["scores_ready"], 1)

                def weigh(b, t, u, par):
                    r = rows_of(t)
                    pe.wait_ge(s["probs_ready"], b * (2 * KEY_TILES) + (2 * t + u + 1))
                    if t == 0 and u == 0:
                        pe.wait_ge(s["v_written"], (b * 3 + 3) * (1, 2)[l])
                        if not (isinstance(b, int) and b == 0):
                            pe.wait_ge(s["oraw_ready"], b)
                    for g in range(2 * u, 2 * u + 2):
                        for j in range(J):
                            h = J * g + j
                            mm = nc.tensor.matmul(po[32 * j:32 * j + 32, g * S:(g + 1) * S],
                                                  vaug[par][0:r, t, 9 * h:9 * h + 32],
                                                  probs[t % 2][0:r, h * S:(h + 1) * S],
                                                  start=(t == 0 and g == 0), stop=(t == KEY_TILES - 1),
                                                  tile_position=(0, 32 * j), skip_group_check=True)
                    if u == 1:
                        mm.then_inc(s["pv_done"], 1)

                def den(b, prep):
                    if prep:
                        pe.wait_ge(s["klo_ready"], b * 3 + 9)
                    elif isinstance(b, int) and b == B - 1:
                        pe.wait_ge(s["tail_step"], TAIL * (B - 1))
                    else:
                        pe.wait_ge(s["negm_ready"], (b + 2) * len(NEGM_WRITES[l]))
                    pe.wait_ge(s["oraw_ready"], b + 1)
                    nc.tensor.matmul(pc[:, 0:GQ], den_sel[:], oraw[:], start=True, stop=True)\
                        .then_inc(s["tail_ready"], 1)

                def project(b):
                    pe.wait_ge(s["onorm_ready"], b + 1)
                    for g in range(G):
                        mm = nc.tensor.matmul(pc[0:S, 0:D], onorm[:, g * S:(g + 1) * S], wo[l][:, g, :],
                                              start=(g == 0), stop=(g == G - 1))
                    mm.then_inc(s["tail_ready"], 1)

                def slots(b, main, after, prep, par):
                    for t in range(KEY_TILES):
                        blocks_here = MAX_SLOTS[l][t] if prep else []
                        weighs = main and t >= 1 or after and t == 0
                        projects_k = prep and main and t < 3
                        projects_v = prep and main and t in V_SLOTS
                        spreads = after and t == DEN_SLOT
                        projects_out = after and t == OUT_SLOT
                        turns_maxima = prep and t == KEY_TILES - 1
                        whole = (main * G * SCORES_WORK[l] + weighs * 2 * WEIGH_WORK + projects_k * K_WORK
                                 + projects_v * V_WORK + spreads * DEN_WORK + projects_out * OUT_WORK
                                 + turns_maxima * TURN_WORK)
                        spent, taken = 0, 0

                        def maxima(work):
                            nonlocal spent, taken
                            spent += work
                            while whole and taken < len(blocks_here) * spent // whole:
                                max_chunk(b + 1, blocks_here[taken])
                                taken += 1

                        if main:
                            scores(b, t, 0, par)
                            maxima(SCORES_WORK[l])
                            scores(b, t, 1, par)
                            maxima(SCORES_WORK[l])
                        if weighs:
                            if t >= 1:
                                weigh(b, t - 1, 0, par)
                            else:
                                weigh(b - 1, KEY_TILES - 1, 0, 1 - par)
                            maxima(WEIGH_WORK)
                        if projects_k:
                            k_chunk(b + 1, t, 1 - par)
                            maxima(K_WORK)
                        if projects_v:
                            v_chunk(b + 1, V_SLOTS.index(t), 0, 1 - par, after)
                            maxima(V_WORK // 2)
                            v_chunk(b + 1, V_SLOTS.index(t), 1, 1 - par, after)
                            maxima(V_WORK // 2)
                        if spreads:
                            den(b - 1, prep)
                            maxima(DEN_WORK)
                        if projects_out:
                            project(b - 1)
                            maxima(OUT_WORK)
                        if turns_maxima:
                            max_rows(b + 1)
                            maxima(TURN_WORK)
                        if main:
                            scores(b, t, 2, par)
                            maxima(SCORES_WORK[l])
                            scores(b, t, 3, par)
                            maxima(SCORES_WORK[l])
                        if weighs:
                            if t >= 1:
                                weigh(b, t - 1, 1, par)
                            else:
                                weigh(b - 1, KEY_TILES - 1, 1, 1 - par)
                            maxima(WEIGH_WORK)
                        if main and not prep and t == TURN_SLOT:
                            turn(2 * l + 1, "a")
                        if main and not prep and t == LOGITS_SLOT:
                            logits(l, "a")
                        for k in blocks_here[taken:]:
                            max_chunk(b + 1, k)

                slots(-1, False, False, True, 1)
                slots(0, True, False, True, 0)
                with pe.Fori(0, (B - 2) // 2) as i:
                    for k in range(2):
                        slots(i * 2 + (1 + k), True, True, True, 1 - k)
                slots(B - 1, True, True, False, 1)
                for u in range(2):
                    weigh(B - 1, KEY_TILES - 1, u, 1)
                den(B - 1, False)
                project(B - 1)

            def experts(l, opening=False):
                m = M[l]
                units = (UNITS0, UNITS1)[l]

                def product(dst, hi, lo, x_high, x_low, alone):
                    for k, (w, x) in enumerate(((hi, x_high), (lo, x_high), (hi, x_low))):
                        mm = nc.tensor.matmul(dst, w, x, start=(alone and k == 0), stop=(alone and k == 2),
                                              skip_group_check=not alone)
                    return mm

                def gate_up(u, slot):
                    pe.wait_ge(m["w_low"], u + 1)
                    for v in range(2):
                        cols = slice(v * HALF, (v + 1) * HALF)
                        if not (isinstance(u, int) and u == 0):
                            pe.wait_ge(m["prod_done"], u * 2 + (v - 1))
                        product(ps[:, v, 0:HALF], w_hi[slot][:, 0, :], w_lo[slot][:, 0, :], x_hi[:, cols], x_lo[:, cols],
                                True).then_inc(m["gate_ready"], 1)
                        product(ps[:, 2 + v, 0:HALF], w_hi[slot][:, 1, :], w_lo[slot][:, 1, :], x_hi[:, cols],
                                x_lo[:, cols], True).then_inc(m["up_ready"], 1)

                def down(u, slot):
                    for v in range(2):
                        pe.wait_ge(m["h_low"], u * 2 + (v + 1))
                        product(pm[:, v, 0:HALF], w_hi[slot][:, 2, :], w_lo[slot][:, 2, :], h_hi[v], h_lo[v],
                                False).then_inc(m["down_done"], 1)

                if opening:
                    pe.wait_ge(dve_done, marks[f"tokens{l}b"])
                    gate_up(0, 0)
                    return
                pe.wait_ge(act_done, ACT_MARK[f"wT{l}"])
                for v in range(2):
                    nc.tensor.matmul(pm[:, v, 0:HALF], zero_b[:, 0:128], zero_b[:, 0:HALF], start=True, stop=False,
                                     skip_group_check=True)
                with pe.Fori(0, (units - 1) // RING) as i:
                    for k in range(RING):
                        gate_up(i * RING + (k + 1), (k + 1) % RING)
                        down(i * RING + k, k)
                for u in range((units - 1) // RING * RING, units):
                    if u + 1 < units:
                        gate_up(u + 1, (u + 1) % RING)
                    down(u, u % RING)
                for v in range(2):
                    mm = nc.tensor.matmul(pm[:, v, 0:HALF], zero_b[:, 0:128], zero_b[:, 0:HALF], start=False, stop=True,
                                          skip_group_check=True)
                step(mm, f"moe_sum{l}")
                pe.wait_ge(act_done, ACT_MARK[f"yT{l}"])
                for v in range(2):
                    for b in range(HB):
                        mm = nc.tensor.transpose(ps[0:S, v, b * D:(b + 1) * D], yT[:, (v * HB + b) * S:(v * HB + b + 1) * S],
                                                 ident[:])
                    step(mm, f"y{l}_{v}")

            def weights_across(l, e):
                pe.wait_ge(dve_done, marks[f"weights{l}"])
                w3 = rw[:, 0:B * e].rearrange("p (b e) -> p b e", e=e)
                for b in range(B):
                    mm = nc.tensor.transpose(pm[0:e, b // HB, (b % HB) * 128:(b % HB) * 128 + S], w3[:, b, :],
                                             ident[0:S, 0:S])
                step(mm, f"wT{l}")

            pe.wait_ge(consts_early, len(CONSTS_EARLY) * 16)
            pe.wait_ge(pool_init, 3)
            first_k(0)
            transpose_tokens(0)
            pe.wait_ge(dve_done, marks["any_diag"])
            pe.wait_ge(A[0]["klo_ready"], 3)
            step(nc.tensor.matmul(pc[:, 0:S], ones_f[0:S, :], any_diag[:], start=True, stop=True), "any_b")
            queries(0)
            first_v(0)
            pe.wait_ge(dve_done, marks["any_b"])
            pe.wait_ge(pool_init, 8)
            pe.wait_ge(consts_late, len(CONSTS_LATE) * 16)
            attention(0)
            turn(1, "b")
            logits(0, "b")
            experts(0, opening=True)
            pe.wait_ge(dve_done, marks["chosenb"])
            for b in range(B):
                for c in range(b + 1):
                    mm = nc.tensor.matmul(pc[0:S, b * E0:(b + 1) * E0], (before_b[:] if c == b else ones_b[0:S, 0:S]),
                                          rsel_b[:, c, :], start=(c == 0), stop=(c == b))
            step(mm, "ranks")
            weights_across(0, E0)
            experts(0)
            first_k(1)
            transpose_tokens(2)
            queries(1)
            first_v(1)
            attention(1)
            turn(3, "b")
            logits(1, "b")
            experts(1, opening=True)
            weights_across(1, E1)
            experts(1)

        @block.sync
        def _(sp):
            sp.dma_start(xres[:], a["x"].rearrange("b q d -> q b d")).then_inc(x_in, 16)

            def context(l, b, par):
                s = A[l]
                if not (isinstance(b, int) and b < 2):
                    sp.wait_ge(s["vproj_done"], b * 3 - 3)
                sp.dma_start(ctxT[par][:, 0:NK], a["ctxT"][bass.ds(b, 1)].rearrange("a p n -> p (a n)"))\
                    .then_inc(s["ctx_in"][par], 16)

            def stack(l, b, par):
                s = A[l]
                sp.wait_ge(s["klo_ready"], b * 3 + 3)
                if not (isinstance(b, int) and b < 2):
                    sp.wait_ge(s["pv_done"], b * KEY_TILES - KEY_TILES)
                for g in range(G):
                    for i, part in enumerate((khi, klo, khi)):
                        sp.dma_start(kst[par][32 * i:32 * i + 32, g, :].bitcast(F32),
                                     part[32 * g:32 * g + 32, :].bitcast(F32)).then_inc(s["kstack_in"][par], 16)

            tile_of = dict(ident=ident, head_mask=head_mask, head16_mask=head16_mask, max_mask=max_mask, den_sel=den_sel,
                           before=before, tie_mask=tie_mask, gates=gates, wr0=wr0, wr1=wr1, ebias=ebias)
            for l in range(2):
                for name, tiles in (("wq", wq), ("wk", wk), ("wv", wv), ("wo", wo), ("bq", bq), ("bk", bk), ("bv", bv),
                                    ("bo", bo)):
                    tile_of[f"{name}{l}"] = tiles[l]
            context(0, 0, 0)
            for name in CONSTS_EARLY:
                sp.dma_start(tile_of[name][:], a[name]).then_inc(consts_early, 16)
            sp.dma_start(mask_u[:], a["mask"]).then_inc(mask_in, 16)
            sp.wait_ge(pool_init, 1)
            full = (KEY_TILES - 1) * KEY_TILE
            sp.dma_start(maskT_u[:, 0:KEY_TILES - 1, :], a["maskT"][0:full].rearrange("(t p) q -> p t q", p=KEY_TILE))\
                .then_inc(mask_in, 16)
            sp.dma_start(maskT_u[0:LAST_ROWS, KEY_TILES - 1, :], a["maskT"][full:NK]).then_inc(mask_in, 16)
            for name in CONSTS_LATE:
                sp.dma_start(tile_of[name][:], a[name]).then_inc(consts_late, 16)
            sp.wait_ge(pool_init, 2)
            context(0, 1, 1)

            def energies():
                en = tmpf[0:KEY_TILE, 0:B * KEY_TILES * 8].rearrange("p (b t e) -> p b t e", b=B, e=8)
                for b in range(B):
                    sp.dma_start(en[:, b, 0:KEY_TILES - 1, :],
                                 a["ctxb"][b, 0:full].rearrange("(t p) e -> p t e", p=KEY_TILE)).then_inc(energy_in, 16)
                    sp.dma_start(en[0:LAST_ROWS, b, KEY_TILES - 1, :], a["ctxb"][b, full:NK]).then_inc(energy_in, 16)

            def attention(l):
                stack(l, 0, 0)
                for part, tile, mark in ((0, qhi, "qhi"), (1, qhi, "qhi"), (2, qlo, "q_ready")):
                    sp.wait_ge(dve_done, marks[f"{mark}{l}"])
                    for g in range(G):
                        sp.dma_start(qsel[32 * part:32 * part + 32, g, :].bitcast(F32),
                                     tile[32 * g:32 * g + 32, :].bitcast(F32)).then_inc(A[l]["qsel_in"], 16)
                if l == 0:
                    energies()
                context(l, 2, 0)
                stack(l, 1, 1)
                context(l, 3, 1)
                with sp.Fori(0, (B - 4) // 2) as i:
                    for k in range(2):
                        stack(l, i * 2 + (2 + k), k)
                        context(l, i * 2 + (4 + k), k)
                stack(l, B - 2, 0)
                stack(l, B - 1, 1)

            def experts(l):
                m = M[l]
                units = (UNITS0, UNITS1)[l]

                def weights(u, slot):
                    if not (isinstance(u, int) and u < RING):
                        sp.wait_ge(m["w_low"], u - (RING - 1))
                    sp.dma_start(wts[slot][:], a[f"experts{l}"][bass.ds(u, 1)].rearrange("a p c n -> p (a c) n"))\
                        .then_inc(m["w_in"][slot], 16)

                def spread(u, slot):
                    if not (isinstance(u, int) and u < RING):
                        sp.wait_ge(m["weighted"], u * 2 - (2 * RING - 2))
                    n = STRETCHES[l]
                    sp.dma_start(wb[slot][:], scratch[l][bass.ds(u * n, n), :].unsqueeze(1).broadcast_to([n, 128 // n, TOK]))\
                        .then_inc(m["wb_in"][slot], 16)

                for u in range(RING):
                    weights(u, u)
                sp.wait_ge(act_done, ACT_MARK[f"wT{l}"])
                if l == 0:
                    sp.dma_start(scratch[0][0:E0, :], wT).then_inc(m["w_out"], 16)
                    sp.dma_start(scratch[0][E0:E0 + 2, :].rearrange("a (b n) -> a b n", n=100),
                                 ones_f[0:2, 0:100].unsqueeze(1).broadcast_to([2, 8, 100])).then_inc(m["w_out"], 16)
                    sp.wait_ge(m["w_out"], 32)
                else:
                    per = UNITS1 * STRETCHES[1] // E1
                    sp.dma_start(scratch[1].rearrange("(e s) t -> e s t", s=per),
                                 wT[0:E1, :].unsqueeze(1).broadcast_to([E1, per, TOK])).then_inc(m["w_out"], 16)
                    sp.wait_ge(m["w_out"], 16)
                for u in range(RING):
                    spread(u, u)
                if l == 0:
                    context(1, 0, 0)
                    context(1, 1, 1)
                with sp.Fori(0, (units - RING) // RING) as i:
                    for k in range(RING):
                        weights(i * RING + (RING + k), k)
                        spread(i * RING + (RING + k), k)
                for u in range(units // RING * RING, units):
                    weights(u, u % RING)
                    spread(u, u % RING)

            attention(0)
            experts(0)
            attention(1)
            experts(1)
            sp.wait_ge(dve_done, marks["moe_out1_1"])
            sp.dma_start(out.rearrange("b q d -> q b d"), xres[:]).then_inc(out_done, 16)
            sp.wait_ge(out_done, 16)


_IN = ["x", "ctxT", "ctxb", "mask", "maskT", "experts0", "experts1"] + CONSTS_EARLY + CONSTS_LATE


def kernel(**inputs):
    import numpy as np
    import concourse.bacc as bacc
    from concourse.bass_utils import run_bass_kernel_spmd

    i = {k: np.asarray(v) for k, v in inputs.items()}
    a = {"x": i["x"], "ctxT": i["ctx_1024"].transpose(0, 2, 1), "ctxb": i["ctxb_2048x8"]}
    mask = i["mask_1x1xSxS2_bk0"][0, 0]
    a["mask"], a["maskT"] = mask, mask.T

    f = np.float32
    row = np.arange(128)
    a["ident"] = np.eye(128, dtype=f)
    a["head_mask"] = ((row[:, None] % 32 // DH == np.arange(J)) & (row[:, None] < 96)).astype(f)
    a["head16_mask"] = (row[:, None] // DH == np.arange(H)).astype(f)
    a["max_mask"] = (row[:, None] - 96 == np.arange(H)).astype(f)
    a["den_sel"] = (row[:, None] == row // 32 * 32 + DH).astype(f)
    a["before"] = (row[:S, None] < row[:S]).astype(f)
    a["tie_mask"] = np.ascontiguousarray(np.broadcast_to((np.arange(8) < np.arange(8)[:, None]).astype(f), (S, 8, 8)))

    a["gates"] = np.broadcast_to(np.concatenate([i["g_xattn"], i["g_ffn"]]), (128, 4))
    for l in range(2):
        w = {n: i[f"L{l}_xattn_W{n}"] for n in "qkvo"}
        if l == 0:
            w = {n: m.T for n, m in w.items()}
        b = {n: i[f"L{l}_xattn_b{n}"] for n in "qkvo"}
        a[f"wq{l}"], a[f"wk{l}"], a[f"wv{l}"] = w["q"], w["k"], w["v"]
        wo = np.zeros((J, 32, G, D), f)
        wo[:, 0:DH] = w["o"].reshape(G, J, DH, D).transpose(1, 2, 0, 3)
        a[f"wo{l}"] = wo.reshape(128, G, D)
        a[f"bq{l}"], a[f"bk{l}"] = b["q"][:, None], b["k"][:, None]
        a[f"bv{l}"], a[f"bo{l}"] = np.broadcast_to(b["v"], (128, 128)), np.broadcast_to(b["o"], (128, 128))
    a["wr0"], a["wr1"] = i["L0_ffn_gate_weight"].T, i["L1_ffn_router_w"].T
    a["ebias"] = np.broadcast_to(i["L0_ffn_e_bias"], (S, E0))

    ex = np.zeros((UNITS0, 128, 3, 128), f)
    ex[:-1, :, 0] = i["L0_ffn_w1"].reshape(-1, 128, D).transpose(0, 2, 1)
    ex[:-1, :, 1] = i["L0_ffn_w3"].reshape(-1, 128, D).transpose(0, 2, 1)
    ex[:-1, :, 2] = i["L0_ffn_w2"].transpose(0, 2, 1).reshape(-1, 128, D)
    ex[-1, :, 0], ex[-1, :, 1], ex[-1, :, 2] = (i["L0_ffn_shared_gate"].T, i["L0_ffn_shared_up"].T,
                                                i["L0_ffn_shared_down"].T)
    a["experts0"] = ex
    ex = np.zeros((UNITS1, 128, 3, 128), f)
    ex[:, :, 0] = i["L1_ffn_gate_w"].reshape(-1, 128, D).transpose(0, 2, 1)
    ex[:, :, 1] = i["L1_ffn_up_w"].reshape(-1, 128, D).transpose(0, 2, 1)
    ex[:, :, 2] = i["L1_ffn_down_w"].transpose(0, 2, 1).reshape(-1, 128, D)
    a["experts1"] = ex

    nc = bacc.Bacc("TRN2", target_bir_lowering=False, num_devices=1)
    arrays, aps = {}, {}
    for name in _IN:
        arr = np.ascontiguousarray(a[name])
        arrays[f"in_{name}"] = arr
        aps[name] = nc.dram_tensor(f"in_{name}", arr.shape, mybir.dt.from_np(arr.dtype), kind="ExternalInput").ap()
    out = nc.dram_tensor("out_dram", (B, S, D), F32, kind="ExternalOutput").ap()
    scratch = [nc.dram_tensor(f"routing{l}", (STRETCHES[l] * (UNITS0, UNITS1)[l], TOK), F32, kind="Internal").ap() for l in range(2)]
    flamingo(nc, aps, out, scratch)
    r = run_bass_kernel_spmd(nc, [arrays], core_ids=[0])
    return r.results[0]["out_dram"]
```
